# Optimizing a Trainium2 kernel written in Bass

```python
import numpy as np
import jax
import jax.numpy as jnp

def _softmax(x, axis=-1):
    return jax.nn.softmax(x, axis=axis)

def _gelu(x):
    return jax.nn.gelu(x, approximate=True)

def _silu(x):
    return jax.nn.silu(x)

def _sigmoid(x):
    return jax.nn.sigmoid(x)

def _layernorm(x, axis=-1, eps=1e-05):
    m = jnp.mean(x, axis=axis, keepdims=True)
    v = jnp.var(x, axis=axis, keepdims=True)
    return (x - m) / jnp.sqrt(v + eps)

def _scatter_add(tgt, idx, src, axis=0):
    return tgt.at[idx].add(src)

def _segment_sum(src, seg, n):
    return jax.ops.segment_sum(src, seg, n)
kernel_name = 'mk_adaln_attn_ffn_d1_seqx_r4_bf0022'

def setup_inputs(seed: int=0):
    np.random.seed(seed)
    _w = jnp.asarray

    def _rec_inputs():
        import jax
        import jax.numpy as jnp
        _rk = jax.random.key(seed)
        x = -7.109e-05 + 0.9999 * jax.random.normal(jax.random.fold_in(_rk, 1), (64, 64, 512), jnp.float32)
        _lenS = 64 - jax.random.randint(jax.random.fold_in(_rk, 7), (64,), 0, max(1, 64 // 4) + 1, jnp.int32)
        _lenS2 = 64 - jax.random.randint(jax.random.fold_in(_rk, 8), (64,), 0, max(1, 64 // 4) + 1, jnp.int32)
        itok_B_0_6 = jax.random.randint(jax.random.fold_in(_rk, 11), (64,), 0, 7, jnp.int32)
        itok_B_1_198 = jax.random.randint(jax.random.fold_in(_rk, 12), (64,), 1, 199, jnp.int32)
        return (x, itok_B_0_6, itok_B_1_198)
    x, itok_B_0_6, itok_B_1_198 = _rec_inputs()

    def _L0_cond_setup():
        import jax, jax.numpy as jnp
        import numpy as np
        B, T, D_IN, D_OUT = (16, 512, 512, 512)
        N_ADAPTERS, RANK = (8, 16)
        key = jax.random.key(seed)
        k_x, k_w, k_a, k_b, k_s, k_idx = jax.random.split(key, 6)
        x = jax.random.normal(k_x, (B, T, D_IN), dtype=jnp.float32)
        W = jax.random.normal(k_w, (D_OUT, D_IN), dtype=jnp.float32) * (1.0 / np.sqrt(D_IN))
        A = jax.random.normal(k_a, (N_ADAPTERS, RANK, D_IN), dtype=jnp.float32) * 0.02
        Bm = jax.random.normal(k_b, (N_ADAPTERS, D_OUT, RANK), dtype=jnp.float32) * 0.02
        scalings = jnp.ones((N_ADAPTERS,), dtype=jnp.float32)
        adapter_idx = jax.random.randint(k_idx, (B,), 0, N_ADAPTERS, dtype=jnp.int32)
        return {'x': x, 'W': W, 'A': A, 'Bm': Bm, 'scalings': scalings, 'adapter_idx': adapter_idx}
    _L0_cond_all = _L0_cond_setup()
    _L0_cond_in = {k: v for k, v in _L0_cond_all.items() if k in ('W', 'A', 'Bm', 'scalings')}
    del _L0_cond_all

    def _L0_attn_setup():
        import jax, jax.numpy as jnp
        import numpy as np
        B, T, D, H = (2, 512, 512, 16)
        DH = D // H
        ROPE_BASE = 10000.0

        def _rope(x, cos, sin):
            x0 = x[..., 0::2]
            x1 = x[..., 1::2]
            r0 = cos * x0 - sin * x1
            r1 = sin * x0 + cos * x1
            return jnp.stack((r0, r1), axis=-1).reshape(x.shape)
        key = jax.random.key(seed)
        ks = jax.random.split(key, 5)
        s = D ** (-0.5)
        return {'X': jax.random.normal(ks[0], (B, T, D), dtype=jnp.float32), 'Wq': jax.random.normal(ks[1], (D, D), dtype=jnp.float32) * s, 'Wk': jax.random.normal(ks[2], (D, D), dtype=jnp.float32) * s, 'Wv': jax.random.normal(ks[3], (D, D), dtype=jnp.float32) * s, 'Wo': jax.random.normal(ks[4], (D, D), dtype=jnp.float32) * s}
    _L0_attn_all = _L0_attn_setup()
    _L0_attn_in = {k: v for k, v in _L0_attn_all.items() if k in ('Wq', 'Wk', 'Wv', 'Wo')}
    del _L0_attn_all

    def _L0_cond2_setup():
        import jax, jax.numpy as jnp
        import numpy as np
        B, C, T = (128, 64, 512)
        S, D = (200, 64)
        key = jax.random.key(seed)
        k1, k2, k3 = jax.random.split(key, 3)
        x = jax.random.normal(k1, (B, C, T), dtype=jnp.float32)
        conditions = jax.random.randint(k2, (B,), 0, S, dtype=jnp.int64)
        weights = jax.random.normal(k3, (S, C, D), dtype=jnp.float32) / jnp.sqrt(jnp.float32(C))
        return {'x': x, 'conditions': conditions, 'weights': weights}
    _L0_cond2_all = _L0_cond2_setup()
    _L0_cond2_in = {k: v for k, v in _L0_cond2_all.items() if k in ('weights',)}
    del _L0_cond2_all

    def _L0_ffn_setup():
        import jax, jax.numpy as jnp
        import numpy as np
        B, T, C = (2, 256, 512)
        E, TOPK = (8, 2)
        F_MOE = 352
        F_SHARED = 1408
        key = jax.random.key(seed)
        ks = jax.random.split(key, 9)
        s = 0.02
        return {'x': jax.random.normal(ks[0], (B, T, C), dtype=jnp.float32), 'gate_w': jax.random.normal(ks[1], (E, C), dtype=jnp.float32) * s, 'expert_fc1': jax.random.normal(ks[2], (E, F_MOE, C), dtype=jnp.float32) * s, 'expert_fc2': jax.random.normal(ks[3], (E, F_MOE, C), dtype=jnp.float32) * s, 'expert_proj': jax.random.normal(ks[4], (E, C, F_MOE), dtype=jnp.float32) * s, 'shared_fc1': jax.random.normal(ks[5], (F_SHARED, C), dtype=jnp.float32) * s, 'shared_fc2': jax.random.normal(ks[6], (F_SHARED, C), dtype=jnp.float32) * s, 'shared_proj': jax.random.normal(ks[7], (C, F_SHARED), dtype=jnp.float32) * s, 'shared_gate_w': jax.random.normal(ks[8], (1, C), dtype=jnp.float32) * s}
    _L0_ffn_all = _L0_ffn_setup()
    _L0_ffn_in = {k: v for k, v in _L0_ffn_all.items() if k in ('gate_w', 'expert_fc1', 'expert_fc2', 'expert_proj', 'shared_fc1', 'shared_fc2', 'shared_proj', 'shared_gate_w')}
    del _L0_ffn_all
    return {'x': x, 'itok_B_0_6': itok_B_0_6, 'itok_B_1_198': itok_B_1_198, 'L0_cond_W': _L0_cond_in['W'], 'L0_cond_A': _L0_cond_in['A'], 'L0_cond_Bm': _L0_cond_in['Bm'], 'L0_cond_scalings': _L0_cond_in['scalings'], 'L0_attn_Wq': _L0_attn_in['Wq'], 'L0_attn_Wk': _L0_attn_in['Wk'], 'L0_attn_Wv': _L0_attn_in['Wv'], 'L0_attn_Wo': _L0_attn_in['Wo'], 'L0_cond2_weights': _L0_cond2_in['weights'], 'L0_ffn_gate_w': _L0_ffn_in['gate_w'], 'L0_ffn_expert_fc1': _L0_ffn_in['expert_fc1'], 'L0_ffn_expert_fc2': _L0_ffn_in['expert_fc2'], 'L0_ffn_expert_proj': _L0_ffn_in['expert_proj'], 'L0_ffn_shared_fc1': _L0_ffn_in['shared_fc1'], 'L0_ffn_shared_fc2': _L0_ffn_in['shared_fc2'], 'L0_ffn_shared_proj': _L0_ffn_in['shared_proj'], 'L0_ffn_shared_gate_w': _L0_ffn_in['shared_gate_w']}

def reference(x, itok_B_0_6, itok_B_1_198, L0_cond_W, L0_cond_A, L0_cond_Bm, L0_cond_scalings, L0_attn_Wq, L0_attn_Wk, L0_attn_Wv, L0_attn_Wo, L0_cond2_weights, L0_ffn_gate_w, L0_ffn_expert_fc1, L0_ffn_expert_fc2, L0_ffn_expert_proj, L0_ffn_shared_fc1, L0_ffn_shared_fc2, L0_ffn_shared_proj, L0_ffn_shared_gate_w):
    import jax
    import jax.numpy as jnp

    def _L0_cond_ref(x, W, A, Bm, scalings, adapter_idx):
        import jax, jax.numpy as jnp
        import numpy as np
        B, T, D_IN, D_OUT = (16, 512, 512, 512)
        N_ADAPTERS, RANK = (8, 16)
        H = jnp.einsum('btd,od->bto', x, W)
        A_b = A[adapter_idx]
        B_b = Bm[adapter_idx]
        s_b = scalings[adapter_idx]
        xa = jnp.einsum('btd,brd->btr', x, A_b)
        delta = jnp.einsum('btr,bor->bto', xa, B_b)
        delta = jax.lax.stop_gradient(delta * s_b[:, None, None])
        return H + delta

    def _L0_attn_ref(X, Wq, Wk, Wv, Wo):
        import jax, jax.numpy as jnp
        import numpy as np
        B, T, D, H = (2, 512, 512, 16)
        DH = D // H
        ROPE_BASE = 10000.0

        def _rope(x, cos, sin):
            x0 = x[..., 0::2]
            x1 = x[..., 1::2]
            r0 = cos * x0 - sin * x1
            r1 = sin * x0 + cos * x1
            return jnp.stack((r0, r1), axis=-1).reshape(x.shape)
        b, t, d = X.shape
        Q = X @ Wq.T
        K = X @ Wk.T
        V = X @ Wv.T
        Qh = Q.reshape(b, t, H, DH).transpose(0, 2, 1, 3)
        Kh = K.reshape(b, t, H, DH).transpose(0, 2, 1, 3)
        Vh = V.reshape(b, t, H, DH).transpose(0, 2, 1, 3)
        theta = ROPE_BASE ** (-2.0 * jnp.arange(DH // 2, dtype=jnp.float32) / DH)
        angles = jnp.arange(t, dtype=jnp.float32)[:, None] * theta[None, :]
        cos = jnp.cos(angles).astype(X.dtype)
        sin = jnp.sin(angles).astype(X.dtype)
        Qr = _rope(Qh, cos, sin)
        Kr = _rope(Kh, cos, sin)
        scores = jnp.einsum('bhqd,bhkd->bhqk', Qr, Kr) * DH ** (-0.5)
        causal = jnp.triu(jnp.ones((t, t), dtype=bool), 1)
        scores = jnp.where(causal, jnp.finfo(scores.dtype).min, scores)
        pattern = jax.nn.softmax(scores, axis=-1)
        heads = jnp.einsum('bhqk,bhkd->bqhd', pattern, Vh).reshape(b, t, d)
        return heads @ Wo.T

    def _L0_cond2_ref(x, conditions, weights):
        import jax, jax.numpy as jnp
        import numpy as np
        B, C, T = (128, 64, 512)
        S, D = (200, 64)
        w = weights[conditions]
        return jnp.einsum('bct,bcd->bdt', x, w)

    def _L0_ffn_ref(x, gate_w, expert_fc1, expert_fc2, expert_proj, shared_fc1, shared_fc2, shared_proj, shared_gate_w):
        import jax, jax.numpy as jnp
        import numpy as np
        B, T, C = (2, 256, 512)
        E, TOPK = (8, 2)
        F_MOE = 352
        F_SHARED = 1408
        b, t, c = x.shape
        xf = x.reshape(-1, c)
        n = xf.shape[0]
        router = xf @ gate_w.T
        probs = jax.nn.softmax(router.astype(jnp.float32), axis=1).astype(x.dtype)
        top_p, top_i = jax.lax.top_k(probs, TOPK)
        combine = jnp.zeros((n, E), dtype=x.dtype).at[jnp.arange(n)[:, None], top_i].set(top_p)
        h1 = jnp.einsum('nc,efc->enf', xf, expert_fc1)
        h2 = jnp.einsum('nc,efc->enf', xf, expert_fc2)
        h = jax.nn.silu(h1) * h2
        out_e = jnp.einsum('enf,ecf->enc', h, expert_proj)
        y = jnp.einsum('ne,enc->nc', combine, out_e)
        s1 = xf @ shared_fc1.T
        s2 = xf @ shared_fc2.T
        shared = jax.nn.silu(s1) * s2 @ shared_proj.T
        y = y + jax.nn.sigmoid(xf @ shared_gate_w.T) * shared
        return y.reshape(b, t, c)
    x = x + _L0_attn_ref(_L0_cond_ref(x, L0_cond_W, L0_cond_A, L0_cond_Bm, L0_cond_scalings, itok_B_0_6), L0_attn_Wq, L0_attn_Wk, L0_attn_Wv, L0_attn_Wo)
    x = x + _L0_ffn_ref(_L0_cond2_ref(x, itok_B_1_198, L0_cond2_weights), L0_ffn_gate_w, L0_ffn_expert_fc1, L0_ffn_expert_fc2, L0_ffn_expert_proj, L0_ffn_shared_fc1, L0_ffn_shared_fc2, L0_ffn_shared_proj, L0_ffn_shared_gate_w)
    return x

_drawn_inputs = setup_inputs


def setup_inputs(seed=0):
    import zlib

    import numpy as np

    out = dict(_drawn_inputs(seed))
    spreads = {'L0_cond_scalings': (1.0, 0.6)}
    factors = {'L0_ffn_gate_w': 4.545,
     'L0_ffn_expert_fc1': 3.999,
     'L0_ffn_expert_fc2': 3.901,
     'L0_ffn_expert_proj': 3.905,
     'L0_ffn_shared_gate_w': 23.778,
     'L0_ffn_shared_fc1': 2.712}
    for name, (base, spread) in spreads.items():
        noise = np.random.default_rng([zlib.crc32(name.encode()), seed]).standard_normal(out[name].shape)
        drawn = base * np.exp(spread * noise) if base else spread * noise
        out[name] = jnp.asarray(drawn.astype(out[name].dtype))
    for name, factor in factors.items():
        out[name] = (out[name] * factor).astype(out[name].dtype)
    return out
```

```python
from contextlib import ExitStack

import concourse.bass as bass
from concourse import mybir

P = 128
F32 = mybir.dt.float32
F32R = mybir.dt.float32r
I32 = mybir.dt.int32
ALU = mybir.AluOpType
ACT = mybir.ActivationFunctionType
AX_X = mybir.AxisListType.X

B, T, D = 64, 64, 512
N = B * T
KD = D // P
H, DH = 16, 32
ADAPTERS, RANK = 8, 16
E, TOPK, FE = 8, 2, 352
FS = 1408
KS = FS // P
BLK = 512
NBLK = N // BLK
UNITS = BLK // P
NT = N // P
BB = BLK // T
SCALE = float(DH) ** -0.5
MASKED = -3.0e38
ROUTED = (TOPK * N + E * (P - 1)) // P
TILES = ROUTED + ROUTED % 2
FCH = [(0, 128), (128, 128), (256, 96)]
SWAP = [i ^ 1 for i in range(32)]

XA, HG, KG, QG, VG = 0, 1, 5, 9, 13
GROUPS = 17


def schedule(dense, attn, ahead):
    groups = list(range(GROUPS)) if dense else []
    steps = []

    def d(n=1):
        for _ in range(n):
            if groups:
                steps.append(("dense", groups.pop(0)))

    def x(*pieces):
        if ahead:
            steps.extend(pieces)

    if not attn:
        d(VG)
        x(*[("xload", c) for c in (0, 1)])
        for c in range(KD):
            d()
            x(("xsplit", c))
            if c < KD - 2:
                x(("xload", c + 2))
        return steps
    def pair(kind, u, half):
        steps.extend([(kind, (u, 2 * half)), (kind, (u, 2 * half + 1))])

    def of(kind, u):
        if u >= 0:
            steps.append((kind, u))

    last = UNITS - 1
    for u in range(UNITS):
        of("load", u)
        if u == 0:
            d()
        steps.append(("scores", (u, 0)))
        pair("soft", u, 0)
        if u:
            pair("PT", u - 1, 1)
        of("mixT", u - 2)
        if u > 1:
            x(("xsplit", 2 * u - 4))
        d()
        if u:
            pair("PV", u - 1, 1)
        of("oT", u - 1)
        pair("norm", u, 0)
        steps.append(("scores", (u, 1)))
        pair("soft", u, 1)
        of("router", u - 2)
        if u == 1:
            x(("xload", 0), ("xload", 1))
        if u == 2:
            x(("xload", 2))
        d()
        of("wo", u - 1)
        if u > 1:
            x(("xsplit", 2 * u - 3))
        if u == 2:
            x(("xload", 3))
        pair("PT", u, 0)
        if u < last:
            d()
        else:
            of("mix", u - 1)
        pair("PV", u, 0)
        if u < last:
            of("mix", u - 1)
        pair("norm", u, 1)
    of("mixT", last - 1)
    pair("PT", last, 1)
    d()
    of("router", last - 1)
    pair("PV", last, 1)
    of("oT", last)
    for kind in ("wo", "mix", "mixT", "router"):
        d()
        of(kind, last)
    return steps


def stage_attention(nc, a, keep):
    with ExitStack() as ctx:
        def sb(name, shape, dt=F32):
            return ctx.enter_context(nc.sbuf_tensor(name, shape, dt))

        def sem(name):
            return ctx.enter_context(nc.semaphore(name))

        names = ["W", "Wk", "Wq", "Wv", "Wo"]
        w_hi = {n: sb(f"{n}_hi", [P, KD, D], F32R) for n in names}
        w_lo = {n: sb(f"{n}_lo", [P, KD, D], F32R) for n in names}
        A_hi, A_lo = sb("A_hi", [P, KD, P], F32R), sb("A_lo", [P, KD, P], F32R)
        B_hi, B_lo = sb("B_hi", [P, D], F32R), sb("B_lo", [P, D], F32R)
        gate = sb("gate", [P, KD, E + 1])
        raw = [sb(f"raw{i}", [P, BLK]) for i in range(2)]
        x_hi, x_lo = sb("x_hi", [P, KD, BLK], F32R), sb("x_lo", [P, KD, BLK], F32R)
        h_hi, h_lo = sb("h_hi", [P, KD, BLK], F32R), sb("h_lo", [P, KD, BLK], F32R)
        KT = [sb(f"KT{i}", [P, KD, BLK]) for i in range(2)]
        QT = [sb(f"QT{i}", [P, KD, BLK]) for i in range(2)]
        V = sb("V", [P, UNITS, D])
        rot = [sb(f"rot{i}", [P, BLK]) for i in range(2)]
        swp = [sb(f"swp{i}", [P, BLK]) for i in range(2)]
        probs = sb("probs", [P, 4, 4, P])
        PT = [sb(f"PT{i}", [P, 4, P]) for i in range(2)]
        o_hi, o_lo = sb("o_hi", [P, KD, P], F32R), sb("o_lo", [P, KD, P], F32R)
        x1 = [sb(f"x1_{i}", [P, D]) for i in range(2)]
        xf = sb("xf", [P, D])
        xfT = sb("xfT", [P, KD, P])
        mixw = [sb(f"mixw{i}", [P, P]) for i in range(2)]
        cos, sin = sb("cos", [P, T]), sb("sin", [P, T])
        causal = sb("causal", [P, P])
        ident = sb("ident", [P, P])
        cond = sb("cond", [1, B], I32)
        lidx = sb("lidx", [P, B], I32)
        lidf = sb("lidf", [P, B])
        lmask = sb("lmask", [P, B])
        owner, scal = sb("owner", [P, 1]), sb("scal", [P, 1])
        nmax, sums, rinv = sb("nmax", [P, H]), sb("sums", [P, H]), sb("rinv", [P, H])
        rmax = sb("rmax", [P, H])
        zero = sb("zero", [P, D])
        xa_f = swp[0]
        xa_hi, xa_lo = sb("xa_hi", [P, BLK], F32R), sb("xa_lo", [P, BLK], F32R)

        ps = [ctx.enter_context(nc.psum_tensor(f"ps{i}", [P, 512], F32)) for i in range(8)]
        SB, DB, OB, XB = ps[0:4], ps[4:6], ps[6], ps[7]

        s_const = sem("const_loaded")
        s_wraw = [sem(f"weight_raw{i}") for i in range(3)]
        s_whi, s_wlo = sem("weight_hi"), sem("weight_lo")
        s_lidf, s_lmask = sem("adapter_index"), sem("adapter_mask")
        s_zero, s_dump = sem("zero_set"), sem("dump_rows_zeroed")
        s_raw = [sem(f"x_raw{i}") for i in range(2)]
        s_xhi, s_xlo = sem("x_hi_done"), sem("x_lo_done")
        s_dense = sem("projection_done")
        s_free = [sem(f"projection_bank_free{i}") for i in range(2)]
        s_xahi, s_xalo, s_hhi = sem("xa_hi_done"), sem("xa_lo_done"), sem("h_hi_done")
        s_cosd, s_swp = sem("cos_part"), sem("swapped")
        s_sind, s_rope = sem("sin_part"), sem("rope_done")
        s_sc, s_sm, s_nm, s_max = sem("scores_done"), sem("masked_done"), sem("negmax_done"), sem("max_done")
        s_exp, s_rinv, s_pn = sem("exp_done"), sem("rinv_done"), sem("probs_done")
        s_pt, s_pte, s_pv = sem("probsT_done"), sem("probsT_copied"), sem("pv_done")
        s_ohi, s_olo = sem("o_hi_done"), sem("o_lo_done")
        s_wo, s_x1 = sem("wo_done"), sem("x1_done")
        s_xt = [sem(f"x_tokens_loaded{i}") for i in range(2)]
        s_mw = [sem(f"mix_weights_loaded{i}") for i in range(2)]
        s_x1st = [sem(f"x1_stored{i}") for i in range(2)]
        s_mix, s_xfe, s_mixT, s_xfTe = sem("mix_done"), sem("xf_copied"), sem("mixT_done"), sem("xfT_copied")
        s_turn = sem("buffer_turn")
        s_rt, s_rte = sem("router_done"), sem("logits_copied")
        s_xfst, s_xfTst = sem("xf_stored"), sem("xfT_stored")

        WLOADS = [("A", a["A_T"].rearrange("(k p) m -> p k m", p=P), A_hi, A_lo),
                  ("W", a["W_T"].rearrange("(k p) m -> p k m", p=P), w_hi["W"], w_lo["W"]),
                  ("B", a["B_T"], B_hi, B_lo)]
        WLOADS += [(n, a[f"{n}_T"].rearrange("(k p) m -> p k m", p=P), w_hi[n], w_lo[n])
                   for n in ("Wk", "Wq", "Wv", "Wo")]
        WREADY = {n: i + 1 for i, (n, *_) in enumerate(WLOADS)}
        stage_bufs = [KT[1], QT[1], V]

        def staged(i, dst):
            flat = stage_bufs[i % 3][:].rearrange("p a b -> p (a b)")
            n = dst[:].free_size()
            return flat[:, 0:n]

        def flat(t):
            return t[:] if len(t.shape) == 2 else t[:].rearrange("p a b -> p (a b)")

        def blk(ii, p, per, c=0):
            return ii * (2 * per) + (per * p + c)

        def unit(jj, q, u, per=1, c=0):
            return jj * (2 * UNITS * per) + (per * (UNITS * q + u) + c)

        def bank_of(p, k):
            return (GROUPS * p + k) % 2

        def bank_uses(ii, p, k):
            return ii * GROUPS + (GROUPS * p + k) // 2

        def positive(eng, s, value):
            if isinstance(value, int) and value <= 0:
                return
            eng.wait_ge(s, value)

        CONSTS = 9

        def unit_half(jj, q, u, per):
            return jj * (UNITS * per) + per * ((UNITS * q + u) // 2)

        def run(eng, handlers):
            def step(dense, attn, ahead=None):
                for kind, arg in schedule(dense is not None, attn is not None, ahead is not None):
                    f = handlers.get(kind)
                    if f is not None:
                        block = dense if kind == "dense" else ahead if kind in ("xload", "xsplit") else attn
                        f(*block, arg)

            last = NBLK // 2 - 1
            step((0, 0), None, (0, 1))
            step((0, 1), (0, 0), (1, 0))
            with eng.Fori(1, last) as ii:
                step((ii, 0), (ii - 1, 1), (ii, 1))
                step((ii, 1), (ii, 0), (ii + 1, 0))
            step((last, 0), (last - 1, 1), (last, 1))
            step((last, 1), (last, 0))
            step(None, (last, 1))

        with nc.Block() as block:
            @block.sync
            def _(sp):
                def xload(ii, p, c):
                    if not (isinstance(ii, int) and ii == 0 and p == 0 and c < 2):
                        sp.wait_ge(s_xlo, blk(ii, p, KD, c - 1))
                    sp.dma_start(raw[c % 2][:], a["x_T"][c * P:(c + 1) * P, bass.ds(blk(ii, p, BLK), BLK)])\
                      .then_inc(s_raw[c % 2], 16)

                for i, (n, src, hi, _) in enumerate(WLOADS):
                    if i >= 3:
                        sp.wait_ge(s_wlo, i - 2)
                    dst = staged(i, hi)
                    if len(src.shape) == 3:
                        dst = dst.rearrange("p (k m) -> p k m", k=KD)
                    sp.dma_start(dst, src).then_inc(s_wraw[i % 3], 16)
                    if i == 0:
                        for dst, src in ((cos, a["cos"]), (sin, a["sin"]), (causal, a["causal"]),
                                         (ident, a["ident"]), (owner, a["owner"]), (scal, a["scal"])):
                            sp.dma_start(dst[:], src).then_inc(s_const, 16)
                        sp.dma_start(cond[:], a["cond"]).then_inc(s_const, 16)
                        sp.dma_start(lidx[:], a["lora_idx"].broadcast_to([P, B])).then_inc(s_const, 16)
                        sp.dma_start(gate[:], a["gate_T"].rearrange("(k p) m -> p k m", p=P)).then_inc(s_const, 16)
                    if i == 1:
                        for c in range(KD):
                            xload(0, 0, c)
                sp.wait_ge(s_zero, 3)
                sp.dma_start(a["xf"][N:N + P, :], zero[:]).then_inc(s_dump, 16)
                sp.dma_start(a["out"][N:N + P, :], zero[:]).then_inc(s_dump, 16)
                sp.wait_ge(s_dump, 32)
                sp.wait_ge(s_const, CONSTS * 16)

                def load(jj, q, u):
                    j = u % 2
                    if not (isinstance(jj, int) and jj == 0 and q == 0 and u < 2):
                        sp.wait_ge(s_mix, unit(jj, q, u, 1, -1))
                        sp.sem_inc(s_turn, 1)
                        sp.wait_ge(s_x1st[j], unit_half(jj, q, u, 16))
                    g = unit(jj, q, u)
                    sp.dma_start(x1[j][:], a["x"][bass.ds(g * P, P), :]).then_inc(s_xt[j], 16)
                    for m in range(2):
                        c = sp.value_load(cond[0:1, bass.ds(g * 2 + m, 1)], min_val=0, max_val=a["mix_w"].shape[0] - 1)
                        sp.dma_start(mixw[j][m * T:(m + 1) * T, m * T:(m + 1) * T],
                                     a["mix_w"][bass.ds(c, 1), :, :].rearrange("o c d -> (o c) d")).then_inc(s_mw[j], 16)

                def wo(jj, q, u):
                    g = unit(jj, q, u)
                    sp.wait_ge(s_x1, unit(jj, q, u, 1, 1))
                    sp.dma_start(a["x1"][bass.ds(g * P, P), :], x1[u % 2][:]).then_inc(s_x1st[u % 2], 16)

                def mix(jj, q, u):
                    g = unit(jj, q, u)
                    sp.wait_ge(s_xfe, unit(jj, q, u, 1, 1))
                    sp.dma_start(a["xf"][bass.ds(g * P, P), :], xf[:]).then_inc(s_xfst, 16)

                def mixT(jj, q, u):
                    g = unit(jj, q, u)
                    sp.wait_ge(s_xfTe, unit(jj, q, u, 1, 1))
                    sp.dma_start(a["xfT"][bass.ds(g, 1), :, :].rearrange("g p n -> (g p) n"),
                                 xfT[:].rearrange("p k n -> p (k n)")).then_inc(s_xfTst, 16)

                run(sp, {"xload": xload, "load": load, "wo": wo, "mix": mix, "mixT": mixT})
                for s in s_x1st:
                    sp.wait_ge(s, 16 * (NT // 2))
                sp.wait_ge(s_xfst, 16 * NT)
                sp.wait_ge(s_xfTst, 16 * NT)

            @block.scalar
            def _(act):
                def xsplit(ii, p, c):
                    act.wait_ge(s_raw[c % 2], blk(ii, p, 32, 16 * (c // 2 + 1)))
                    if c == 0:
                        positive(act, s_dense, blk(ii, p, GROUPS, HG + KD - GROUPS))
                    act.activation(x_hi[:, c, :], raw[c % 2][:], ACT.Copy).then_inc(s_xhi, 1)

                for i, (n, _, hi, _) in enumerate(WLOADS):
                    act.wait_ge(s_wraw[i % 3], 16 * (i // 3 + 1))
                    act.activation(flat(hi), staged(i, hi), ACT.Copy).then_inc(s_whi, 1)
                    if i == 1:
                        for c in range(KD):
                            xsplit(0, 0, c)

                def dense(ii, p, k):
                    bank = DB[bank_of(p, k)]
                    if k == XA:
                        act.wait_ge(s_free[bank_of(p, k)], bank_uses(ii, p, k) + 1)
                        act.activation(xa_hi[:], xa_f[:], ACT.Copy).then_inc(s_xahi, 1)
                        return
                    act.wait_ge(s_dense, blk(ii, p, GROUPS, k + 1))
                    if k < KG:
                        act.activation(h_hi[:, k - HG, :], bank[:], ACT.Copy).then_inc(s_hhi, 1)
                    elif k < VG:
                        n = k - KG
                        positive(act, s_swp, blk(ii, p, 8, n - 1))
                        act.activation(rot[n % 2][:], bank[:], ACT.Copy).then_inc(s_free[bank_of(p, k)], 1)
                    else:
                        act.activation(V[:, k - VG, :], bank[:], ACT.Copy).then_inc(s_free[bank_of(p, k)], 1)

                def soft(jj, q, ur):
                    u, r = ur
                    act.wait_ge(s_nm, unit(jj, q, u, 4, r + 1))
                    for c in range(4):
                        m = 4 * r + c
                        last = act.activation(probs[:, r, c, :], probs[:, r, c, :], ACT.Exp,
                                              bias=nmax[:, m:m + 1], accum_out=sums[:, m:m + 1])
                    last.then_inc(s_exp, 1)

                def PTc(jj, q, ur):
                    u, r = ur
                    act.wait_ge(s_pt, unit(jj, q, u, 4, r + 1))
                    positive(act, s_pv, unit(jj, q, u, 4, r - 1))
                    act.activation(PT[r % 2][:].rearrange("p c k -> p (c k)"), SB[r][:], ACT.Copy).then_inc(s_pte, 1)

                def oT(jj, q, u):
                    act.wait_ge(s_pv, unit(jj, q, u, 4, 4))
                    positive(act, s_wo, unit(jj, q, u))
                    act.activation(o_hi[:].rearrange("p c k -> p (c k)"), OB[:], ACT.Copy).then_inc(s_ohi, 1)

                def mix(jj, q, u):
                    act.wait_ge(s_mix, unit(jj, q, u, 1, 1))
                    positive(act, s_mixT, unit(jj, q, u))
                    positive(act, s_xfst, unit(jj, q, u, 16))
                    act.activation(xf[:], XB[:], ACT.Copy).then_inc(s_xfe, 1)

                def mixT(jj, q, u):
                    act.wait_ge(s_mixT, unit(jj, q, u, 1, 1))
                    positive(act, s_rt, unit(jj, q, u))
                    positive(act, s_xfTst, unit(jj, q, u, 16))
                    act.activation(xfT[:].rearrange("p c k -> p (c k)"), XB[:], ACT.Copy).then_inc(s_xfTe, 1)

                run(act, {"xsplit": xsplit, "dense": dense, "soft": soft, "PT": PTc, "oT": oT, "mix": mix, "mixT": mixT})

            @block.gpsimd
            def _(pool):
                nc.gpsimd.memset(zero[:], 0.0).then_inc(s_zero, 1)
                for m in mixw:
                    nc.gpsimd.memset(m[:], 0.0).then_inc(s_zero, 1)

                def dense(ii, p, k):
                    if not KG <= k < VG:
                        return
                    n = k - KG
                    dst = (KT if k < QG else QT)[p][:, n % 4, :]
                    sw = swp[n % 2][:]
                    pool.wait_ge(s_swp, blk(ii, p, 8, n + 1))
                    if k == KG and isinstance(ii, int) and ii == 0 and p == 0:
                        pool.wait_ge(s_const, CONSTS * 16)
                    nc.gpsimd.tensor_tensor(sw.rearrange("p (b t) -> p b t", t=T), sw.rearrange("p (b t) -> p b t", t=T),
                                            sin[:].unsqueeze(1).broadcast_to([P, BB, T]), ALU.mult).then_inc(s_sind, 1)
                    pool.wait_ge(s_sind, blk(ii, p, 8, n + 1))
                    pool.wait_ge(s_cosd, blk(ii, p, 8, n + 1))
                    nc.gpsimd.tensor_tensor(dst, dst, sw, ALU.add).then_inc(s_rope, 1)

                run(pool, {"dense": dense})

            @block.tensor
            def _(pe):
                def three(out, pairs, more=False, before=False):
                    n = len(pairs)
                    for i, ((lh, ll), (rh, rl)) in enumerate(pairs):
                        pe.matmul(out, lh, rh, start=(i == 0 and not before), stop=False)
                        pe.matmul(out, lh, rl, start=False, stop=False)
                        last = pe.matmul(out, ll, rh, start=False, stop=(i == n - 1 and not more))
                    return last

                def need(n, ii, p, upto=0):
                    if isinstance(ii, int) and ii == 0 and p == upto:
                        pe.wait_ge(s_wlo, WREADY[n])

                def dense(ii, p, k):
                    b = bank_of(p, k)
                    out = DB[b][:]
                    positive(pe, s_free[b], bank_uses(ii, p, k))
                    if k == XA:
                        need("A", ii, p)
                        pe.wait_ge(s_xlo, blk(ii, p, KD, KD))
                        last = three(out, [((A_hi[:, c, :], A_lo[:, c, :]), (x_hi[:, c, :], x_lo[:, c, :]))
                                           for c in range(KD)])
                    elif k < KG:
                        if k == HG:
                            need("W", ii, p)
                        m = slice((k - HG) * P, (k - HG + 1) * P)
                        three(out, [((w_hi["W"][:, c, m], w_lo["W"][:, c, m]), (x_hi[:, c, :], x_lo[:, c, :]))
                                    for c in range(KD)], more=True)
                        if k == HG:
                            need("B", ii, p)
                            pe.wait_ge(s_xalo, blk(ii, p, 1, 1))
                        last = three(out, [((B_hi[:, m], B_lo[:, m]), (xa_hi[:], xa_lo[:]))], before=True)
                    elif k < VG:
                        w = "Wk" if k < QG else "Wq"
                        if k == KG:
                            pe.wait_ge(s_free[bank_of(p, KG - 1)], bank_uses(ii, p, KG - 1) + 1)
                        if k in (KG, QG):
                            need(w, ii, p)
                        c0 = (k - KG) % 4
                        m = slice(c0 * P, (c0 + 1) * P)
                        last = three(out, [((w_hi[w][:, c, m], w_lo[w][:, c, m]), (h_hi[:, c, :], h_lo[:, c, :]))
                                           for c in range(KD)])
                    else:
                        if k == VG:
                            need("Wv", ii, p)
                        t = slice((k - VG) * P, (k - VG + 1) * P)
                        last = three(out, [((h_hi[:, c, t], h_lo[:, c, t]), (w_hi["Wv"][:, c, :], w_lo["Wv"][:, c, :]))
                                           for c in range(KD)])
                    last.then_inc(s_dense, 1)

                def scores(jj, q, uh):
                    u, half = uh
                    if u == 0 and half == 0:
                        pe.wait_ge(s_rope, blk(jj, q, 8, 8))
                    t = slice(u * P, (u + 1) * P)
                    for c in range(4):
                        for r in (2 * half, 2 * half + 1):
                            if c == 0:
                                positive(pe, s_pte, unit(jj, q, u, 4, r + 1 - 4))
                            rows = slice(DH * r, DH * r + DH)
                            mm = pe.matmul(SB[r][:, c * P:(c + 1) * P], QT[q][rows, c, t], KT[q][rows, c, t],
                                           start=True, stop=True)
                            if c == 3:
                                mm.then_inc(s_sc, 1)

                def PTp(jj, q, ur):
                    u, r = ur
                    if isinstance(jj, int) and jj == 0 and q == 0 and u == 0 and r == 0:
                        pe.wait_ge(s_const, CONSTS * 16)
                    pe.wait_ge(s_pn, unit(jj, q, u, 4, r + 1))
                    for c in range(4):
                        mm = pe.transpose(SB[r][:, c * P:(c + 1) * P], probs[:, r, c, :], ident[:])
                    mm.then_inc(s_pt, 1)

                def PV(jj, q, ur):
                    u, r = ur
                    if r == 0:
                        if u == 0:
                            last_v(pe, jj, q)
                        positive(pe, s_olo, unit(jj, q, u))
                    pe.wait_ge(s_pte, unit(jj, q, u, 4, r + 1))
                    for c in range(4):
                        h = 4 * c + r
                        mm = pe.matmul(OB[DH * r:DH * (r + 1), c * P:(c + 1) * P], V[:, u, h * DH:(h + 1) * DH],
                                       PT[r % 2][:, c, :], start=True, stop=True)
                    mm.then_inc(s_pv, 1)

                def last_v(pe, jj, q):
                    for k in (GROUPS - 2, GROUPS - 1):
                        pe.wait_ge(s_free[bank_of(q, k)], bank_uses(jj, q, k) + 1)

                def wo(jj, q, u):
                    if isinstance(jj, int) and jj == 0 and q == 0 and u == 0:
                        pe.wait_ge(s_wlo, WREADY["Wo"])
                    pe.wait_ge(s_olo, unit(jj, q, u, 1, 1))
                    positive(pe, s_rte, unit(jj, q, u))
                    last = three(XB[:], [((o_hi[:, c, :], o_lo[:, c, :]), (w_hi["Wo"][:, c, :], w_lo["Wo"][:, c, :]))
                                         for c in range(KD)])
                    last.then_inc(s_wo, 1)

                def mix(jj, q, u):
                    pe.wait_ge(s_x1, unit(jj, q, u, 1, 1))
                    if isinstance(jj, int) and jj == 0 and q == 0 and u == 0:
                        pe.wait_ge(s_zero, 3)
                    pe.wait_ge(s_mw[u % 2], unit_half(jj, q, u, 32) + 32)
                    pe.matmul(XB[:], mixw[u % 2][:], x1[u % 2][:], start=True, stop=True).then_inc(s_mix, 1)

                def mixT(jj, q, u):
                    pe.wait_ge(s_xfe, unit(jj, q, u, 1, 1))
                    for c in range(KD):
                        mm = pe.transpose(XB[:, c * P:(c + 1) * P], xf[:, c * P:(c + 1) * P], ident[:])
                    mm.then_inc(s_mixT, 1)

                def router(jj, q, u):
                    pe.wait_ge(s_xfTe, unit(jj, q, u, 1, 1))
                    for c in range(KD):
                        mm = pe.matmul(XB[:, 0:E + 1], xfT[:, c, :], gate[:, c, :], start=(c == 0), stop=(c == KD - 1))
                    mm.then_inc(s_rt, 1)

                run(pe, {"dense": dense, "scores": scores, "PT": PTp, "PV": PV, "wo": wo, "mix": mix,
                         "mixT": mixT, "router": router})

            @block.vector
            def _(dve):
                v = nc.vector

                def xsplit(ii, p, c):
                    dve.wait_ge(s_xhi, blk(ii, p, KD, c + 1))
                    v.tensor_tensor(x_lo[:, c, :], raw[c % 2][:], x_hi[:, c, :].bitcast(F32), ALU.subtract)\
                     .then_inc(s_xlo, 1)

                for i, (n, _, hi, lo) in enumerate(WLOADS):
                    dve.wait_ge(s_whi, i + 1)
                    v.tensor_tensor(flat(lo), staged(i, hi), flat(hi).bitcast(F32), ALU.subtract).then_inc(s_wlo, 1)
                    if i == 0:
                        dve.wait_ge(s_const, CONSTS * 16)
                        v.tensor_copy(lidf[:], lidx[:]).then_inc(s_lidf, 1)
                        dve.wait_ge(s_lidf, 1)
                        v.tensor_scalar(lmask[:], lidf[:], owner[:, 0:1], scal[:, 0:1], ALU.is_equal, ALU.mult)\
                         .then_inc(s_lmask, 1)
                        dve.wait_ge(s_lmask, 1)
                    if i == 1:
                        for c in range(KD):
                            xsplit(0, 0, c)

                def dense(ii, p, k):
                    b = bank_of(p, k)
                    if k == XA:
                        dve.wait_ge(s_dense, blk(ii, p, GROUPS, 1))
                        positive(dve, s_rope, blk(ii, p, 8))
                        mask = lmask[:, bass.ds(blk(ii, p, BB), BB)].unsqueeze(2).broadcast_to([P, BB, T])
                        v.tensor_tensor(xa_f[:].rearrange("p (b t) -> p b t", t=T),
                                        DB[b][:].rearrange("p (b t) -> p b t", t=T), mask, ALU.mult)\
                         .then_inc(s_free[b], 1)
                        dve.wait_ge(s_xahi, blk(ii, p, 1, 1))
                        v.tensor_tensor(xa_lo[:], xa_f[:], xa_hi[:].bitcast(F32), ALU.subtract).then_inc(s_xalo, 1)
                    elif k < KG:
                        dve.wait_ge(s_hhi, blk(ii, p, KD, k - HG + 1))
                        v.tensor_tensor(h_lo[:, k - HG, :], DB[b][:], h_hi[:, k - HG, :].bitcast(F32), ALU.subtract)\
                         .then_inc(s_free[b], 1)
                    elif k < VG:
                        n = k - KG
                        dst = (KT if k < QG else QT)[p][:, n % 4, :]
                        dve.wait_ge(s_free[b], bank_uses(ii, p, k) + 1)
                        positive(dve, s_rope, blk(ii, p, 8, n - 1))
                        v.tensor_tensor(dst.rearrange("p (b t) -> p b t", t=T), rot[n % 2][:].rearrange("p (b t) -> p b t", t=T),
                                        cos[:].unsqueeze(1).broadcast_to([P, BB, T]), ALU.mult).then_inc(s_cosd, 1)
                        v.stream_shuffle(swp[n % 2][:], rot[n % 2][:], SWAP).then_inc(s_swp, 1)

                def soft(jj, q, ur):
                    u, r = ur
                    n = unit(jj, q, u, 4, r + 1)
                    dve.wait_ge(s_sc, n)
                    v.scalar_tensor_tensor(probs[:, r, :, :], SB[r][:].rearrange("p (c k) -> p c k", c=4), SCALE,
                                           causal[:].unsqueeze(1).broadcast_to([P, 4, P]), ALU.mult, ALU.add)\
                     .then_inc(s_sm, 1)
                    dve.wait_ge(s_sm, n)
                    h = slice(4 * r, 4 * r + 4)
                    v.tensor_reduce(rmax[:, h], probs[:, r, :, :], AX_X, ALU.max).then_inc(s_max, 1)
                    dve.wait_ge(s_max, n)
                    v.tensor_scalar(nmax[:, h], rmax[:, h], -1.0, None, ALU.mult).then_inc(s_nm, 1)

                def norm(jj, q, ur):
                    u, r = ur
                    n = unit(jj, q, u, 4, r + 1)
                    h = slice(4 * r, 4 * r + 4)
                    dve.wait_ge(s_exp, n)
                    v.reciprocal(rinv[:, h], sums[:, h]).then_inc(s_rinv, 1)
                    dve.wait_ge(s_rinv, n)
                    v.tensor_tensor(probs[:, r, :, :], probs[:, r, :, :], rinv[:, h].unsqueeze(2).broadcast_to([P, 4, P]),
                                    ALU.mult).then_inc(s_pn, 1)

                def oT(jj, q, u):
                    dve.wait_ge(s_ohi, unit(jj, q, u, 1, 1))
                    v.tensor_tensor(o_lo[:].rearrange("p c k -> p (c k)"), OB[:],
                                    o_hi[:].rearrange("p c k -> p (c k)").bitcast(F32), ALU.subtract).then_inc(s_olo, 1)

                def wo(jj, q, u):
                    dve.wait_ge(s_wo, unit(jj, q, u, 1, 1))
                    dve.wait_ge(s_xt[u % 2], unit_half(jj, q, u, 16) + 16)
                    v.tensor_tensor(x1[u % 2][:], XB[:], x1[u % 2][:], ALU.add).then_inc(s_x1, 1)

                def router(jj, q, u):
                    dve.wait_ge(s_rt, unit(jj, q, u, 1, 1))
                    v.tensor_copy(keep["logits"][:, bass.ds(unit(jj, q, u), 1), :],
                                  XB[:, 0:E + 1].unsqueeze(1)).then_inc(s_rte, 1)

                run(dve, {"xsplit": xsplit, "dense": dense, "soft": soft, "norm": norm, "oT": oT, "wo": wo, "router": router})


def stage_shared(nc, a, keep):
    with ExitStack() as ctx:
        def sb(name, shape, dt=F32):
            return ctx.enter_context(nc.sbuf_tensor(name, shape, dt))

        def sem(name):
            return ctx.enter_context(nc.semaphore(name))

        PIECE = FS
        f1_hi, f1_lo = sb("f1_hi", [P, KD, FS], F32R), sb("f1_lo", [P, KD, FS], F32R)
        f2_hi, f2_lo = sb("f2_hi", [P, KD, FS], F32R), sb("f2_lo", [P, KD, FS], F32R)
        pj_hi, pj_lo = sb("pj_hi", [P, KS, D], F32R), sb("pj_lo", [P, KS, D], F32R)
        raw = [sb(f"sraw{i}", [P, PIECE]) for i in range(2)]
        x_hi = [sb(f"xb_hi{i}", [P, KD, BLK], F32R) for i in range(2)]
        x_lo = [sb(f"xb_lo{i}", [P, KD, BLK], F32R) for i in range(2)]
        work = sb("work", [P, 4, BLK])
        silu, hf = [work[:, 0, :], work[:, 1, :]], [work[:, 2, :], work[:, 3, :]]
        h_hi = [sb(f"hs_hi{i}", [P, BLK], F32R) for i in range(2)]
        h_lo = [sb(f"hs_lo{i}", [P, BLK], F32R) for i in range(2)]
        x1 = [sb(f"x1s{i}", [P, D]) for i in range(2)]
        gcol = sb("gcol", [P, UNITS])
        prob, pick = sb("prob", [P, NT, E]), sb("pick", [P, 2, NT, E])
        both, slot = sb("both", [P, NT, E]), sb("slot", [P, NT, E])
        tmp, cnt = sb("tmp", [P, NT, E]), sb("cnt", [P, NT, E])
        col, sg = sb("col", [P, NT]), sb("sg", [P, NT])
        ones, before, lower = sb("ones", [P, P]), sb("before", [P, P]), sb("lower", [P, E, E])
        starts, tno = sb("starts", [P, NT]), sb("tno", [P, TILES])
        ntile, ctile, base = sb("ntile", [P, E]), sb("ctile", [P, E]), sb("base", [P, E])
        rowf = sb("rowf", [P, 2, NT])
        rowi, rowa, rowb = sb("rowi", [P, 2, NT], I32), sb("rowa", [P, 2, NT], I32), sb("rowb", [P, 2, NT], I32)
        pair = sb("pair", [P, 2, NT, 2])
        tok = sb("tok", [P, NT], I32)
        tix = [sb(f"tix{i}", [P, 1], I32) for i in range(2)]
        tpay = [sb(f"tpay{i}", [P, 2]) for i in range(2)]

        ps = [ctx.enter_context(nc.psum_tensor(f"pt{i}", [P, 512], F32)) for i in range(8)]
        F1, F2, Y = ps[0:2], ps[2:4], ps[4:8]

        s_const = sem("s2_const")
        s_praw = [sem(f"s2_piece_raw{i}") for i in range(2)]
        s_phi, s_plo = sem("s2_piece_hi"), sem("s2_piece_lo")
        s_xraw = [sem(f"s2_x_raw{i}") for i in range(2)]
        s_xhi, s_xlo = sem("s2_x_hi"), sem("s2_x_lo")
        s_step = sem("s2_routing_step")
        s_exp, s_counts, s_pairs = sem("s2_router_exp"), sem("s2_counts"), sem("s2_pairs")
        s_tinit, s_tcopy = sem("s2_table_init"), sem("s2_pair_copied")
        s_tst = [sem(f"s2_pair_stored{i}") for i in range(2)]
        s_tb, s_issue = sem("s2_routed"), sem("s2_pair_issued")
        s_fc, s_silu, s_h, s_hhi, s_hlo = sem("s2_fc"), sem("s2_silu"), sem("s2_h"), sem("s2_h_hi"), sem("s2_h_lo")
        s_pj, s_yt, s_yo, s_g = sem("s2_proj"), sem("s2_y"), sem("s2_y_read"), sem("s2_gate_column")
        s_x1 = [sem(f"s2_x1_loaded{i}") for i in range(2)]
        s_ost = [sem(f"s2_out_stored{i}") for i in range(2)]

        f1_v = a["sfc1_T"].rearrange("(k p) m -> p k m", p=P)
        f2_v = a["sfc2_T"].rearrange("(k p) m -> p k m", p=P)
        pj_v = a["sproj_T"].rearrange("(k p) m -> p k m", p=P)
        pieces = []
        for src, hi, lo in ((f1_v, f1_hi, f1_lo), (f2_v, f2_hi, f2_lo)):
            pieces += [(src[:, c, :], hi[:, c, :], lo[:, c, :], FS) for c in range(KD)]
        for c in range(0, KS, 2):
            n = min(2, KS - c)
            pieces.append((pj_v[:, c:c + n, :], pj_hi[:, c:c + n, :].rearrange("p a b -> p (a b)"),
                           pj_lo[:, c:c + n, :].rearrange("p a b -> p (a b)"), n * D))
        NP_ = len(pieces)
        FC_PIECES = 2 * KD
        PREFIX_READ = 17

        def blk(ii, p, per, c=0):
            return ii * (2 * per) + (per * p + c)

        def positive(eng, s, value):
            if isinstance(value, int) and value <= 0:
                return
            eng.wait_ge(s, value)

        def blocks(eng, body):
            body(0, 0)
            body(0, 1)
            with eng.Fori(1, NBLK // 2) as ii:
                body(ii, 0)
                body(ii, 1)

        with nc.Block() as block:
            @block.sync
            def _(sp):
                consts = ((ones, a["ones"]), (before, a["before"]), (starts, a["starts"]), (tno, a["tno"]), (tok, a["tok"]))
                for dst, src in consts:
                    sp.dma_start(dst[:], src).then_inc(s_const, 16)
                sp.dma_start(lower[:].rearrange("p a b -> p (a b)"), a["lower"]).then_inc(s_const, 16)
                sp.dma_start(a["table"], a["table_init"]).then_inc(s_tinit, 16)

                def load_x(ii, p):
                    for c in range(UNITS):
                        positive(sp, s_xlo, blk(ii, p, UNITS, c - 1))
                        if isinstance(ii, int) and ii == 0 and p == 0 and c == 0:
                            sp.wait_ge(s_plo, NP_)
                        sp.dma_start(raw[c % 2][:, 0:D], a["xfT"][bass.ds(blk(ii, p, UNITS, c), 1), :, :]
                                     .rearrange("g p n -> (g p) n"))\
                          .then_inc(s_xraw[c % 2], 16)

                for i, (src, _, _, n) in enumerate(pieces):
                    if i >= 2:
                        sp.wait_ge(s_plo, i - 1)
                    dst = raw[i % 2][:, 0:n]
                    if len(src.shape) == 3:
                        dst = dst.rearrange("p (a b) -> p a b", b=D)
                    sp.dma_start(dst, src).then_inc(s_praw[i % 2], 16)
                load_x(0, 0)

                def body(ii, p):
                    if not (isinstance(ii, int) and False):
                        nii, np_ = (ii, 1) if p == 0 else (ii + 1, 0)
                        if not (p == 1 and last_pair[0]):
                            load_x(nii, np_)
                    for t in range(UNITS):
                        j = t % 2
                        n = blk(ii, p, 2, t // 2)
                        positive(sp, s_ost[j], n * 16)
                        row = blk(ii, p, BLK, t * P)
                        sp.dma_start(x1[j][:], a["x1"][bass.ds(row, P), :]).then_inc(s_x1[j], 16)
                        if t >= 1:
                            store(ii, p, t - 1)
                    store(ii, p, UNITS - 1)

                def store(ii, p, t):
                    sp.wait_ge(s_yo, blk(ii, p, UNITS, t + 1))
                    sp.dma_start(a["out"][bass.ds(blk(ii, p, BLK, t * P), P), :], x1[t % 2][:]).then_inc(s_ost[t % 2], 16)

                last_pair = [False]
                body(0, 0)
                body(0, 1)
                with sp.Fori(1, NBLK // 2 - 1) as ii:
                    body(ii, 0)
                    body(ii, 1)
                last_pair[0] = True
                body(NBLK // 2 - 1, 0)
                body(NBLK // 2 - 1, 1)
                for s in s_ost:
                    sp.wait_ge(s, 16 * NT // 2)

            @block.scalar
            def _(act):
                def split_x(ii, p):
                    for c in range(KD):
                        act.wait_ge(s_xraw[c % 2], blk(ii, p, 32, 16 * (c // 2 + 1)))
                        if c == 0:
                            positive(act, s_fc, blk(ii, p, KS, -KS))
                        act.activation(x_hi[p][:, :, c * P:(c + 1) * P], raw[c % 2][:, 0:D].rearrange("p (k n) -> p k n", k=KD),
                                       ACT.Copy).then_inc(s_xhi, 1)

                lg = keep["logits"]
                for i, (_, hi, _, n) in enumerate(pieces):
                    act.wait_ge(s_praw[i % 2], 16 * (i // 2 + 1))
                    act.activation(hi, raw[i % 2][:, 0:n], ACT.Copy).then_inc(s_phi, 1)
                    if i == 0:
                        act.activation(sg[:], lg[:, :, E], ACT.Exp, scale=-1.0).then_inc(s_exp, 1)
                        act.wait_ge(s_step, 2)
                        act.activation(tmp[:], prob[:], ACT.Exp).then_inc(s_exp, 1)
                split_x(0, 0)

                def body(ii, p, more=True):
                    for m in range(KS):
                        n = blk(ii, p, KS, m)
                        j = (KS * p + m) % 2
                        act.wait_ge(s_fc, n + 1)
                        positive(act, s_h, n - 1)
                        act.activation(silu[j], F1[j][:], ACT.Silu).then_inc(s_silu, 1)
                        act.wait_ge(s_h, n + 1)
                        positive(act, s_pj, n - 1)
                        act.activation(h_hi[j][:], hf[j], ACT.Copy).then_inc(s_hhi, 1)
                        if m == 3 and more:
                            split_x(*((ii, 1) if p == 0 else (ii + 1, 0)))

                body(0, 0)
                body(0, 1)
                with act.Fori(1, NBLK // 2 - 1) as ii:
                    body(ii, 0)
                    body(ii, 1)
                body(NBLK // 2 - 1, 0)
                body(NBLK // 2 - 1, 1, False)

            @block.gpsimd
            def _(pool):
                pool.wait_ge(s_pairs, 1)
                pool.wait_ge(s_tinit, 16)
                rows = rowi[:].rearrange("p k j -> p (k j)")
                pays = pair[:].rearrange("p k j w -> p (k j) w")

                def put(ii, j, first):
                    n = ii * 2 + j
                    if not first:
                        pool.wait_ge(s_tst[j], ii * 16)
                    nc.gpsimd.tensor_copy(tix[j][:], rows[:, bass.ds(n, 1)]).then_inc(s_tcopy, 1)
                    nc.gpsimd.tensor_copy(tpay[j][:].unsqueeze(1), pays[:, bass.ds(n, 1), :]).then_inc(s_tcopy, 1)
                    pool.wait_ge(s_tcopy, n * 2 + 2)
                    pool.sem_inc(s_issue, 1)
                    nc.gpsimd.indirect_dma_start(out=a["table"], out_offset=bass.IndirectOffsetOnAxis(ap=tix[j][:], axis=0),
                                                 in_=tpay[j][:], in_offset=None).then_inc(s_tst[j], 16)
                put(0, 0, True)
                put(0, 1, True)
                with pool.Fori(1, NT) as ii:
                    put(ii, 0, False)
                    put(ii, 1, False)
                for s in s_tst:
                    pool.wait_ge(s, 16 * NT)

            @block.tensor
            def _(pe):
                pe.wait_ge(s_const, 96)
                pe.wait_ge(s_tb, 1)
                m = both[:].rearrange("p j e -> p (j e)")
                pe.matmul(F1[0][:, 0:NT * E], before[:], m, start=True, stop=True).then_inc(s_counts, 1)
                pe.matmul(F1[1][:, 0:NT * E], ones[:], m, start=True, stop=True).then_inc(s_counts, 1)

                def three(out, lh, ll, rh, rl, first, last):
                    pe.matmul(out, lh, rh, start=first, stop=False)
                    pe.matmul(out, lh, rl, start=False, stop=False)
                    return pe.matmul(out, ll, rh, start=False, stop=last)

                def proj(ii, p, m):
                    n = blk(ii, p, KS, m)
                    j = (KS * p + m) % 2
                    if m == 0 and isinstance(ii, int) and ii == 0 and p == 0:
                        pe.wait_ge(s_plo, NP_)
                    pe.wait_ge(s_hlo, n + 1)
                    for t in range(UNITS):
                        if m == 0:
                            positive(pe, s_yo, blk(ii, p, UNITS, t + 1 - UNITS))
                        c = slice(t * P, (t + 1) * P)
                        mm = three(Y[t][:], h_hi[j][:, c], h_lo[j][:, c], pj_hi[:, m, :], pj_lo[:, m, :], m == 0, m == KS - 1)
                        if t == UNITS - 1:
                            mm.then_inc(s_pj, 1)
                        elif m == KS - 1:
                            mm.then_inc(s_yt, 1)

                def body(ii, p):
                    for m in range(KS):
                        n = blk(ii, p, KS, m)
                        j = (KS * p + m) % 2
                        if m == 0:
                            pe.wait_ge(s_xlo, blk(ii, p, KD, KD))
                            if isinstance(ii, int) and ii == 0 and p == 0:
                                pe.wait_ge(s_plo, FC_PIECES)
                                pe.wait_ge(s_step, PREFIX_READ)
                        positive(pe, s_h, n - 1)
                        c = slice(m * P, (m + 1) * P)
                        for bank, hi, lo in ((F1[j], f1_hi, f1_lo), (F2[j], f2_hi, f2_lo)):
                            for k in range(KD):
                                mm = three(bank[:], hi[:, k, c], lo[:, k, c], x_hi[p][:, k, :], x_lo[p][:, k, :],
                                           k == 0, k == KD - 1)
                        mm.then_inc(s_fc, 1)
                        if m:
                            proj(ii, p, m - 1)
                    proj(ii, p, KS - 1)

                blocks(pe, body)

            @block.vector
            def _(dve):
                v = nc.vector
                steps = [0]

                def then(ins):
                    ins.then_inc(s_step, 1)
                    steps[0] += 1
                    dve.wait_ge(s_step, steps[0])

                lg = keep["logits"]
                by_e = [P, NT, E]
                wide = work[:].rearrange("p a b -> p (a b)").rearrange("p (j e f) -> p j e f", e=E, f=E)

                def softmax():
                    then(v.tensor_reduce(col[:], lg[:, :, 0:E], AX_X, ALU.max))
                    then(v.tensor_tensor(prob[:], lg[:, :, 0:E], col[:].unsqueeze(2).broadcast_to(by_e), ALU.subtract))
                    dve.wait_ge(s_exp, 2)
                    then(v.tensor_reduce(col[:], tmp[:], AX_X, ALU.add))
                    then(v.reciprocal(col[:], col[:]))
                    then(v.tensor_tensor(prob[:], tmp[:], col[:].unsqueeze(2).broadcast_to(by_e), ALU.mult))
                    then(v.tensor_scalar(sg[:], sg[:], 1.0, None, ALU.add))
                    then(v.reciprocal(keep["gate"][:], sg[:]))

                def rank():
                    mine = prob[:].unsqueeze(3).broadcast_to([P, NT, E, E])
                    other = prob[:].unsqueeze(2).broadcast_to([P, NT, E, E])
                    then(v.tensor_tensor(wide, other, mine, ALU.is_equal))
                    then(v.tensor_tensor(wide, wide, lower[:].unsqueeze(1).broadcast_to([P, NT, E, E]), ALU.mult))
                    then(v.tensor_reduce(tmp[:], wide, AX_X, ALU.add))
                    then(v.tensor_tensor(wide, other, mine, ALU.is_gt))
                    then(v.tensor_reduce(cnt[:], wide, AX_X, ALU.add))
                    then(v.tensor_tensor(cnt[:], cnt[:], tmp[:], ALU.add))
                    for k in range(TOPK):
                        then(v.tensor_scalar(pick[:, k, :, :], cnt[:], float(k), None, ALU.is_equal))
                    v.tensor_tensor(both[:], pick[:, 0, :, :], pick[:, 1, :, :], ALU.add).then_inc(s_tb, 1)
                    dve.wait_ge(s_tb, 1)

                def places():
                    dve.wait_ge(s_counts, 2)
                    then(v.tensor_copy(slot[:].rearrange("p j e -> p (j e)"), F1[0][:, 0:NT * E]))
                    then(v.tensor_copy(tmp[:].rearrange("p j e -> p (j e)"), F1[1][:, 0:NT * E]))
                    assert steps[0] == PREFIX_READ
                    for e in range(E):
                        then(v.tensor_tensor_scan(cnt[:, :, e], ones[:, 0:NT], tmp[:, :, e], 0.0, ALU.mult, ALU.add))
                    then(v.tensor_tensor(slot[:], slot[:], cnt[:], ALU.add))
                    then(v.tensor_tensor(slot[:], slot[:], tmp[:], ALU.subtract))
                    few = work[:, 0, 0:NT * E].rearrange("p (e j) -> p e j", e=E)
                    then(v.tensor_tensor(few, cnt[:, NT - 1, :].unsqueeze(2).broadcast_to([P, E, NT]),
                                         starts[:].unsqueeze(1).broadcast_to([P, E, NT]), ALU.is_gt))
                    then(v.tensor_reduce(ntile[:], few, AX_X, ALU.add))
                    then(v.tensor_tensor_scan(ctile[:], ones[:, 0:E], ntile[:], 0.0, ALU.mult, ALU.add))
                    then(v.tensor_tensor(base[:], ctile[:], ntile[:], ALU.subtract))
                    then(v.tensor_scalar(base[:], base[:], float(P), None, ALU.mult))
                    then(v.tensor_tensor(slot[:], slot[:], base[:].unsqueeze(1).broadcast_to(by_e), ALU.add))
                    ends = work[:, 1:3, :].rearrange("p a b -> p (a b)")[:, 0:TILES * E].rearrange("p (t e) -> p t e", e=E)
                    then(v.tensor_tensor(ends, ctile[:].unsqueeze(1).broadcast_to([P, TILES, E]),
                                         tno[:].unsqueeze(2).broadcast_to([P, TILES, E]), ALU.is_le))
                    then(v.tensor_reduce(tno[:], ends, AX_X, ALU.add))
                    then(v.tensor_scalar(keep["expert"][:], tno[0:1, :], float(E - 1), None, ALU.min))

                def pairs():
                    for k in range(TOPK):
                        then(v.tensor_tensor(tmp[:], slot[:], pick[:, k, :, :], ALU.mult))
                        then(v.tensor_reduce(rowf[:, k, :], tmp[:], AX_X, ALU.add))
                        then(v.tensor_tensor(tmp[:], prob[:], pick[:, k, :, :], ALU.mult))
                        then(v.tensor_reduce(pair[:, k, :, 1], tmp[:], AX_X, ALU.add))
                        then(v.tensor_copy(pair[:, k, :, 0], tok[:]))
                    then(v.tensor_copy(rowi[:], rowf[:]))
                    then(v.tensor_scalar(rowa[:], rowi[:], P - 1, None, ALU.bitwise_and))
                    then(v.tensor_scalar(rowb[:], rowi[:], P.bit_length() - 1, None, ALU.logical_shift_right))
                    then(v.tensor_scalar(rowa[:], rowa[:], TILES, None, ALU.mult))
                    v.tensor_tensor(rowi[:], rowa[:], rowb[:], ALU.add).then_inc(s_pairs, 1)

                def split_x(ii, p):
                    for c in range(KD):
                        dve.wait_ge(s_xhi, blk(ii, p, KD, c + 1))
                        t = slice(c * P, (c + 1) * P)
                        v.tensor_tensor(x_lo[p][:, :, t], raw[c % 2][:, 0:D].rearrange("p (k n) -> p k n", k=KD),
                                        x_hi[p][:, :, t].bitcast(F32), ALU.subtract)\
                         .then_inc(s_xlo, 1)

                parts = [softmax, rank, places, pairs]
                for i, (_, hi, lo, n) in enumerate(pieces):
                    dve.wait_ge(s_phi, i + 1)
                    v.tensor_tensor(lo, raw[i % 2][:, 0:n], hi.bitcast(F32), ALU.subtract).then_inc(s_plo, 1)
                    if i == 0:
                        dve.wait_ge(s_const, 96)
                    if i % 2 == 0 and i // 2 < len(parts):
                        parts[i // 2]()
                split_x(0, 0)

                def body(ii, p, more=True):
                    positive(dve, s_yo, blk(ii, p, UNITS))
                    v.tensor_copy(gcol[:], keep["gate"][:, bass.ds(blk(ii, p, UNITS), UNITS)]).then_inc(s_g, 1)
                    for m in range(KS):
                        n = blk(ii, p, KS, m)
                        j = (KS * p + m) % 2
                        dve.wait_ge(s_silu, n + 1)
                        positive(dve, s_hhi, n - 1)
                        v.tensor_tensor(hf[j], silu[j], F2[j][:], ALU.mult).then_inc(s_h, 1)
                        dve.wait_ge(s_hhi, n + 1)
                        v.tensor_tensor(h_lo[j][:], hf[j], h_hi[j][:].bitcast(F32), ALU.subtract).then_inc(s_hlo, 1)
                        if m == 3 and more:
                            split_x(*((ii, 1) if p == 0 else (ii + 1, 0)))
                    dve.wait_ge(s_g, blk(ii, p, 1, 1))
                    for t in range(UNITS):
                        if t < UNITS - 1:
                            dve.wait_ge(s_yt, blk(ii, p, UNITS - 1, t + 1))
                        else:
                            dve.wait_ge(s_pj, blk(ii, p, KS, KS))
                        dve.wait_ge(s_x1[t % 2], blk(ii, p, 32, 16 * (t // 2 + 1)))
                        v.scalar_tensor_tensor(x1[t % 2][:], Y[t][:], gcol[:, t:t + 1], x1[t % 2][:], ALU.mult, ALU.add)\
                         .then_inc(s_yo, 1)

                body(0, 0)
                body(0, 1)
                with dve.Fori(1, NBLK // 2 - 1) as ii:
                    body(ii, 0)
                    body(ii, 1)
                body(NBLK // 2 - 1, 0)
                body(NBLK // 2 - 1, 1, False)



def stage_experts(nc, a, keep):
    with ExitStack() as ctx:
        def sb(name, shape, dt=F32):
            return ctx.enter_context(nc.sbuf_tensor(name, shape, dt))

        def sem(name):
            return ctx.enter_context(nc.semaphore(name))

        f1, f2 = sb("e_f1", [P, KD, E * FE]), sb("e_f2", [P, KD, E * FE])
        pj = sb("e_pj", [P, E * len(FCH), D])
        ident = sb("e_ident", [P, P])
        table = sb("e_table", [P, TILES, 2])
        two = range(2)
        gix = [sb(f"gix{i}", [P, 1], I32) for i in two]
        six = [sb(f"six{i}", [P, 1], I32) for i in two]
        wt = [sb(f"wt{i}", [P, 1]) for i in two]
        xg = [sb(f"xg{i}", [P, D]) for i in two]
        xgT = [sb(f"xgT{i}", [P, KD, P]) for i in two]
        silu = [sb(f"e_silu{i}", [P, FE]) for i in two]
        h = [sb(f"e_h{i}", [P, FE]) for i in two]
        hT = [sb(f"e_hT{i}", [P, len(FCH), P]) for i in two]
        y = [sb(f"e_y{i}", [P, D]) for i in two]
        ps = [ctx.enter_context(nc.psum_tensor(f"pu{i}", [P, 512], F32)) for i in range(8)]
        TX, TH, H1, H2, Y = ps[0], ps[1], ps[2:4], ps[4:6], ps[6:8]

        s_tab, s_id, s_w = sem("table_loaded"), sem("e_ident_loaded"), sem("expert_weights")
        s_issue = sem("row_move_issued")
        s_gix, s_six, s_wt = sem("gather_index"), sem("scatter_index"), sem("weight_column")
        s_g = [sem(f"gathered{i}") for i in two]
        s_tx, s_txe, s_f1, s_f2 = sem("xT_done"), sem("xT_copied"), sem("fc1_done"), sem("fc2_done")
        s_silu, s_h, s_th, s_the = sem("e_silu_done"), sem("e_h_done"), sem("hT_done"), sem("hT_copied")
        s_pj, s_yo, s_add = sem("e_proj_done"), sem("y_copied"), sem("y_added")

        def at(ii, p, per=1, c=0):
            return ii * (2 * per) + (per * p + c)

        def positive(eng, s, value):
            if isinstance(value, int) and value <= 0:
                return
            eng.wait_ge(s, value)

        def tiles(eng, body):
            for ii in (0, 1):
                body(ii, 0)
                body(ii, 1)
            with eng.Fori(2, TILES // 2 - 1) as ii:
                body(ii, 0)
                body(ii, 1)
            body(TILES // 2 - 1, 0)
            body(TILES // 2 - 1, 1)

        def after(ii, p, n):
            ii, p = ii + (p + n) // 2, (p + n) % 2
            return None if isinstance(ii, int) and ii >= TILES // 2 else (ii, p)

        with nc.Block() as block:
            @block.sync
            def _(sp):
                sp.dma_start(table[:].rearrange("p t w -> p (t w)"), a["table"].rearrange("(p t) w -> p (t w)", p=P))\
                  .then_inc(s_tab, 16)
                sp.dma_start(ident[:], a["ident"]).then_inc(s_id, 16)
                for e in range(E):
                    if e:
                        sp.wait_ge(s_w, 64 * e)
                    cols = slice(e * FE, (e + 1) * FE)
                    sp.dma_start(f1[:, :, cols], a["efc1_T"][e].rearrange("(k p) m -> p k m", p=P)).then_inc(s_w, 16)
                    sp.dma_start(f2[:, :, cols], a["efc2_T"][e].rearrange("(k p) m -> p k m", p=P)).then_inc(s_w, 16)
                    last, rows = FCH[-1]
                    sp.dma_start(pj[:, e * 3:e * 3 + 2, :], a["eproj_T"][e][0:last, :].rearrange("(k p) m -> p k m", p=P))\
                      .then_inc(s_w, 16)
                    sp.dma_start(pj[0:rows, e * 3 + 2, :], a["eproj_T"][e][last:last + rows, :]).then_inc(s_w, 16)

            @block.gpsimd
            def _(pool):
                pool.wait_ge(s_tab, 16)
                toks = table[:].rearrange("p t w -> p (t w)")

                def gather(ii, p):
                    positive(pool, s_tx, at(ii, p, 1, -1))
                    positive(pool, s_g[p], ii * 16)
                    nc.gpsimd.tensor_copy(gix[p][:], toks[:, bass.ds(at(ii, p, 2), 1)]).then_inc(s_gix, 1)
                    pool.wait_ge(s_gix, at(ii, p, 1, 1))
                    pool.sem_inc(s_issue, 1)
                    nc.gpsimd.indirect_dma_start(out=xg[p][:], out_offset=None, in_=a["xf"],
                                                 in_offset=bass.IndirectOffsetOnAxis(ap=gix[p][:], axis=0))\
                      .then_inc(s_g[p], 16)

                def body(ii, p):
                    if (nxt := after(ii, p, 2)) is not None:
                        gather(*nxt)
                    positive(pool, s_add, at(ii, p, 16))
                    nc.gpsimd.tensor_copy(six[p][:], toks[:, bass.ds(at(ii, p, 2), 1)]).then_inc(s_six, 1)
                    pool.wait_ge(s_six, at(ii, p, 1, 1))
                    pool.wait_ge(s_yo, at(ii, p, 1, 1))
                    pool.sem_inc(s_issue, 1)
                    nc.gpsimd.indirect_dma_start(out=a["out"], out_offset=bass.IndirectOffsetOnAxis(ap=six[p][:], axis=0),
                                                 in_=y[p][:], in_offset=None, compute_op=ALU.add).then_inc(s_add, 16)

                gather(0, 0)
                gather(0, 1)
                tiles(pool, body)
                pool.wait_ge(s_add, 16 * TILES)

            @block.scalar
            def _(act):
                def copy_x(ii, p):
                    act.wait_ge(s_tx, at(ii, p, 1, 1))
                    positive(act, s_f2, at(ii, p, 1, -1))
                    act.activation(xgT[p][:].rearrange("p c t -> p (c t)"), TX[:], ACT.Copy).then_inc(s_txe, 1)

                def gate(ii, p):
                    act.wait_ge(s_f1, at(ii, p, 1, 1))
                    positive(act, s_h, at(ii, p, 1, -1))
                    act.activation(silu[p][:], H1[p][:, 0:FE], ACT.Silu).then_inc(s_silu, 1)

                def body(ii, p):
                    if (nxt := after(ii, p, 1)) is not None:
                        gate(*nxt)
                    if (nxt := after(ii, p, 2)) is not None:
                        copy_x(*nxt)

                copy_x(0, 0)
                gate(0, 0)
                copy_x(0, 1)
                tiles(act, body)

            @block.tensor
            def _(pe):
                def turn_x(ii, p):
                    pe.wait_ge(s_g[p], ii * 16 + 16)
                    positive(pe, s_txe, at(ii, p))
                    for c in range(KD):
                        mm = pe.transpose(TX[:, c * P:(c + 1) * P], xg[p][:, c * P:(c + 1) * P], ident[:])
                    mm.then_inc(s_tx, 1)

                def expert(ii, p):
                    return pe.value_load(keep["expert"][0:1, bass.ds(at(ii, p), 1)], min_val=0, max_val=E - 1)

                def fc(ii, p, e, w, bank, done):
                    positive(pe, s_h, at(ii, p, 1, -1))
                    for c in range(KD):
                        mm = pe.matmul(bank[:, 0:FE], xgT[p][:, c, :], w[:, c, bass.ds(e * FE, FE)],
                                       start=(c == 0), stop=(c == KD - 1))
                    mm.then_inc(done, 1)

                def turn_h(ii, p):
                    pe.wait_ge(s_h, at(ii, p, 1, 1))
                    positive(pe, s_the, at(ii, p))
                    for c, (f, w) in enumerate(FCH):
                        mm = pe.transpose(TH[0:w, c * P:(c + 1) * P], h[p][:, f:f + w], ident[:])
                    mm.then_inc(s_th, 1)

                def proj(ii, p, e):
                    pe.wait_ge(s_the, at(ii, p, 1, 1))
                    positive(pe, s_yo, at(ii, p, 1, -1))
                    for c, (_, w) in enumerate(FCH):
                        mm = pe.matmul(Y[p][:], hT[p][0:w, c, :],
                                       pj[0:w, bass.ds(e * len(FCH) + c, 1), :].rearrange("p o n -> p (o n)"),
                                       start=(c == 0), stop=(c == len(FCH) - 1))
                    mm.then_inc(s_pj, 1)

                def body(ii, p):
                    nxt = after(ii, p, 1)
                    if nxt is not None:
                        e1 = expert(*nxt)
                        pe.wait_ge(s_w, e1 * 64 + 64)
                        pe.wait_ge(s_txe, at(*nxt, 1, 1))
                        fc(*nxt, e1, f1, H1[nxt[1]], s_f1)
                    turn_h(ii, p)
                    if nxt is not None:
                        fc(*nxt, e1, f2, H2[nxt[1]], s_f2)
                    proj(ii, p, expert(ii, p))
                    if (nxt := after(ii, p, 2)) is not None:
                        turn_x(*nxt)

                pe.wait_ge(s_id, 16)
                turn_x(0, 0)
                e0 = expert(0, 0)
                pe.wait_ge(s_w, e0 * 64 + 64)
                pe.wait_ge(s_txe, 1)
                fc(0, 0, e0, f1, H1[0], s_f1)
                fc(0, 0, e0, f2, H2[0], s_f2)
                turn_x(0, 1)
                tiles(pe, body)

            @block.vector
            def _(dve):
                v = nc.vector
                flat = table[:].rearrange("p t w -> p (t w)")
                dve.wait_ge(s_tab, 16)

                def weigh(ii, p):
                    v.tensor_copy(wt[p][:], flat[:, bass.ds(at(ii, p, 2, 1), 1)]).then_inc(s_wt, 1)
                    dve.wait_ge(s_wt, at(ii, p, 1, 1))
                    dve.wait_ge(s_silu, at(ii, p, 1, 1))
                    dve.wait_ge(s_f2, at(ii, p, 1, 1))
                    positive(dve, s_th, at(ii, p, 1, -1))
                    v.scalar_tensor_tensor(h[p][:], silu[p][:], wt[p][:, 0:1], H2[p][:, 0:FE], ALU.mult, ALU.mult)\
                     .then_inc(s_h, 1)

                def body(ii, p):
                    dve.wait_ge(s_th, at(ii, p, 1, 1))
                    positive(dve, s_pj, at(ii, p, 1, -1))
                    full = sum(w == P for _, w in FCH)
                    w = FCH[-1][1]
                    v.tensor_copy(hT[p][:, 0:full, :].rearrange("p c t -> p (c t)"), TH[:, 0:full * P])
                    v.tensor_copy(hT[p][0:w, full, :], TH[0:w, full * P:(full + 1) * P]).then_inc(s_the, 1)
                    if (nxt := after(ii, p, 1)) is not None:
                        weigh(*nxt)
                    dve.wait_ge(s_pj, at(ii, p, 1, 1))
                    positive(dve, s_add, at(ii, p, 16, -16))
                    v.tensor_copy(y[p][:], Y[p][:]).then_inc(s_yo, 1)

                weigh(0, 0)
                tiles(dve, body)


def build(nc, a):
    a["xf"] = nc.dram_tensor("xf_rows", [N + P, D], F32).ap()
    a["xfT"] = nc.dram_tensor("xf_T", [NT, P, D], F32).ap()
    a["x1"] = nc.dram_tensor("x1_rows", [N, D], F32).ap()
    a["table"] = nc.dram_tensor("slot_table", [P * TILES, 2], F32).ap()
    with ExitStack() as ctx:
        keep = {"logits": ctx.enter_context(nc.sbuf_tensor("logits", [P, NT, E + 1], F32)),
                "gate": ctx.enter_context(nc.sbuf_tensor("gate_keep", [P, NT], F32)),
                "expert": ctx.enter_context(nc.sbuf_tensor("tile_expert", [1, TILES], I32))}
        stage_attention(nc, a, keep)
        stage_shared(nc, a, keep)
        stage_experts(nc, a, keep)


def layouts(np, inputs):
    x = np.asarray(inputs["x"]).reshape(N, D)
    turned = lambda name: np.ascontiguousarray(np.swapaxes(np.asarray(inputs[name]), -1, -2))
    r = {
        "x": x, "x_T": np.ascontiguousarray(x.T),
        "lora_idx": np.asarray(inputs["itok_B_0_6"]).reshape(1, B),
        "cond": np.asarray(inputs["itok_B_1_198"]).reshape(1, B),
        "W_T": turned("L0_cond_W"),
        "A_T": np.ascontiguousarray(np.asarray(inputs["L0_cond_A"]).reshape(ADAPTERS * RANK, D).T),
        "B_T": turned("L0_cond_Bm").reshape(ADAPTERS * RANK, D),
        "scal": np.repeat(np.asarray(inputs["L0_cond_scalings"]), RANK).reshape(P, 1),
        "Wq_T": turned("L0_attn_Wq"), "Wk_T": turned("L0_attn_Wk"), "Wv_T": turned("L0_attn_Wv"),
        "Wo_T": turned("L0_attn_Wo"),
        "mix_w": np.asarray(inputs["L0_cond2_weights"]),
        "gate_T": np.ascontiguousarray(np.concatenate([np.asarray(inputs["L0_ffn_gate_w"]),
                                                       np.asarray(inputs["L0_ffn_shared_gate_w"])]).T),
        "efc1_T": turned("L0_ffn_expert_fc1"), "efc2_T": turned("L0_ffn_expert_fc2"),
        "eproj_T": turned("L0_ffn_expert_proj"),
        "sfc1_T": turned("L0_ffn_shared_fc1"), "sfc2_T": turned("L0_ffn_shared_fc2"),
        "sproj_T": turned("L0_ffn_shared_proj"),
    }
    f = np.float32
    p = np.arange(P)
    theta = f(10000.0) ** (f(-2.0) * np.arange(DH // 2, dtype=f) / f(DH))
    angles = np.arange(T, dtype=f)[:, None] * theta.astype(f)[None, :]
    lane = (p % DH) // 2
    sign = np.where(p % 2 == 0, -1, 1).astype(f)
    r["cos"] = np.ascontiguousarray(np.cos(angles).astype(f)[:, lane].T)
    r["sin"] = np.ascontiguousarray(np.sin(angles).astype(f)[:, lane].T * sign[:, None])
    same = (p[:, None] // T == p[None, :] // T) & (p[None, :] <= p[:, None])
    r["causal"] = np.where(same, 0, MASKED).astype(f)
    r["ident"] = np.eye(P, dtype=f)
    r["owner"] = (p // RANK).astype(f).reshape(P, 1)
    r["ones"] = np.ones((P, P), f)
    r["before"] = (p[:, None] < p[None, :]).astype(f)
    e = np.arange(E)
    r["lower"] = np.broadcast_to((e[None, :] < e[:, None]).astype(f).reshape(1, E * E), (P, E * E)).copy()
    r["starts"] = np.broadcast_to((np.arange(NT) * P).astype(f), (P, NT)).copy()
    r["tno"] = np.broadcast_to(np.arange(TILES).astype(f), (P, TILES)).copy()
    r["tok"] = np.ascontiguousarray((np.arange(NT)[None, :] * P + p[:, None]).astype(np.int32))
    init = np.zeros((P, TILES, 2), f)
    init[:, :, 0] = (N + p)[:, None]
    r["table_init"] = init.reshape(P * TILES, 2)
    return r


def kernel(**inputs):
    import numpy as np
    import concourse.bacc as bacc
    from concourse.bass_utils import run_bass_kernel_spmd

    nc = bacc.Bacc("TRN2", target_bir_lowering=False, num_devices=1)
    arrays = layouts(np, inputs)
    a = {n: nc.dram_tensor(f"in_{n}", v.shape, mybir.dt.from_np(v.dtype), kind="ExternalInput").ap() for n, v in arrays.items()}
    a["out"] = nc.dram_tensor("out", [N + P, D], F32, kind="ExternalOutput").ap()
    build(nc, a)
    got = run_bass_kernel_spmd(nc, [{f"in_{n}": v for n, v in arrays.items()}], core_ids=[0])
    return got.results[0]["out"][:N].reshape(B, T, D)
```

```python
from contextlib import ExitStack

import concourse.bass as bass
from concourse import mybir

P = 128
F32 = mybir.dt.float32
F32R = mybir.dt.float32r
I32 = mybir.dt.int32
ALU = mybir.AluOpType
ACT = mybir.ActivationFunctionType
AX_X = mybir.AxisListType.X

B, T, D = 64, 64, 512
N = B * T
KD = D // P
H, DH = 16, 32
ADAPTERS, RANK = 8, 16
E, TOPK, FE = 8, 2, 352
FS = 1408
KS = FS // P
PIECE = 2 * KD * P + D
BLK = 512
NBLK = N // BLK
UNITS = BLK // P
NT = N // P
BB = BLK // T
SCALE = float(DH) ** -0.5
MASKED = -3.0e38
ROUTED = (TOPK * N + E * (P - 1)) // P
TILES = ROUTED + ROUTED % 2
KE = -(-FE // P)
PARTS = [(0, KD * FE), (KD * FE, 2 * KD * FE), (2 * KD * FE, 2 * KD * FE + KE * D)]
EW = PARTS[2][1]
RING = 3
ROTS = 3
SWAP = [i ^ 1 for i in range(32)]

XA, HG, KG, QG, VG = 0, 1, 5, 9, 13
GROUPS = 17
LATER = ["Wk", "Wq", "Wv", "Wo"]


def schedule(dense, attn, ahead, carried, final):
    groups = list(range(GROUPS)) if dense else []
    steps = []

    def d(n=1):
        for _ in range(n):
            if groups:
                steps.append(("dense", groups.pop(0)))

    def x(*pieces):
        if ahead:
            steps.extend(pieces)

    if not attn:
        d()
        for i, n in enumerate(LATER):
            steps.append(("weights", i))
            d(2)
        d(VG - 1 - 2 * len(LATER))
        x(*[("xload", c) for c in (0, 1)])
        for c in range(KD):
            d()
            x(("xsplit", c))
            if c < KD - 2:
                x(("xload", c + 2))
        return steps

    def of(kind, u):
        if u >= 0 or carried:
            steps.append((kind, u))

    for u in range(UNITS):
        steps.append(("load", u))
        steps.append(("scores", u))
        steps.append(("soft", (u, 0)))
        steps.append(("exp", (u, 0)))
        steps.append(("soft", (u, 1)))
        d()
        steps.append(("exp", (u, 1)))
        steps.append(("norm", (u, 0)))
        of("wo", u - 1)
        steps.append(("norm", (u, 1)))
        if u > 1:
            x(("xsplit", 2 * u - 4))
        d()
        of("mix", u - 1)
        steps.append(("PT", (u, 0)))
        steps.append(("PT", (u, 1)))
        if u == 1:
            d()
            x(("xload", 0), ("xload", 1))
        if u == 2:
            x(("xload", 2))
        d()
        if u > 1:
            x(("xsplit", 2 * u - 3))
        if u == 2:
            x(("xload", 3))
        of("mixT", u - 1)
        steps.append(("PV", u))
        of("router", u - 1)
        steps.append(("oT", u))
        d()
    if final:
        for kind in ("wo", "mix", "mixT", "router"):
            of(kind, UNITS - 1)
    return steps


def stage_attention(nc, a, keep):
    with ExitStack() as ctx:
        def sb(name, shape, dt=F32):
            return ctx.enter_context(nc.sbuf_tensor(name, shape, dt))

        def sem(name):
            return ctx.enter_context(nc.semaphore(name))

        names = ["W", "Wk", "Wq", "Wv", "Wo"]
        w_hi = {n: sb(f"{n}_hi", [P, KD, D], F32R) for n in names}
        w_lo = {n: sb(f"{n}_lo", [P, KD, D], F32R) for n in names}
        A_hi, A_lo = sb("A_hi", [P, KD, P], F32R), sb("A_lo", [P, KD, P], F32R)
        B_hi, B_lo = sb("B_hi", [P, D], F32R), sb("B_lo", [P, D], F32R)
        gate = sb("gate", [P, KD, E + 1])
        raw = [sb(f"raw{i}", [P, BLK]) for i in range(2)]
        x_hi, x_lo = sb("x_hi", [P, KD, BLK], F32R), sb("x_lo", [P, KD, BLK], F32R)
        h_hi, h_lo = sb("h_hi", [P, KD, BLK], F32R), sb("h_lo", [P, KD, BLK], F32R)
        KT = [sb(f"KT{i}", [P, KD, BLK]) for i in range(2)]
        QT = [sb(f"QT{i}", [P, KD, BLK]) for i in range(2)]
        V = sb("V", [P, UNITS, 2, H // 2, 2 * DH])
        rot = [sb(f"rot{i}", [P, BLK]) for i in range(ROTS)]
        probs = sb("probs", [P, 2, KD, 2, T])
        PT = [sb(f"PT{i}", [P, KD, P]) for i in range(2)]
        o_hi, o_lo = sb("o_hi", [P, KD, P], F32R), sb("o_lo", [P, KD, P], F32R)
        x1 = [sb(f"x1_{i}", [P, D]) for i in range(2)]
        xf = sb("xf", [P, D])
        xfT = sb("xfT", [P, KD, P])
        mixw = [sb(f"mixw{i}", [P, P]) for i in range(2)]
        cos, sin = sb("cos", [P, T]), sb("sin", [P, T])
        causal = sb("causal", [P, T])
        ident = sb("ident", [P, P])
        cond = sb("cond", [1, B], I32)
        lidx = sb("lidx", [P, B], I32)
        lidf = sb("lidf", [P, B])
        lmask = sb("lmask", [P, B])
        owner, scal = sb("owner", [P, 1]), sb("scal", [P, 1])
        rmax, sums, rinv = sb("rmax", [P, 2, H // 2]), sb("sums", [P, 2, H // 2]), sb("rinv", [P, 2, H // 2])
        xa_f = rot[0]
        xa_hi, xa_lo = sb("xa_hi", [P, BLK], F32R), sb("xa_lo", [P, BLK], F32R)

        SB = ctx.enter_context(nc.psum_tensor("score_banks", [P, 4, 512], F32))
        ps = [ctx.enter_context(nc.psum_tensor(f"ps{i}", [P, 512], F32)) for i in range(4)]
        DB, OB, XB = ps[0:2], ps[2], ps[3]

        s_const = sem("const_loaded")
        s_lora = sem("lora_const_loaded")
        s_wraw = [sem(f"weight_raw{i}") for i in range(4)]
        s_whi, s_wlo = sem("weight_hi"), sem("weight_lo")
        s_lidf, s_lmask = sem("adapter_index"), sem("adapter_mask")
        s_zero, s_dump, s_vzero = sem("zero_set"), sem("dump_rows_zeroed"), sem("v_zeroed")
        s_x0 = [sem(f"first_x_raw{i}") for i in range(KD)]
        s_raw = [sem(f"x_raw{i}") for i in range(2)]
        s_xhi, s_xlo = sem("x_hi_done"), sem("x_lo_done")
        s_dense = sem("projection_done")
        s_free = [sem(f"projection_bank_free{i}") for i in range(2)]
        s_xahi, s_xalo, s_hhi = sem("xa_hi_done"), sem("xa_lo_done"), sem("h_hi_done")
        s_cosd, s_swp = sem("cos_part"), sem("swapped")
        s_sind, s_rope = sem("sin_part"), sem("rope_done")
        s_sc, s_sm, s_max, s_off = sem("scores_done"), sem("masked_done"), sem("max_done"), sem("max_subtracted")
        s_exp, s_sum, s_rinv, s_pn = sem("exp_done"), sem("sums_done"), sem("rinv_done"), sem("probs_done")
        s_pt, s_pte, s_pv = sem("probsT_done"), sem("probsT_copied"), sem("pv_done")
        s_ohi, s_olo = sem("o_hi_done"), sem("o_lo_done")
        s_wo, s_x1 = sem("wo_done"), sem("x1_done")
        s_xt = [sem(f"x_tokens_loaded{i}") for i in range(2)]
        s_mw = [sem(f"mix_weights_loaded{i}") for i in range(2)]
        s_x1st = [sem(f"x1_stored{i}") for i in range(2)]
        s_mix, s_xfe, s_mixT, s_xfTe = sem("mix_done"), sem("xf_copied"), sem("mixT_done"), sem("xfT_copied")
        s_turn, s_shuffle = sem("buffer_turn"), sem("shuffle_turn")
        s_rt, s_rte = sem("router_done"), sem("logits_copied")
        s_xfst, s_xfTst = sem("xf_stored"), sem("xfT_stored")

        WLOADS = [("A", a["A_T"].rearrange("(k p) m -> p k m", p=P), A_hi, A_lo),
                  ("W", a["W_T"].rearrange("(k p) m -> p k m", p=P), w_hi["W"], w_lo["W"]),
                  ("B", a["B_T"], B_hi, B_lo)]
        WLOADS += [(n, a[f"{n}_T"].rearrange("(k p) m -> p k m", p=P), w_hi[n], w_lo[n]) for n in LATER]
        FIRST = len(WLOADS) - len(LATER)
        WREADY = {n: i + 1 for i, (n, *_) in enumerate(WLOADS)}
        v_flat = V[:].rearrange("p u b h d -> p (u b h d)")
        stage_bufs = [KT[1][:].rearrange("p a b -> p (a b)"), QT[1][:].rearrange("p a b -> p (a b)"),
                      v_flat[:, 0:KD * D], v_flat[:, KD * D:2 * KD * D]]
        STAGE_OF = [0, 1, 2, 3, 0, 1, 0]
        BEFORE = [STAGE_OF[:i].count(k) for i, k in enumerate(STAGE_OF)]

        def staged(i, dst):
            return stage_bufs[STAGE_OF[i]][:, 0:dst[:].free_size()]

        def flat(t):
            return t[:] if len(t.shape) == 2 else t[:].rearrange("p a b -> p (a b)")

        def heads_of(t, half):
            return t[:, half, :, :, :].rearrange("p c e k -> p (c e) k")

        def blk(ii, p, per, c=0):
            return ii * (2 * per) + (per * p + c)

        def unit(jj, q, u, per=1, c=0):
            return jj * (2 * UNITS * per) + (per * (UNITS * q + u) + c)

        def bank_of(p, k):
            return (GROUPS * p + k) % 2

        def bank_uses(ii, p, k):
            return ii * GROUPS + (GROUPS * p + k) // 2

        def positive(eng, s, value):
            if isinstance(value, int) and value <= 0:
                return
            eng.wait_ge(s, value)

        CONSTS = 6

        def unit_half(jj, q, u, per):
            return jj * (UNITS * per) + per * ((UNITS * q + u) // 2)

        def run(eng, handlers):
            def step(dense, attn, ahead=None):
                first = attn is not None and isinstance(attn[0], int) and attn == (0, 0)
                for kind, arg in schedule(dense is not None, attn is not None, ahead is not None,
                                          carried=not first, final=dense is None):
                    f = handlers.get(kind)
                    if f is not None:
                        block = dense if kind in ("dense", "weights") else ahead if kind in ("xload", "xsplit") else attn
                        f(*block, arg)

            last = NBLK // 2 - 1
            step((0, 0), None, (0, 1))
            step((0, 1), (0, 0), (1, 0))
            with eng.Fori(1, last) as ii:
                step((ii, 0), (ii - 1, 1), (ii, 1))
                step((ii, 1), (ii, 0), (ii + 1, 0))
            step((last, 0), (last - 1, 1), (last, 1))
            step((last, 1), (last, 0))
            step(None, (last, 1))

        with nc.Block() as block:
            @block.sync
            def _(sp):
                def xload(ii, p, c):
                    sp.wait_ge(s_xlo, blk(ii, p, KD, c - 1))
                    sp.dma_start(raw[c % 2][:], a["x_T"][c * P:(c + 1) * P, bass.ds(blk(ii, p, BLK), BLK)])\
                      .then_inc(s_raw[c % 2], 16)

                for i, (n, src, hi, _) in enumerate(WLOADS):
                    if BEFORE[i]:
                        last = max(k for k in range(i) if STAGE_OF[k] == STAGE_OF[i])
                        sp.wait_ge(s_wlo, last + 1)
                    dst = staged(i, hi)
                    if len(src.shape) == 3:
                        dst = dst.rearrange("p (k m) -> p k m", k=KD)
                    sp.dma_start(dst, src).then_inc(s_wraw[STAGE_OF[i]], 16)
                    if n == "A":
                        for c in range(KD):
                            sp.dma_start(KT[0][:, c, :], a["x_T"][c * P:(c + 1) * P, 0:BLK]).then_inc(s_x0[c], 16)
                        for dst, src in ((owner, a["owner"]), (scal, a["scal"]), (lidx, a["lora_idx"].broadcast_to([P, B]))):
                            sp.dma_start(dst[:], src).then_inc(s_lora, 16)
                    if n == "Wk":
                        for dst, src in ((cos, a["cos"]), (sin, a["sin"]), (causal, a["causal"]), (ident, a["ident"]),
                                         (cond, a["cond"]), (gate, a["gate_T"].rearrange("(k p) m -> p k m", p=P))):
                            sp.dma_start(dst[:], src).then_inc(s_const, 16)
                sp.wait_ge(s_zero, 3)
                for rows in (a["xf"], a["out"]):
                    sp.dma_start(rows[N:N + P, :], xfT[:].rearrange("p k n -> p (k n)")).then_inc(s_dump, 16)
                sp.wait_ge(s_dump, 32)
                sp.wait_ge(s_const, CONSTS * 16)

                def load(jj, q, u):
                    j = u % 2
                    if not (isinstance(jj, int) and jj == 0 and q == 0 and u < 2):
                        sp.wait_ge(s_mix, unit(jj, q, u, 1, -1))
                        sp.sem_inc(s_turn, 1)
                        sp.wait_ge(s_x1st[j], unit_half(jj, q, u, 16))
                    g = unit(jj, q, u)
                    sp.dma_start(x1[j][:], a["x"][bass.ds(g * P, P), :]).then_inc(s_xt[j], 16)
                    for m in range(2):
                        c = sp.value_load(cond[0:1, bass.ds(g * 2 + m, 1)], min_val=0, max_val=a["mix_w"].shape[0] - 1)
                        sp.dma_start(mixw[j][m * T:(m + 1) * T, m * T:(m + 1) * T],
                                     a["mix_w"][bass.ds(c, 1), :, :].rearrange("o c d -> (o c) d")).then_inc(s_mw[j], 16)

                def wo(jj, q, u):
                    g = unit(jj, q, u)
                    sp.wait_ge(s_x1, unit(jj, q, u, 1, 1))
                    sp.dma_start(a["x1"][bass.ds(g * P, P), :], x1[u % 2][:]).then_inc(s_x1st[u % 2], 16)

                def mix(jj, q, u):
                    g = unit(jj, q, u)
                    sp.wait_ge(s_xfe, unit(jj, q, u, 1, 1))
                    sp.dma_start(a["xf"][bass.ds(g * P, P), :], xf[:]).then_inc(s_xfst, 16)

                def mixT(jj, q, u):
                    g = unit(jj, q, u)
                    sp.wait_ge(s_xfTe, unit(jj, q, u, 1, 1))
                    sp.dma_start(a["xfT"][bass.ds(g, 1), :, :].rearrange("g p n -> (g p) n"),
                                 xfT[:].rearrange("p k n -> p (k n)")).then_inc(s_xfTst, 16)

                run(sp, {"xload": xload, "load": load, "wo": wo, "mix": mix, "mixT": mixT})
                for s in s_x1st:
                    sp.wait_ge(s, 16 * (NT // 2))
                sp.wait_ge(s_xfst, 16 * NT)
                sp.wait_ge(s_xfTst, 16 * NT)

            @block.scalar
            def _(act):
                def xsplit(ii, p, c):
                    act.wait_ge(s_raw[c % 2], blk(ii, p, 32, 16 * (c // 2 + 1) - 32))
                    if c == 0:
                        positive(act, s_dense, blk(ii, p, GROUPS, HG + KD - GROUPS))
                    act.activation(x_hi[:, c, :], raw[c % 2][:], ACT.Copy).then_inc(s_xhi, 1)

                def split_w(i):
                    _, _, hi, _ = WLOADS[i]
                    act.wait_ge(s_wraw[STAGE_OF[i]], 16 * (BEFORE[i] + 1))
                    act.activation(flat(hi), staged(i, hi), ACT.Copy).then_inc(s_whi, 1)

                for i in range(FIRST):
                    split_w(i)
                    if i == 0:
                        for c in range(KD):
                            act.wait_ge(s_x0[c], 16)
                            act.activation(x_hi[:, c, :], KT[0][:, c, :], ACT.Copy).then_inc(s_xhi, 1)

                def weights(ii, p, n):
                    split_w(FIRST + n)

                def dense(ii, p, k):
                    bank = DB[bank_of(p, k)]
                    if k == XA:
                        act.wait_ge(s_free[bank_of(p, k)], bank_uses(ii, p, k) + 1)
                        act.activation(xa_hi[:], xa_f[:], ACT.Copy).then_inc(s_xahi, 1)
                        return
                    act.wait_ge(s_dense, blk(ii, p, GROUPS, k + 1))
                    if k < KG:
                        act.activation(h_hi[:, k - HG, :], bank[:], ACT.Copy).then_inc(s_hhi, 1)
                    elif k < VG:
                        n = k - KG
                        positive(act, s_rope, blk(ii, p, 8, max(0, n + 1 - ROTS)))
                        act.activation(rot[n % ROTS][:], bank[:], ACT.Copy).then_inc(s_free[bank_of(p, k)], 1)

                def exp(jj, q, uh):
                    u, half = uh
                    act.wait_ge(s_off, unit(jj, q, u, 2, half + 1))
                    act.activation(heads_of(probs, half), heads_of(probs, half), ACT.Exp).then_inc(s_exp, 1)

                def PTc(jj, q, uh):
                    u, half = uh
                    act.wait_ge(s_pt, unit(jj, q, u, 2, half + 1))
                    positive(act, s_pv, unit(jj, q, u))
                    act.activation(PT[half][:].rearrange("p c k -> p (c k)"), SB[:, 2 * half, :], ACT.Copy).then_inc(s_pte, 1)

                def oT(jj, q, u):
                    act.wait_ge(s_pv, unit(jj, q, u, 1, 1))
                    positive(act, s_wo, unit(jj, q, u))
                    act.activation(o_hi[:].rearrange("p c k -> p (c k)"), OB[:], ACT.Copy).then_inc(s_ohi, 1)

                def mix(jj, q, u):
                    act.wait_ge(s_mix, unit(jj, q, u, 1, 1))
                    positive(act, s_mixT, unit(jj, q, u))
                    positive(act, s_xfst, unit(jj, q, u, 16))
                    act.activation(xf[:], XB[:], ACT.Copy).then_inc(s_xfe, 1)

                def mixT(jj, q, u):
                    act.wait_ge(s_mixT, unit(jj, q, u, 1, 1))
                    positive(act, s_rt, unit(jj, q, u))
                    if isinstance(jj, int) and jj == 0 and q == 0 and u == 0:
                        act.wait_ge(s_dump, 32)
                    positive(act, s_xfTst, unit(jj, q, u, 16))
                    act.activation(xfT[:].rearrange("p c k -> p (c k)"), XB[:], ACT.Copy).then_inc(s_xfTe, 1)

                run(act, {"weights": weights, "xsplit": xsplit, "dense": dense, "exp": exp, "PT": PTc, "oT": oT, "mix": mix, "mixT": mixT})

            @block.gpsimd
            def _(pool):
                nc.gpsimd.memset(xfT[:], 0.0).then_inc(s_zero, 1)
                for m in mixw:
                    nc.gpsimd.memset(m[:], 0.0).then_inc(s_zero, 1)
                pool.wait_ge(s_wlo, max(i for i, k in enumerate(STAGE_OF) if k >= 2) + 1)
                nc.gpsimd.memset(V[:], 0.0).then_inc(s_vzero, 1)

                def dense(ii, p, k):
                    if not KG <= k < VG:
                        return
                    n = k - KG
                    dst = (KT if k < QG else QT)[p][:, n % 4, :]
                    pool.wait_ge(s_swp, blk(ii, p, 8, n + 1))
                    if k == KG and isinstance(ii, int) and ii == 0 and p == 0:
                        pool.wait_ge(s_const, CONSTS * 16)
                    nc.gpsimd.tensor_tensor(dst.rearrange("p (b t) -> p b t", t=T), dst.rearrange("p (b t) -> p b t", t=T),
                                            sin[:].unsqueeze(1).broadcast_to([P, BB, T]), ALU.mult).then_inc(s_sind, 1)
                    pool.wait_ge(s_sind, blk(ii, p, 8, n + 1))
                    pool.wait_ge(s_cosd, blk(ii, p, 8, n + 1))
                    nc.gpsimd.tensor_tensor(dst, dst, rot[n % ROTS][:], ALU.add).then_inc(s_rope, 1)

                run(pool, {"dense": dense})

            @block.tensor
            def _(pe):
                def three(out, pairs, more=False, before=False):
                    n = len(pairs)
                    for i, ((lh, ll), (rh, rl)) in enumerate(pairs):
                        pe.matmul(out, lh, rh, start=(i == 0 and not before), stop=False)
                        pe.matmul(out, lh, rl, start=False, stop=False)
                        last = pe.matmul(out, ll, rh, start=False, stop=(i == n - 1 and not more))
                    return last

                def need(n, ii, p, upto=0):
                    if isinstance(ii, int) and ii == 0 and p == upto:
                        pe.wait_ge(s_wlo, WREADY[n])

                def dense(ii, p, k):
                    b = bank_of(p, k)
                    out = DB[b][:]
                    positive(pe, s_free[b], bank_uses(ii, p, k))
                    if k == XA:
                        need("A", ii, p)
                        pe.wait_ge(s_xlo, blk(ii, p, KD, KD))
                        last = three(out, [((A_hi[:, c, :], A_lo[:, c, :]), (x_hi[:, c, :], x_lo[:, c, :]))
                                           for c in range(KD)])
                    elif k < KG:
                        if k == HG:
                            need("W", ii, p)
                        m = slice((k - HG) * P, (k - HG + 1) * P)
                        three(out, [((w_hi["W"][:, c, m], w_lo["W"][:, c, m]), (x_hi[:, c, :], x_lo[:, c, :]))
                                    for c in range(KD)], more=True)
                        if k == HG:
                            need("B", ii, p)
                            pe.wait_ge(s_xalo, blk(ii, p, 1, 1))
                        last = three(out, [((B_hi[:, m], B_lo[:, m]), (xa_hi[:], xa_lo[:]))], before=True)
                    elif k < VG:
                        w = "Wk" if k < QG else "Wq"
                        if k == KG:
                            pe.wait_ge(s_free[bank_of(p, KG - 1)], bank_uses(ii, p, KG - 1) + 1)
                        if k in (KG, QG):
                            need(w, ii, p)
                        c0 = (k - KG) % 4
                        m = slice(c0 * P, (c0 + 1) * P)
                        last = three(out, [((w_hi[w][:, c, m], w_lo[w][:, c, m]), (h_hi[:, c, :], h_lo[:, c, :]))
                                           for c in range(KD)])
                    else:
                        if k == VG:
                            need("Wv", ii, p)
                        t = slice((k - VG) * P, (k - VG + 1) * P)
                        last = three(out, [((h_hi[:, c, t], h_lo[:, c, t]), (w_hi["Wv"][:, c, :], w_lo["Wv"][:, c, :]))
                                           for c in range(KD)])
                    last.then_inc(s_dense, 1)

                def scores(jj, q, u):
                    if u == 0:
                        pe.wait_ge(s_rope, blk(jj, q, 8, 8))
                    positive(pe, s_pte, unit(jj, q, u, 2))
                    for c in range(KD):
                        for r in range(4):
                            for b in range(2):
                                rows = slice(DH * r, DH * r + DH)
                                t = slice(u * P + b * T, u * P + (b + 1) * T)
                                mm = pe.matmul(SB[b * T:(b + 1) * T, r, c * T:(c + 1) * T], QT[q][rows, c, t],
                                               KT[q][rows, c, t], start=True, stop=True)
                    mm.then_inc(s_sc, 1)

                def PTp(jj, q, uh):
                    u, half = uh
                    if isinstance(jj, int) and jj == 0 and q == 0 and u == 0 and half == 0:
                        pe.wait_ge(s_const, CONSTS * 16)
                    pe.wait_ge(s_pn, unit(jj, q, u, 2, half + 1))
                    for c in range(KD):
                        mm = pe.transpose(SB[:, 2 * half, c * P:(c + 1) * P], probs[:, half, c, :, :].rearrange("p e k -> p (e k)"),
                                          ident[:])
                    mm.then_inc(s_pt, 1)

                def PV(jj, q, u):
                    if u == 0:
                        last_v(pe, jj, q)
                    positive(pe, s_olo, unit(jj, q, u))
                    pe.wait_ge(s_pte, unit(jj, q, u, 2, 2))
                    for c in range(KD):
                        for b in range(2):
                            for half in range(2):
                                o = c * P + b * T
                                mm = pe.matmul(OB[half * 2 * DH:(half + 1) * 2 * DH, o:o + T], V[:, u, b, 2 * c + half, :],
                                               PT[half][:, c, b * T:(b + 1) * T], start=True, stop=True)
                    mm.then_inc(s_pv, 1)

                def last_v(pe, jj, q):
                    for k in (GROUPS - 2, GROUPS - 1):
                        pe.wait_ge(s_free[bank_of(q, k)], bank_uses(jj, q, k) + 1)

                def wo(jj, q, u):
                    if isinstance(jj, int) and jj == 0 and q == 0 and u == 0:
                        pe.wait_ge(s_wlo, WREADY["Wo"])
                    pe.wait_ge(s_olo, unit(jj, q, u, 1, 1))
                    positive(pe, s_rte, unit(jj, q, u))
                    last = three(XB[:], [((o_hi[:, c, :], o_lo[:, c, :]), (w_hi["Wo"][:, c, :], w_lo["Wo"][:, c, :]))
                                         for c in range(KD)])
                    last.then_inc(s_wo, 1)

                def mix(jj, q, u):
                    pe.wait_ge(s_x1, unit(jj, q, u, 1, 1))
                    if isinstance(jj, int) and jj == 0 and q == 0 and u == 0:
                        pe.wait_ge(s_zero, 3)
                    pe.wait_ge(s_mw[u % 2], unit_half(jj, q, u, 32) + 32)
                    pe.matmul(XB[:], mixw[u % 2][:], x1[u % 2][:], start=True, stop=True).then_inc(s_mix, 1)

                def mixT(jj, q, u):
                    pe.wait_ge(s_xfe, unit(jj, q, u, 1, 1))
                    for c in range(KD):
                        mm = pe.transpose(XB[:, c * P:(c + 1) * P], xf[:, c * P:(c + 1) * P], ident[:])
                    mm.then_inc(s_mixT, 1)

                def router(jj, q, u):
                    pe.wait_ge(s_xfTe, unit(jj, q, u, 1, 1))
                    for c in range(KD):
                        mm = pe.matmul(XB[:, 0:E + 1], xfT[:, c, :], gate[:, c, :], start=(c == 0), stop=(c == KD - 1))
                    mm.then_inc(s_rt, 1)

                run(pe, {"dense": dense, "scores": scores, "PT": PTp, "PV": PV, "wo": wo, "mix": mix,
                         "mixT": mixT, "router": router})

            @block.vector
            def _(dve):
                v = nc.vector

                def xsplit(ii, p, c):
                    dve.wait_ge(s_xhi, blk(ii, p, KD, c + 1))
                    v.tensor_tensor(x_lo[:, c, :], raw[c % 2][:], x_hi[:, c, :].bitcast(F32), ALU.subtract)\
                     .then_inc(s_xlo, 1)

                def split_w(i):
                    _, _, hi, lo = WLOADS[i]
                    dve.wait_ge(s_whi, i + 1)
                    v.tensor_tensor(flat(lo), staged(i, hi), flat(hi).bitcast(F32), ALU.subtract).then_inc(s_wlo, 1)

                for i in range(FIRST):
                    split_w(i)
                    if i == 0:
                        for c in range(KD):
                            dve.wait_ge(s_xhi, c + 1)
                            v.tensor_tensor(x_lo[:, c, :], KT[0][:, c, :], x_hi[:, c, :].bitcast(F32), ALU.subtract)\
                             .then_inc(s_xlo, 1)
                        dve.wait_ge(s_lora, 48)
                        v.tensor_copy(lidf[:], lidx[:]).then_inc(s_lidf, 1)
                        dve.wait_ge(s_lidf, 1)
                        v.tensor_scalar(lmask[:], lidf[:], owner[:, 0:1], scal[:, 0:1], ALU.is_equal, ALU.mult)\
                         .then_inc(s_lmask, 1)
                        dve.wait_ge(s_lmask, 1)

                def weights(ii, p, n):
                    split_w(FIRST + n)

                def dense(ii, p, k):
                    b = bank_of(p, k)
                    if k == XA:
                        dve.wait_ge(s_dense, blk(ii, p, GROUPS, 1))
                        positive(dve, s_rope, blk(ii, p, 8))
                        mask = lmask[:, bass.ds(blk(ii, p, BB), BB)].unsqueeze(2).broadcast_to([P, BB, T])
                        v.tensor_tensor(xa_f[:].rearrange("p (b t) -> p b t", t=T),
                                        DB[b][:].rearrange("p (b t) -> p b t", t=T), mask, ALU.mult)\
                         .then_inc(s_free[b], 1)
                        dve.wait_ge(s_xahi, blk(ii, p, 1, 1))
                        v.tensor_tensor(xa_lo[:], xa_f[:], xa_hi[:].bitcast(F32), ALU.subtract).then_inc(s_xalo, 1)
                    elif k < KG:
                        dve.wait_ge(s_hhi, blk(ii, p, KD, k - HG + 1))
                        v.tensor_tensor(h_lo[:, k - HG, :], DB[b][:], h_hi[:, k - HG, :].bitcast(F32), ALU.subtract)\
                         .then_inc(s_free[b], 1)
                    elif k < VG:
                        n = k - KG
                        dst = (KT if k < QG else QT)[p][:, n % 4, :]
                        dve.wait_ge(s_free[b], bank_uses(ii, p, k) + 1)
                        dve.sem_inc(s_shuffle, 1)
                        if k == KG and isinstance(ii, int) and ii == 0 and p == 0:
                            dve.wait_ge(s_const, CONSTS * 16)
                        v.stream_shuffle(dst, rot[n % ROTS][:], SWAP).then_inc(s_swp, 1)
                        dve.wait_ge(s_swp, blk(ii, p, 8, n + 1))
                        r = rot[n % ROTS][:].rearrange("p (b t) -> p b t", t=T)
                        v.tensor_tensor(r, r, cos[:].unsqueeze(1).broadcast_to([P, BB, T]), ALU.mult).then_inc(s_cosd, 1)
                    else:
                        if k == VG and isinstance(ii, int) and ii == 0 and p == 0:
                            dve.wait_ge(s_vzero, 1)
                        dve.wait_ge(s_dense, blk(ii, p, GROUPS, k + 1))
                        for bb in range(2):
                            tokens = DB[b][bb * T:(bb + 1) * T, :].rearrange("t (m e d) -> t m e d", e=2, d=DH)
                            for e in range(2):
                                last = v.tensor_copy(V[e * T:(e + 1) * T, k - VG, bb, :, e * DH:(e + 1) * DH], tokens[:, :, e, :])
                        last.then_inc(s_free[b], 1)

                by_head = [P, H // 2, T]

                def soft(jj, q, uh):
                    u, half = uh
                    n = unit(jj, q, u, 2, half + 1)
                    pr = heads_of(probs, half)
                    dve.wait_ge(s_sc, unit(jj, q, u, 1, 1))
                    for r in range(2):
                        last = v.scalar_tensor_tensor(probs[:, half, :, r, :], SB[:, 2 * half + r, 0:KD * T].rearrange("p (c k) -> p c k", c=KD),
                                                      SCALE, causal[:].unsqueeze(1).broadcast_to([P, KD, T]), ALU.mult, ALU.add)
                    last.then_inc(s_sm, 1)
                    dve.wait_ge(s_sm, n)
                    v.tensor_reduce(rmax[:, half, :], pr, AX_X, ALU.max).then_inc(s_max, 1)
                    dve.wait_ge(s_max, n)
                    v.tensor_tensor(pr, pr, rmax[:, half, :].unsqueeze(2).broadcast_to(by_head), ALU.subtract).then_inc(s_off, 1)

                def norm(jj, q, uh):
                    u, half = uh
                    n = unit(jj, q, u, 2, half + 1)
                    pr = heads_of(probs, half)
                    dve.wait_ge(s_exp, n)
                    v.tensor_reduce(sums[:, half, :], pr, AX_X, ALU.add).then_inc(s_sum, 1)
                    dve.wait_ge(s_sum, n)
                    v.reciprocal(rinv[:, half, :], sums[:, half, :]).then_inc(s_rinv, 1)
                    dve.wait_ge(s_rinv, n)
                    v.tensor_tensor(pr, pr, rinv[:, half, :].unsqueeze(2).broadcast_to(by_head), ALU.mult).then_inc(s_pn, 1)

                def oT(jj, q, u):
                    dve.wait_ge(s_ohi, unit(jj, q, u, 1, 1))
                    v.tensor_tensor(o_lo[:].rearrange("p c k -> p (c k)"), OB[:],
                                    o_hi[:].rearrange("p c k -> p (c k)").bitcast(F32), ALU.subtract).then_inc(s_olo, 1)

                def wo(jj, q, u):
                    dve.wait_ge(s_wo, unit(jj, q, u, 1, 1))
                    dve.wait_ge(s_xt[u % 2], unit_half(jj, q, u, 16) + 16)
                    v.tensor_tensor(x1[u % 2][:], XB[:], x1[u % 2][:], ALU.add).then_inc(s_x1, 1)

                def router(jj, q, u):
                    dve.wait_ge(s_rt, unit(jj, q, u, 1, 1))
                    v.tensor_copy(keep["logits"][:, bass.ds(unit(jj, q, u), 1), :],
                                  XB[:, 0:E + 1].unsqueeze(1)).then_inc(s_rte, 1)

                run(dve, {"weights": weights, "xsplit": xsplit, "dense": dense, "soft": soft, "norm": norm, "oT": oT, "wo": wo, "router": router})


def stage_shared(nc, a, keep):
    with ExitStack() as ctx:
        def sb(name, shape, dt=F32):
            return ctx.enter_context(nc.sbuf_tensor(name, shape, dt))

        def sem(name):
            return ctx.enter_context(nc.semaphore(name))

        w_hi, w_lo = sb("s_hi", [P, KS, PIECE], F32R), sb("s_lo", [P, KS, PIECE], F32R)
        wraw = [sb(f"wraw{i}", [P, PIECE]) for i in range(2)]
        xraw = [sb(f"xraw{i}", [P, D]) for i in range(UNITS)]
        x_hi, x_lo = sb("xb_hi", [P, KD, BLK], F32R), sb("xb_lo", [P, KD, BLK], F32R)
        work = sb("work", [P, 4, BLK])
        silu, hf = [work[:, 0, :], work[:, 1, :]], [work[:, 2, :], work[:, 3, :]]
        h_hi = [sb(f"hs_hi{i}", [P, BLK], F32R) for i in range(2)]
        h_lo = [sb(f"hs_lo{i}", [P, BLK], F32R) for i in range(2)]
        x1 = [sb(f"x1s{i}", [P, D]) for i in range(2)]
        gcol = sb("gcol", [P, UNITS])
        rank_tmp = sb("rank_tmp", [P, NT // 2, E, E])
        prob, pick = sb("prob", [P, NT, E]), sb("pick", [P, 2, NT, E])
        both, slot = sb("both", [P, NT, E]), sb("slot", [P, NT, E])
        tmp, cnt = sb("tmp", [P, NT, E]), sb("cnt", [P, NT, E])
        col, sg = sb("col", [P, NT]), sb("sg", [P, NT])
        gate_of = sb("gate_of", [P, NT])
        ones, before, lower = sb("ones", [P, P]), sb("before", [P, P]), sb("lower", [P, E, E])
        starts, tno = sb("starts", [P, NT]), sb("tno", [P, TILES])
        ntile, ctile, base = sb("ntile", [P, E]), sb("ctile", [P, E]), sb("base", [P, E])
        rowf = sb("rowf", [P, 2, NT])
        rowi, rowa, rowb = sb("rowi", [P, 2, NT], I32), sb("rowa", [P, 2, NT], I32), sb("rowb", [P, 2, NT], I32)
        pair = sb("pair", [P, 2, NT, 2])
        tok = sb("tok", [P, NT], I32)
        tix = [sb(f"tix{i}", [P, 1], I32) for i in range(2)]
        tpay = [sb(f"tpay{i}", [P, 2]) for i in range(2)]

        ps = [ctx.enter_context(nc.psum_tensor(f"pt{i}", [P, 512], F32)) for i in range(8)]
        F1, F2, Y = ps[0:2], ps[2:4], ps[4:8]

        s_const = sem("s2_const")
        s_praw = [sem(f"s2_piece_raw{i}") for i in range(2)]
        s_phi, s_plo = sem("s2_piece_hi"), sem("s2_piece_lo")
        s_xraw = [sem(f"s2_x_raw{i}") for i in range(UNITS)]
        s_xhi, s_xlo = sem("s2_x_hi"), sem("s2_x_lo")
        s_step = sem("s2_routing_step")
        s_exp, s_counts, s_pairs = sem("s2_router_exp"), sem("s2_counts"), sem("s2_pairs")
        s_tinit, s_tcopy = sem("s2_table_init"), sem("s2_pair_copied")
        s_tst = [sem(f"s2_pair_stored{i}") for i in range(2)]
        s_tb, s_issue = sem("s2_routed"), sem("s2_pair_issued")
        s_fc, s_silu, s_h, s_hhi, s_hlo = sem("s2_fc"), sem("s2_silu"), sem("s2_h"), sem("s2_h_hi"), sem("s2_h_lo")
        s_pj, s_yt, s_yo, s_g = sem("s2_proj"), sem("s2_y"), sem("s2_y_read"), sem("s2_gate_column")
        s_x1 = [sem(f"s2_x1_loaded{i}") for i in range(2)]
        s_ost = [sem(f"s2_out_stored{i}") for i in range(2)]

        PREFIX_READ = 22

        def blk(ii, p, per, c=0):
            return ii * (2 * per) + (per * p + c)

        def positive(eng, s, value):
            if isinstance(value, int) and value <= 0:
                return
            eng.wait_ge(s, value)

        def blocks(eng, body):
            last = NBLK // 2 - 1
            body(0, 0, (0, 1))
            body(0, 1, (1, 0))
            with eng.Fori(1, last) as ii:
                body(ii, 0, (ii, 1))
                body(ii, 1, (ii + 1, 0))
            body(last, 0, (last, 1))
            body(last, 1, None)

        def is_block(ii, p, n):
            return isinstance(ii, int) and 2 * ii + p == n

        with nc.Block() as block:
            @block.sync
            def _(sp):
                def load_x(ii, p):
                    for u in range(UNITS):
                        positive(sp, s_xlo, blk(ii, p, UNITS, u + 1 - UNITS))
                        sp.dma_start(xraw[u][:], a["xfT"][bass.ds(blk(ii, p, UNITS, u), 1), :, :]
                                     .rearrange("g p n -> (g p) n")).then_inc(s_xraw[u], 16)

                def piece(m):
                    if m >= 2:
                        sp.wait_ge(s_plo, m - 1)
                    sp.dma_start(wraw[m % 2][:], a["shared_w"][m]).then_inc(s_praw[m % 2], 16)

                load_x(0, 0)
                piece(0)
                piece(1)
                consts = ((ones, a["ones"]), (before, a["before"]), (starts, a["starts"]), (tno, a["tno"]), (tok, a["tok"]))
                for dst, src in consts:
                    sp.dma_start(dst[:], src).then_inc(s_const, 16)
                sp.dma_start(lower[:].rearrange("p a b -> p (a b)"), a["lower"]).then_inc(s_const, 16)
                sp.dma_start(a["table"], a["table_init"]).then_inc(s_tinit, 16)
                for m in range(2, KS):
                    piece(m)

                def store(ii, p, t):
                    sp.wait_ge(s_yo, blk(ii, p, UNITS, t + 1))
                    sp.dma_start(a["out"][bass.ds(blk(ii, p, BLK, t * P), P), :], x1[t % 2][:]).then_inc(s_ost[t % 2], 16)

                def body(ii, p, nxt):
                    if nxt is not None:
                        load_x(*nxt)
                    for t in range(UNITS):
                        positive(sp, s_ost[t % 2], blk(ii, p, 32, 16 * (t // 2)))
                        sp.dma_start(x1[t % 2][:], a["x1"][bass.ds(blk(ii, p, BLK, t * P), P), :]).then_inc(s_x1[t % 2], 16)
                        if t >= 1:
                            store(ii, p, t - 1)
                    store(ii, p, UNITS - 1)

                blocks(sp, body)
                for s in s_ost:
                    sp.wait_ge(s, 16 * NT // 2)

            @block.scalar
            def _(act):
                def split_x(ii, p):
                    positive(act, s_fc, blk(ii, p, KS))
                    for u in range(UNITS):
                        act.wait_ge(s_xraw[u], blk(ii, p, 16, 16))
                        act.activation(x_hi[:, :, u * P:(u + 1) * P], xraw[u][:].rearrange("p (k n) -> p k n", k=KD),
                                       ACT.Copy).then_inc(s_xhi, 1)

                def piece(m):
                    act.wait_ge(s_praw[m % 2], 16 * (m // 2 + 1))
                    act.activation(w_hi[:, m, :], wraw[m % 2][:], ACT.Copy).then_inc(s_phi, 1)

                lg = keep["logits"]
                split_x(0, 0)
                piece(0)
                piece(1)
                act.activation(sg[:], lg[:, :, E], ACT.Exp, scale=-1.0).then_inc(s_exp, 1)
                act.wait_ge(s_step, 2)
                act.activation(tmp[:], prob[:], ACT.Exp).then_inc(s_exp, 1)

                def body(ii, p, nxt):
                    for m in range(KS):
                        n = blk(ii, p, KS, m)
                        j = (KS * p + m) % 2
                        act.wait_ge(s_fc, n + 1)
                        positive(act, s_h, n - 1)
                        act.activation(silu[j], F1[j][:], ACT.Silu).then_inc(s_silu, 1)
                        act.wait_ge(s_h, n + 1)
                        positive(act, s_pj, n - 1)
                        act.activation(h_hi[j][:], hf[j], ACT.Copy).then_inc(s_hhi, 1)
                        if is_block(ii, p, 0) and m + 2 < KS:
                            piece(m + 2)
                    if nxt is not None:
                        split_x(*nxt)

                blocks(act, body)

            @block.gpsimd
            def _(pool):
                pool.wait_ge(s_pairs, 1)
                pool.wait_ge(s_tinit, 16)
                rows = rowi[:].rearrange("p k j -> p (k j)")
                pays = pair[:].rearrange("p k j w -> p (k j) w")

                def put(ii, j, first):
                    n = ii * 2 + j
                    if not first:
                        pool.wait_ge(s_tst[j], ii * 16)
                    nc.gpsimd.tensor_copy(tix[j][:], rows[:, bass.ds(n, 1)]).then_inc(s_tcopy, 1)
                    nc.gpsimd.tensor_copy(tpay[j][:].unsqueeze(1), pays[:, bass.ds(n, 1), :]).then_inc(s_tcopy, 1)
                    pool.wait_ge(s_tcopy, n * 2 + 2)
                    pool.sem_inc(s_issue, 1)
                    nc.gpsimd.indirect_dma_start(out=a["table"], out_offset=bass.IndirectOffsetOnAxis(ap=tix[j][:], axis=0),
                                                 in_=tpay[j][:], in_offset=None).then_inc(s_tst[j], 16)
                put(0, 0, True)
                put(0, 1, True)
                with pool.Fori(1, NT) as ii:
                    put(ii, 0, False)
                    put(ii, 1, False)
                for s in s_tst:
                    pool.wait_ge(s, 16 * NT)

            @block.tensor
            def _(pe):
                def three(out, lh, ll, rh, rl, first, last):
                    pe.matmul(out, lh, rh, start=first, stop=False)
                    pe.matmul(out, lh, rl, start=False, stop=False)
                    return pe.matmul(out, ll, rh, start=False, stop=last)

                def counts():
                    pe.wait_ge(s_const, 96)
                    pe.wait_ge(s_tb, 1)
                    pe.wait_ge(s_yo, 1)
                    m = both[:].rearrange("p j e -> p (j e)")
                    pe.matmul(Y[0][:, 0:NT * E], before[:], m, start=True, stop=True)
                    pe.matmul(Y[0][:, NT * E:2 * NT * E], ones[:], m, start=True, stop=True).then_inc(s_counts, 1)

                def proj(ii, p, m):
                    n = blk(ii, p, KS, m)
                    j = (KS * p + m) % 2
                    pe.wait_ge(s_hlo, n + 1)
                    if is_block(ii, p, 1) and m == 0:
                        pe.wait_ge(s_step, PREFIX_READ)
                    w = slice(2 * KD * P, PIECE)
                    for t in range(UNITS):
                        if m == 0:
                            positive(pe, s_yo, blk(ii, p, UNITS, t + 1 - UNITS))
                        c = slice(t * P, (t + 1) * P)
                        mm = three(Y[t][:], h_hi[j][:, c], h_lo[j][:, c], w_hi[:, m, w], w_lo[:, m, w], m == 0, m == KS - 1)
                        if t == UNITS - 1:
                            mm.then_inc(s_pj, 1)
                        elif m == KS - 1:
                            mm.then_inc(s_yt, 1)

                def body(ii, p, nxt):
                    for m in range(KS):
                        n = blk(ii, p, KS, m)
                        j = (KS * p + m) % 2
                        if m == 0:
                            pe.wait_ge(s_xlo, blk(ii, p, UNITS, UNITS))
                        if is_block(ii, p, 0):
                            pe.wait_ge(s_plo, m + 1)
                        positive(pe, s_h, n - 1)
                        for f, bank in ((0, F1[j]), (1, F2[j])):
                            for k in range(KD):
                                c = slice((f * KD + k) * P, (f * KD + k + 1) * P)
                                mm = three(bank[:], w_hi[:, m, c], w_lo[:, m, c], x_hi[:, k, :], x_lo[:, k, :],
                                           k == 0, k == KD - 1)
                        mm.then_inc(s_fc, 1)
                        if m:
                            proj(ii, p, m - 1)
                    proj(ii, p, KS - 1)
                    if is_block(ii, p, 0):
                        counts()

                blocks(pe, body)

            @block.vector
            def _(dve):
                v = nc.vector
                steps = [0]

                def then(ins):
                    ins.then_inc(s_step, 1)
                    steps[0] += 1
                    dve.wait_ge(s_step, steps[0])

                lg = keep["logits"]
                by_e = [P, NT, E]
                wide = rank_tmp[:]
                pairwise = [P, NT // 2, E, E]
                halves = [(t, prob[:, t, :].unsqueeze(3).broadcast_to(pairwise), prob[:, t, :].unsqueeze(2).broadcast_to(pairwise))
                          for t in (slice(0, NT // 2), slice(NT // 2, NT))]

                def softmax():
                    dve.wait_ge(s_exp, 2)
                    then(v.tensor_reduce(col[:], tmp[:], AX_X, ALU.add))
                    then(v.reciprocal(col[:], col[:]))
                    then(v.tensor_tensor(prob[:], tmp[:], col[:].unsqueeze(2).broadcast_to(by_e), ALU.mult))
                    then(v.tensor_scalar(sg[:], sg[:], 1.0, None, ALU.add))
                    then(v.reciprocal(gate_of[:], sg[:]))

                def equal_before():
                    for t, mine, other in halves:
                        then(v.tensor_tensor(wide, other, mine, ALU.is_equal))
                        then(v.tensor_tensor(wide, wide, lower[:].unsqueeze(1).broadcast_to(pairwise), ALU.mult))
                        then(v.tensor_reduce(tmp[:, t, :], wide, AX_X, ALU.add))

                def higher():
                    for t, mine, other in halves:
                        then(v.tensor_tensor(wide, other, mine, ALU.is_gt))
                        then(v.tensor_reduce(cnt[:, t, :], wide, AX_X, ALU.add))
                    then(v.tensor_tensor(cnt[:], cnt[:], tmp[:], ALU.add))
                    for k in range(TOPK):
                        then(v.tensor_scalar(pick[:, k, :, :], cnt[:], float(k), None, ALU.is_equal))
                    v.tensor_tensor(both[:], pick[:, 0, :, :], pick[:, 1, :, :], ALU.add).then_inc(s_tb, 1)
                    dve.wait_ge(s_tb, 1)

                def read_counts():
                    dve.wait_ge(s_counts, 1)
                    then(v.tensor_copy(slot[:].rearrange("p j e -> p (j e)"), Y[0][:, 0:NT * E]))
                    then(v.tensor_copy(tmp[:].rearrange("p j e -> p (j e)"), Y[0][:, NT * E:2 * NT * E]))
                    assert steps[0] == PREFIX_READ

                def places():
                    for e in range(E):
                        then(v.tensor_tensor_scan(cnt[:, :, e], ones[:, 0:NT], tmp[:, :, e], 0.0, ALU.mult, ALU.add))
                    then(v.tensor_tensor(slot[:], slot[:], cnt[:], ALU.add))
                    then(v.tensor_tensor(slot[:], slot[:], tmp[:], ALU.subtract))
                    few = both[:].rearrange("p j e -> p (j e)").rearrange("p (e j) -> p e j", e=E)
                    then(v.tensor_tensor(few, cnt[:, NT - 1, :].unsqueeze(2).broadcast_to([P, E, NT]),
                                         starts[:].unsqueeze(1).broadcast_to([P, E, NT]), ALU.is_gt))
                    then(v.tensor_reduce(ntile[:], few, AX_X, ALU.add))
                    then(v.tensor_scalar(ntile[:], ntile[:], 1.0, None, ALU.max))
                    then(v.tensor_tensor_scan(ctile[:], ones[:, 0:E], ntile[:], 0.0, ALU.mult, ALU.add))
                    then(v.tensor_tensor(base[:], ctile[:], ntile[:], ALU.subtract))
                    then(v.tensor_scalar(base[:], base[:], float(P), None, ALU.mult))
                    then(v.tensor_tensor(slot[:], slot[:], base[:].unsqueeze(1).broadcast_to(by_e), ALU.add))
                    ends = rank_tmp[:].rearrange("p j e f -> p (j e f)")[:, 0:TILES * E].rearrange("p (t e) -> p t e", e=E)
                    then(v.tensor_tensor(ends, ctile[:].unsqueeze(1).broadcast_to([P, TILES, E]),
                                         tno[:].unsqueeze(2).broadcast_to([P, TILES, E]), ALU.is_le))
                    then(v.tensor_reduce(tno[:], ends, AX_X, ALU.add))
                    of = tno[0:1, :]
                    then(v.tensor_scalar(of, of, float(E - 1), None, ALU.min))
                    then(v.tensor_copy(keep["expert"][:], of))
                    more, which = rank_tmp[0:1, 0:2, :, :].rearrange("p j e f -> p (j e f)")[:, 0:TILES], \
                        rank_tmp[0:1, 2:4, :, :].rearrange("p j e f -> p (j e f)")[:, 0:TILES]
                    then(v.tensor_tensor(more[:, 0:TILES - 1], of[:, 1:TILES], of[:, 0:TILES - 1], ALU.subtract))
                    then(v.tensor_scalar(which[:, 0:TILES - 1], of[:, 1:TILES], float(1 - E), None, ALU.add))
                    then(v.tensor_tensor(more[:, 0:TILES - 1], more[:, 0:TILES - 1], which[:, 0:TILES - 1], ALU.mult))
                    then(v.tensor_scalar(keep["fresh"][:, 0:TILES - 1], more[:, 0:TILES - 1], float(E), None, ALU.add))

                def pairs():
                    for k in range(TOPK):
                        then(v.tensor_tensor(tmp[:], slot[:], pick[:, k, :, :], ALU.mult))
                        then(v.tensor_reduce(rowf[:, k, :], tmp[:], AX_X, ALU.add))
                        then(v.tensor_tensor(tmp[:], prob[:], pick[:, k, :, :], ALU.mult))
                        then(v.tensor_reduce(pair[:, k, :, 1], tmp[:], AX_X, ALU.add))
                        then(v.tensor_copy(pair[:, k, :, 0], tok[:]))
                    then(v.tensor_copy(rowi[:], rowf[:]))
                    then(v.tensor_scalar(rowa[:], rowi[:], P - 1, None, ALU.bitwise_and))
                    then(v.tensor_scalar(rowb[:], rowi[:], P.bit_length() - 1, None, ALU.logical_shift_right))
                    then(v.tensor_scalar(rowa[:], rowa[:], TILES, None, ALU.mult))
                    v.tensor_tensor(rowi[:], rowa[:], rowb[:], ALU.add).then_inc(s_pairs, 1)

                def split_x(ii, p):
                    for u in range(UNITS):
                        dve.wait_ge(s_xhi, blk(ii, p, UNITS, u + 1))
                        t = slice(u * P, (u + 1) * P)
                        v.tensor_tensor(x_lo[:, :, t], xraw[u][:].rearrange("p (k n) -> p k n", k=KD),
                                        x_hi[:, :, t].bitcast(F32), ALU.subtract).then_inc(s_xlo, 1)

                def piece(m):
                    dve.wait_ge(s_phi, m + 1)
                    v.tensor_tensor(w_lo[:, m, :], wraw[m % 2][:], w_hi[:, m, :].bitcast(F32), ALU.subtract).then_inc(s_plo, 1)

                split_x(0, 0)
                piece(0)
                piece(1)
                then(v.tensor_reduce(col[:], lg[:, :, 0:E], AX_X, ALU.max))
                then(v.tensor_tensor(prob[:], lg[:, :, 0:E], col[:].unsqueeze(2).broadcast_to(by_e), ALU.subtract))

                def body(ii, p, nxt):
                    positive(dve, s_yo, blk(ii, p, UNITS))
                    v.tensor_copy(gcol[:], gate_of[:, bass.ds(blk(ii, p, UNITS), UNITS)]).then_inc(s_g, 1)
                    for m in range(KS):
                        n = blk(ii, p, KS, m)
                        j = (KS * p + m) % 2
                        dve.wait_ge(s_silu, n + 1)
                        positive(dve, s_hhi, n - 1)
                        v.tensor_tensor(hf[j], silu[j], F2[j][:], ALU.mult).then_inc(s_h, 1)
                        dve.wait_ge(s_hhi, n + 1)
                        v.tensor_tensor(h_lo[j][:], hf[j], h_hi[j][:].bitcast(F32), ALU.subtract).then_inc(s_hlo, 1)
                        if is_block(ii, p, 0):
                            if m + 2 < KS:
                                piece(m + 2)
                            if m == 4:
                                equal_before()
                            if m == 6:
                                higher()
                        if is_block(ii, p, 1) and m == 1:
                            places()
                        if is_block(ii, p, 1) and m == 3:
                            pairs()
                    if nxt is not None:
                        split_x(*nxt)
                    dve.wait_ge(s_g, blk(ii, p, 1, 1))
                    for t in range(UNITS):
                        if t < UNITS - 1:
                            dve.wait_ge(s_yt, blk(ii, p, UNITS - 1, t + 1))
                        else:
                            dve.wait_ge(s_pj, blk(ii, p, KS, KS))
                        dve.wait_ge(s_x1[t % 2], blk(ii, p, 32, 16 * (t // 2 + 1)))
                        v.scalar_tensor_tensor(x1[t % 2][:], Y[t][:], gcol[:, t:t + 1], x1[t % 2][:], ALU.mult, ALU.add)\
                         .then_inc(s_yo, 1)
                    if is_block(ii, p, 0):
                        read_counts()

                dve.wait_ge(s_const, 96)
                softmax()
                blocks(dve, body)


def stage_experts(nc, a, keep):
    with ExitStack() as ctx:
        def sb(name, shape, dt=F32):
            return ctx.enter_context(nc.sbuf_tensor(name, shape, dt))

        def sem(name):
            return ctx.enter_context(nc.semaphore(name))

        raw = sb("e_raw", [P, RING * EW])
        w_hi, w_lo = sb("e_hi", [P, RING * EW], F32R), sb("e_lo", [P, RING * EW], F32R)
        ident = sb("e_ident", [P, P])
        table = sb("e_table", [P, TILES, 2])
        two = range(2)
        gix = [sb(f"gix{i}", [P, 1], I32) for i in two]
        six = [sb(f"six{i}", [P, 1], I32) for i in two]
        wt = [sb(f"wt{i}", [P, 1]) for i in two]
        xg = [sb(f"xg{i}", [P, D]) for i in two]
        xT_hi = [sb(f"xgT_hi{i}", [P, KD, P], F32R) for i in two]
        xT_lo = [sb(f"xgT_lo{i}", [P, KD, P], F32R) for i in two]
        silu = [sb(f"e_silu{i}", [P, FE]) for i in two]
        h = [sb(f"e_h{i}", [P, KE * P]) for i in two]
        hT_hi = [sb(f"e_hT_hi{i}", [P, KE, P], F32R) for i in two]
        hT_lo = [sb(f"e_hT_lo{i}", [P, KE, P], F32R) for i in two]
        y = [sb(f"e_y{i}", [P, D]) for i in two]
        ps = [ctx.enter_context(nc.psum_tensor(f"pu{i}", [P, 512], F32)) for i in range(8)]
        TX, TH, H1, H2, Y = ps[0], ps[1], ps[2:4], ps[4:6], ps[6:8]

        s_tab, s_id, s_pad = sem("table_loaded"), sem("e_ident_loaded"), sem("h_padding_zeroed")
        s_wraw = [sem(f"expert_part_loaded{i}") for i in range(3)]
        s_whi = [sem(f"expert_part_hi{i}") for i in range(3)]
        s_wlo = [sem(f"expert_part_lo{i}") for i in range(3)]
        s_issue = sem("e_dma_issued")
        s_gix, s_six, s_wt = sem("gather_index"), sem("scatter_index"), sem("weight_column")
        s_g = [sem(f"gathered{i}") for i in two]
        s_tx, s_xhi, s_xlo, s_f1, s_f2 = sem("xT_done"), sem("xT_hi"), sem("xT_lo"), sem("fc1_done"), sem("fc2_done")
        s_silu, s_h, s_th, s_hhi, s_hlo = sem("e_silu_done"), sem("e_h_done"), sem("hT_done"), sem("hT_hi"), sem("hT_lo")
        s_pj, s_yo, s_add = sem("e_proj_done"), sem("y_copied"), sem("y_added")

        def at(ii, p, per=1, c=0):
            return ii * (2 * per) + (per * p + c)

        def positive(eng, s, value):
            if isinstance(value, int) and value <= 0:
                return
            eng.wait_ge(s, value)

        def tiles(eng, body):
            for ii in (0, 1):
                body(ii, 0)
                body(ii, 1)
            with eng.Fori(2, TILES // 2 - 2) as ii:
                body(ii, 0)
                body(ii, 1)
            for ii in (TILES // 2 - 2, TILES // 2 - 1):
                body(ii, 0)
                body(ii, 1)

        def after(ii, p, n):
            ii, p = ii + (p + n) // 2, (p + n) % 2
            return None if isinstance(ii, int) and ii >= TILES // 2 else (ii, p)

        def refill(eng, ii, p, split):
            if after(ii, p, 1) is None:
                return
            e = eng.value_load(keep["fresh"][0:1, bass.ds(at(ii, p), 1)], min_val=0, max_val=E)
            with eng.If(e < E):
                split(e, e % RING)

        with nc.Block() as block:
            @block.sync
            def _(sp):
                sp.dma_start(table[:].rearrange("p t w -> p (t w)"), a["table"].rearrange("(p t) w -> p (t w)", p=P))\
                  .then_inc(s_tab, 16)
                sp.dma_start(ident[:], a["ident"]).then_inc(s_id, 16)
                for e in range(E):
                    for i, (c0, c1) in enumerate(PARTS):
                        if e:
                            sp.wait_ge(s_wraw[i], 16 * e)
                        if e >= RING:
                            sp.wait_ge(s_wlo[i], e - RING + 1)
                        o = e % RING * EW
                        sp.dma_start(raw[:, o + c0:o + c1], a["expert_w"][e][:, c0:c1]).then_inc(s_wraw[i], 16)

            @block.gpsimd
            def _(pool):
                pool.wait_ge(s_tab, 16)
                toks = table[:].rearrange("p t w -> p (t w)")

                def gather(ii, p):
                    positive(pool, s_tx, at(ii, p, 1, -1))
                    positive(pool, s_g[p], ii * 16)
                    nc.gpsimd.tensor_copy(gix[p][:], toks[:, bass.ds(at(ii, p, 2), 1)]).then_inc(s_gix, 1)
                    pool.wait_ge(s_gix, at(ii, p, 1, 1))
                    pool.sem_inc(s_issue, 1)
                    nc.gpsimd.indirect_dma_start(out=xg[p][:], out_offset=None, in_=a["xf"],
                                                 in_offset=bass.IndirectOffsetOnAxis(ap=gix[p][:], axis=0))\
                      .then_inc(s_g[p], 16)

                def body(ii, p):
                    if (nxt := after(ii, p, 3)) is not None:
                        gather(*nxt)
                    positive(pool, s_add, at(ii, p, 16))
                    nc.gpsimd.tensor_copy(six[p][:], toks[:, bass.ds(at(ii, p, 2), 1)]).then_inc(s_six, 1)
                    pool.wait_ge(s_six, at(ii, p, 1, 1))
                    pool.wait_ge(s_yo, at(ii, p, 1, 1))
                    pool.sem_inc(s_issue, 1)
                    nc.gpsimd.indirect_dma_start(out=a["out"], out_offset=bass.IndirectOffsetOnAxis(ap=six[p][:], axis=0),
                                                 in_=y[p][:], in_offset=None, compute_op=ALU.add).then_inc(s_add, 16)

                gather(0, 0)
                gather(0, 1)
                gather(1, 0)
                tiles(pool, body)
                pool.wait_ge(s_add, 16 * TILES)

            @block.scalar
            def _(act):
                def split_w(e, place, parts=(0, 1, 2)):
                    for i in parts:
                        act.wait_ge(s_wraw[i], e * 16 + 16)
                        act.sem_inc(s_issue, 1) if not isinstance(e, int) else None
                        w = bass.ds(place * EW + PARTS[i][0], PARTS[i][1] - PARTS[i][0])
                        act.activation(w_hi[:, w], raw[:, w], ACT.Copy).then_inc(s_whi[i], 1)

                def split_x(ii, p):
                    act.wait_ge(s_tx, at(ii, p, 1, 1))
                    positive(act, s_f2, at(ii, p, 1, -1))
                    act.activation(xT_hi[p][:].rearrange("p c t -> p (c t)"), TX[:], ACT.Copy).then_inc(s_xhi, 1)

                def gate(ii, p):
                    act.wait_ge(s_f1, at(ii, p, 1, 1))
                    positive(act, s_h, at(ii, p, 1, -1))
                    act.activation(silu[p][:], H1[p][:, 0:FE], ACT.Silu).then_inc(s_silu, 1)

                def body(ii, p):
                    if (nxt := after(ii, p, 1)) is not None:
                        gate(*nxt)
                    act.wait_ge(s_th, at(ii, p, 1, 1))
                    positive(act, s_pj, at(ii, p, 1, -1))
                    act.activation(hT_hi[p][:].rearrange("p c t -> p (c t)"), TH[:, 0:KE * P], ACT.Copy).then_inc(s_hhi, 1)
                    if (nxt := after(ii, p, 2)) is not None:
                        split_x(*nxt)
                    refill(act, ii, p, split_w)
                    act.wait_ge(s_pj, at(ii, p, 1, 1))
                    positive(act, s_add, at(ii, p, 16, -16))
                    act.activation(y[p][:], Y[p][:], ACT.Copy).then_inc(s_yo, 1)

                split_w(0, 0, (0,))
                split_x(0, 0)
                split_w(0, 0, (1,))
                gate(0, 0)
                split_x(0, 1)
                split_w(0, 0, (2,))
                split_w(1, 1)
                tiles(act, body)

            @block.tensor
            def _(pe):
                def three(out, lh, ll, w, first, last):
                    pe.matmul(out, lh, w_hi[:, w], start=first, stop=False)
                    pe.matmul(out, lh, w_lo[:, w], start=False, stop=False)
                    return pe.matmul(out, ll, w_hi[:, w], start=False, stop=last)

                def turn_x(ii, p):
                    pe.wait_ge(s_g[p], ii * 16 + 16)
                    positive(pe, s_xlo, at(ii, p))
                    for c in range(KD):
                        mm = pe.transpose(TX[:, c * P:(c + 1) * P], xg[p][:, c * P:(c + 1) * P], ident[:])
                    mm.then_inc(s_tx, 1)

                def expert(ii, p):
                    e = pe.value_load(keep["expert"][0:1, bass.ds(at(ii, p), 1)], min_val=0, max_val=E - 1)
                    return e, e % RING

                def fc(ii, p, e, place, f, bank, done):
                    pe.wait_ge(s_wlo[f], e + 1)
                    for c in range(KD):
                        mm = three(bank[:, 0:FE], xT_hi[p][:, c, :], xT_lo[p][:, c, :],
                                   bass.ds(place * EW + (f * KD + c) * FE, FE), c == 0, c == KD - 1)
                    mm.then_inc(done, 1)

                def turn_h(ii, p):
                    pe.wait_ge(s_h, at(ii, p, 1, 1))
                    positive(pe, s_hlo, at(ii, p))
                    for c in range(KE):
                        mm = pe.transpose(TH[:, c * P:(c + 1) * P], h[p][:, c * P:(c + 1) * P], ident[:])
                    mm.then_inc(s_th, 1)

                def proj(ii, p, e, place):
                    pe.wait_ge(s_wlo[2], e + 1)
                    pe.wait_ge(s_hlo, at(ii, p, 1, 1))
                    positive(pe, s_yo, at(ii, p, 1, -1))
                    for c in range(KE):
                        mm = three(Y[p][:], hT_hi[p][:, c, :], hT_lo[p][:, c, :],
                                   bass.ds(place * EW + PARTS[2][0] + c * D, D), c == 0, c == KE - 1)
                    mm.then_inc(s_pj, 1)

                def body(ii, p):
                    nxt = after(ii, p, 1)
                    if nxt is not None:
                        e1, place1 = expert(*nxt)
                        pe.wait_ge(s_xlo, at(*nxt, 1, 1))
                        positive(pe, s_h, at(*nxt, 1, -1))
                        fc(*nxt, e1, place1, 0, H1[nxt[1]], s_f1)
                    turn_h(ii, p)
                    if (later := after(ii, p, 2)) is not None:
                        turn_x(*later)
                    if nxt is not None:
                        fc(*nxt, e1, place1, 1, H2[nxt[1]], s_f2)
                    proj(ii, p, *expert(ii, p))

                pe.wait_ge(s_id, 16)
                turn_x(0, 0)
                pe.wait_ge(s_xlo, 1)
                fc(0, 0, 0, 0, 0, H1[0], s_f1)
                fc(0, 0, 0, 0, 1, H2[0], s_f2)
                turn_x(0, 1)
                tiles(pe, body)

            @block.vector
            def _(dve):
                v = nc.vector
                flat = table[:].rearrange("p t w -> p (t w)")

                def split_w(e, place, parts=(0, 1, 2)):
                    for i in parts:
                        dve.wait_ge(s_whi[i], e + 1)
                        dve.sem_inc(s_issue, 1) if not isinstance(e, int) else None
                        w = bass.ds(place * EW + PARTS[i][0], PARTS[i][1] - PARTS[i][0])
                        v.tensor_tensor(w_lo[:, w], raw[:, w], w_hi[:, w].bitcast(F32), ALU.subtract).then_inc(s_wlo[i], 1)

                def split_x(ii, p):
                    dve.wait_ge(s_xhi, at(ii, p, 1, 1))
                    v.tensor_tensor(xT_lo[p][:].rearrange("p c t -> p (c t)"), TX[:],
                                    xT_hi[p][:].rearrange("p c t -> p (c t)").bitcast(F32), ALU.subtract).then_inc(s_xlo, 1)

                def weigh(ii, p):
                    v.tensor_copy(wt[p][:], flat[:, bass.ds(at(ii, p, 2, 1), 1)]).then_inc(s_wt, 1)
                    dve.wait_ge(s_wt, at(ii, p, 1, 1))
                    dve.wait_ge(s_silu, at(ii, p, 1, 1))
                    dve.wait_ge(s_f2, at(ii, p, 1, 1))
                    positive(dve, s_th, at(ii, p, 1, -1))
                    v.scalar_tensor_tensor(h[p][:, 0:FE], silu[p][:], wt[p][:, 0:1], H2[p][:, 0:FE], ALU.mult, ALU.mult)\
                     .then_inc(s_h, 1)

                def body(ii, p):
                    dve.wait_ge(s_hhi, at(ii, p, 1, 1))
                    v.tensor_tensor(hT_lo[p][:].rearrange("p c t -> p (c t)"), TH[:, 0:KE * P],
                                    hT_hi[p][:].rearrange("p c t -> p (c t)").bitcast(F32), ALU.subtract).then_inc(s_hlo, 1)
                    if (nxt := after(ii, p, 2)) is not None:
                        split_x(*nxt)
                    if (nxt := after(ii, p, 1)) is not None:
                        weigh(*nxt)
                    refill(dve, ii, p, split_w)

                for i in two:
                    v.memset(h[i][:, FE:], 0.0).then_inc(s_pad, 1)
                dve.wait_ge(s_pad, 2)
                split_w(0, 0, (0,))
                split_x(0, 0)
                split_w(0, 0, (1,))
                dve.wait_ge(s_tab, 16)
                split_x(0, 1)
                weigh(0, 0)
                split_w(0, 0, (2,))
                split_w(1, 1)
                tiles(dve, body)


def build(nc, a):
    a["xf"] = nc.dram_tensor("xf_rows", [N + P, D], F32).ap()
    a["xfT"] = nc.dram_tensor("xf_T", [NT, P, D], F32).ap()
    a["x1"] = nc.dram_tensor("x1_rows", [N, D], F32).ap()
    a["table"] = nc.dram_tensor("slot_table", [P * TILES, 2], F32).ap()
    with ExitStack() as ctx:
        keep = {"logits": ctx.enter_context(nc.sbuf_tensor("logits", [P, NT, E + 1], F32))}
        stage_attention(nc, a, keep)
        for name in ("expert", "fresh"):
            keep[name] = ctx.enter_context(nc.sbuf_tensor(f"tile_{name}", [1, TILES], I32))
        stage_shared(nc, a, keep)
        stage_experts(nc, a, keep)


def layouts(np, inputs):
    x = np.asarray(inputs["x"]).reshape(N, D)
    turned = lambda name: np.ascontiguousarray(np.swapaxes(np.asarray(inputs[name]), -1, -2))
    r = {
        "x": x, "x_T": np.ascontiguousarray(x.T),
        "lora_idx": np.asarray(inputs["itok_B_0_6"]).reshape(1, B),
        "cond": np.asarray(inputs["itok_B_1_198"]).reshape(1, B),
        "W_T": turned("L0_cond_W"),
        "A_T": np.ascontiguousarray(np.asarray(inputs["L0_cond_A"]).reshape(ADAPTERS * RANK, D).T),
        "B_T": turned("L0_cond_Bm").reshape(ADAPTERS * RANK, D),
        "scal": np.repeat(np.asarray(inputs["L0_cond_scalings"]), RANK).reshape(P, 1),
        "Wq_T": turned("L0_attn_Wq"), "Wk_T": turned("L0_attn_Wk"), "Wv_T": turned("L0_attn_Wv"),
        "Wo_T": turned("L0_attn_Wo"),
        "mix_w": np.asarray(inputs["L0_cond2_weights"]),
        "gate_T": np.ascontiguousarray(np.concatenate([np.asarray(inputs["L0_ffn_gate_w"]),
                                                       np.asarray(inputs["L0_ffn_shared_gate_w"])]).T),
    }
    fc = [turned(f"L0_ffn_shared_fc{i}").reshape(KD, P, KS, P).transpose(2, 1, 0, 3).reshape(KS, P, KD * P) for i in (1, 2)]
    r["shared_w"] = np.ascontiguousarray(np.concatenate(fc + [turned("L0_ffn_shared_proj").reshape(KS, P, D)], axis=2))
    fc = [turned(f"L0_ffn_expert_fc{i}").reshape(E, KD, P, FE).transpose(0, 2, 1, 3).reshape(E, P, KD * FE) for i in (1, 2)]
    proj = np.zeros((E, KE * P, D), np.float32)
    proj[:, :FE] = turned("L0_ffn_expert_proj")
    r["expert_w"] = np.ascontiguousarray(np.concatenate(
        fc + [proj.reshape(E, KE, P, D).transpose(0, 2, 1, 3).reshape(E, P, KE * D)], axis=2))
    f = np.float32
    p = np.arange(P)
    theta = f(10000.0) ** (f(-2.0) * np.arange(DH // 2, dtype=f) / f(DH))
    angles = np.arange(T, dtype=f)[:, None] * theta.astype(f)[None, :]
    lane = (p % DH) // 2
    sign = np.where(p % 2 == 0, -1, 1).astype(f)
    r["cos"] = np.ascontiguousarray(np.cos(angles).astype(f)[:, lane].T)
    r["sin"] = np.ascontiguousarray(np.sin(angles).astype(f)[:, lane].T * sign[:, None])
    r["causal"] = np.where(np.arange(T)[None, :] <= p[:, None] % T, 0, MASKED).astype(f)
    r["ident"] = np.eye(P, dtype=f)
    r["owner"] = (p // RANK).astype(f).reshape(P, 1)
    r["ones"] = np.ones((P, P), f)
    r["before"] = (p[:, None] < p[None, :]).astype(f)
    e = np.arange(E)
    r["lower"] = np.broadcast_to((e[None, :] < e[:, None]).astype(f).reshape(1, E * E), (P, E * E)).copy()
    r["starts"] = np.broadcast_to((np.arange(NT) * P).astype(f), (P, NT)).copy()
    r["tno"] = np.broadcast_to(np.arange(TILES).astype(f), (P, TILES)).copy()
    r["tok"] = np.ascontiguousarray((np.arange(NT)[None, :] * P + p[:, None]).astype(np.int32))
    init = np.zeros((P, TILES, 2), f)
    init[:, :, 0] = (N + p)[:, None]
    r["table_init"] = init.reshape(P * TILES, 2)
    return r


def kernel(**inputs):
    import numpy as np
    import concourse.bacc as bacc
    from concourse.bass_utils import run_bass_kernel_spmd

    nc = bacc.Bacc("TRN2", target_bir_lowering=False, num_devices=1)
    arrays = layouts(np, inputs)
    a = {n: nc.dram_tensor(f"in_{n}", v.shape, mybir.dt.from_np(v.dtype), kind="ExternalInput").ap() for n, v in arrays.items()}
    a["out"] = nc.dram_tensor("out", [N + P, D], F32, kind="ExternalOutput").ap()
    build(nc, a)
    got = run_bass_kernel_spmd(nc, [{f"in_{n}": v for n, v in arrays.items()}], core_ids=[0])
    return got.results[0]["out"][:N].reshape(B, T, D)
```

```python
from contextlib import ExitStack

import concourse.bass as bass
from concourse import mybir

P = 128
F32 = mybir.dt.float32
F32R = mybir.dt.float32r
I32 = mybir.dt.int32
ALU = mybir.AluOpType
ACT = mybir.ActivationFunctionType
AX_X = mybir.AxisListType.X

B, T, D = 64, 64, 512
N = B * T
KD = D // P
H, DH = 16, 32
ADAPTERS, RANK = 8, 16
E, TOPK, FE = 8, 2, 352
FS = 1408
KS = FS // P
PIECE = 2 * KD * P + D
BLK = 512
NBLK = N // BLK
UNITS = BLK // P
NT = N // P
BB = BLK // T
SCALE = float(DH) ** -0.5
MASKED = -3.0e38
TILES = (TOPK * N + E * (P - 1)) // P
PAIRS = (TILES + 1) // 2
KE = -(-FE // P)
PARTS = [(0, KD * FE), (KD * FE, 2 * KD * FE), (2 * KD * FE, 2 * KD * FE + KE * D)]
EW = PARTS[2][1]
RING = 3
ROTS = 3
SWAP = [i ^ 1 for i in range(32)]

XA, HG, KG, QG, VG = 0, 1, 5, 9, 13
GROUPS = 17
LATER = ["Wk", "Wq", "Wv", "Wo"]


def schedule(dense, attn, ahead, carried, final):
    groups = list(range(GROUPS)) if dense else []
    steps = []

    def d(n=1):
        for _ in range(n):
            if groups:
                steps.append(("dense", groups.pop(0)))

    def x(*pieces):
        if ahead:
            steps.extend(pieces)

    if not attn:
        d()
        for i in range(len(LATER)):
            steps.append(("weights", i))
            d(2)
        d(VG - 1 - 2 * len(LATER))
        x(("xload", 0), ("xload", 1))
        for c in range(KD):
            d()
            x(("xsplit", c))
            if c < KD - 2:
                x(("xload", c + 2))
        return steps

    def of(kind, u):
        if u >= 0 or carried:
            steps.append((kind, u))

    if final:
        def begin(u, half, *kinds):
            if u < UNITS:
                steps.extend((kind, (u, half)) for kind in kinds)

        steps.extend([("preload", 0), ("load", 0), ("scores", 0)])
        begin(0, 0, "soft", "exp")
        begin(0, 1, "soft", "exp")
        for u in range(UNITS):
            if u:
                steps.append(("load", u))
            steps.extend([("norm", (u, 0)), ("norm", (u, 1)), ("wo", u - 1)])
            if u < UNITS - 1:
                steps.append(("scores", u + 1))
            steps.extend([("PT", (u, 0)), ("PT", (u, 1)), ("mix", u - 1)])
            begin(u + 1, 0, "soft", "exp")
            begin(u + 1, 1, "soft")
            steps.extend([("mixT", u - 1), ("PV", u), ("router", u - 1), ("oT", u)])
            begin(u + 1, 1, "exp")
        steps.extend((kind, UNITS - 1) for kind in ("wo", "mix", "mixT", "router"))
        return steps

    for u in range(UNITS):
        steps.append(("load", u))
        steps.append(("scores", u))
        steps.append(("soft", (u, 0)))
        steps.append(("exp", (u, 0)))
        steps.append(("soft", (u, 1)))
        d()
        steps.append(("exp", (u, 1)))
        steps.append(("norm", (u, 0)))
        of("wo", u - 1)
        steps.append(("norm", (u, 1)))
        if u > 1:
            x(("xsplit", 2 * u - 4))
        d()
        of("mix", u - 1)
        steps.append(("PT", (u, 0)))
        steps.append(("PT", (u, 1)))
        if u == 1:
            d()
            x(("xload", 0), ("xload", 1))
        if u == 2:
            x(("xload", 2))
        d()
        if u > 1:
            x(("xsplit", 2 * u - 3))
        if u == 2:
            x(("xload", 3))
        of("mixT", u - 1)
        steps.append(("PV", u))
        of("router", u - 1)
        steps.append(("oT", u))
        d()
    return steps


def stage_attention(nc, a, keep):
    with ExitStack() as ctx:
        def sb(name, shape, dt=F32):
            return ctx.enter_context(nc.sbuf_tensor(name, shape, dt))

        def sem(name):
            return ctx.enter_context(nc.semaphore(name))

        names = ["W", "Wk", "Wq", "Wv", "Wo"]
        w_hi = {n: sb(f"{n}_hi", [P, KD, D], F32R) for n in names}
        w_lo = {n: sb(f"{n}_lo", [P, KD, D], F32R) for n in names}
        A_hi, A_lo = sb("A_hi", [P, KD, P], F32R), sb("A_lo", [P, KD, P], F32R)
        B_hi, B_lo = sb("B_hi", [P, D], F32R), sb("B_lo", [P, D], F32R)
        gate = sb("gate", [P, KD, E + 1])
        raw = keep["rows"][0:2]
        x_hi, x_lo = sb("x_hi", [P, KD, BLK], F32R), sb("x_lo", [P, KD, BLK], F32R)
        h_hi, h_lo = sb("h_hi", [P, KD, BLK], F32R), sb("h_lo", [P, KD, BLK], F32R)
        KT = [keep["big"][:, 0:KD * BLK].rearrange("p (k n) -> p k n", k=KD), sb("KT1", [P, KD, BLK])[:]]
        QT = [keep["big"][:, KD * BLK:2 * KD * BLK].rearrange("p (k n) -> p k n", k=KD), sb("QT1", [P, KD, BLK])[:]]
        V = sb("V", [P, UNITS, 2, H // 2, 2 * DH])
        rot = [keep["rows"][2], keep["rows"][3], sb("rot2", [P, BLK])]
        probs = sb("probs", [P, 2, KD, 2, T])
        PT = [sb(f"PT{i}", [P, KD, P]) for i in range(2)]
        o_hi, o_lo = sb("o_hi", [P, KD, P], F32R), sb("o_lo", [P, KD, P], F32R)
        x1 = [sb(f"x1_{i}", [P, D]) for i in range(2)]
        xf = sb("xf", [P, D])
        xfT = sb("xfT", [P, KD, P])
        mixw = [sb(f"mixw{i}", [P, P]) for i in range(2)]
        cos, sin = sb("cos", [P, T]), sb("sin", [P, T])
        causal = sb("causal", [P, T])
        ident = keep["ident"]
        cond = sb("cond", [1, B], I32)
        lidx = sb("lidx", [P, B], I32)
        lidf = sb("lidf", [P, B])
        lmask = sb("lmask", [P, B])
        owner, scal = sb("owner", [P, 1]), sb("scal", [P, 1])
        rmax, sums, rinv = sb("rmax", [P, 2, H // 2]), sb("sums", [P, 2, H // 2]), sb("rinv", [P, 2, H // 2])
        xa_f = rot[0]
        xa_hi, xa_lo = sb("xa_hi", [P, BLK], F32R), sb("xa_lo", [P, BLK], F32R)

        SB = ctx.enter_context(nc.psum_tensor("score_banks", [P, 4, 512], F32))
        ps = [ctx.enter_context(nc.psum_tensor(f"ps{i}", [P, 512], F32)) for i in range(4)]
        DB, OB, XB = ps[0:2], ps[2], ps[3]

        s_const = sem("const_loaded")
        s_lora = sem("lora_const_loaded")
        s_wraw = [sem(f"weight_raw{i}") for i in range(4)]
        s_whi, s_wlo = sem("weight_hi"), sem("weight_lo")
        s_lidf, s_lmask = sem("adapter_index"), sem("adapter_mask")
        s_zero, s_dump, s_vzero = sem("zero_set"), sem("dump_rows_zeroed"), sem("v_zeroed")
        s_x0 = [sem(f"first_x_raw{i}") for i in range(KD)]
        s_raw = [sem(f"x_raw{i}") for i in range(2)]
        s_xhi, s_xlo = sem("x_hi_done"), sem("x_lo_done")
        s_dense = sem("projection_done")
        s_free = [sem(f"projection_bank_free{i}") for i in range(2)]
        s_xahi, s_xalo, s_hhi = sem("xa_hi_done"), sem("xa_lo_done"), sem("h_hi_done")
        s_cosd, s_swp = sem("cos_part"), sem("swapped")
        s_sind, s_rope = sem("sin_part"), sem("rope_done")
        s_sc, s_sm, s_max, s_off = sem("scores_done"), sem("masked_done"), sem("max_done"), sem("max_subtracted")
        s_exp, s_sum, s_rinv, s_pn = sem("exp_done"), sem("sums_done"), sem("rinv_done"), sem("probs_done")
        s_pt, s_pte, s_pv = sem("probsT_done"), sem("probsT_copied"), sem("pv_done")
        s_ohi, s_olo = sem("o_hi_done"), sem("o_lo_done")
        s_wo, s_x1 = sem("wo_done"), sem("x1_done")
        s_xt = [sem(f"x_tokens_loaded{i}") for i in range(2)]
        s_mw = [sem(f"mix_weights_loaded{i}") for i in range(2)]
        s_x1st = [sem(f"x1_stored{i}") for i in range(2)]
        s_mix, s_xfe, s_mixT, s_xfTe = sem("mix_done"), sem("xf_copied"), sem("mixT_done"), sem("xfT_copied")
        s_turn, s_shuffle = sem("buffer_turn"), sem("shuffle_turn")
        s_rt, s_rte = sem("router_done"), sem("logits_copied")
        s_xfst, s_xfTst = sem("xf_stored"), sem("xfT_stored")

        WLOADS = [("A", a["A_T"].rearrange("(k p) m -> p k m", p=P), A_hi, A_lo),
                  ("W", a["W_T"].rearrange("(k p) m -> p k m", p=P), w_hi["W"], w_lo["W"]),
                  ("B", a["B_T"], B_hi, B_lo)]
        WLOADS += [(n, a[f"{n}_T"].rearrange("(k p) m -> p k m", p=P), w_hi[n], w_lo[n]) for n in LATER]
        FIRST = len(WLOADS) - len(LATER)
        WREADY = {n: i + 1 for i, (n, *_) in enumerate(WLOADS)}
        v_flat = V[:].rearrange("p u b h d -> p (u b h d)")
        stage_bufs = [KT[1].rearrange("p a b -> p (a b)"), QT[1].rearrange("p a b -> p (a b)"),
                      v_flat[:, 0:KD * D], v_flat[:, KD * D:2 * KD * D]]
        STAGE_OF = [0, 1, 2, 3, 0, 1, 0]
        BEFORE = [STAGE_OF[:i].count(k) for i, k in enumerate(STAGE_OF)]

        def staged(i, dst):
            return stage_bufs[STAGE_OF[i]][:, 0:dst[:].free_size()]

        def flat(t):
            return t[:] if len(t.shape) == 2 else t[:].rearrange("p a b -> p (a b)")

        def is_final(jj, q):
            return isinstance(jj, int) and 2 * jj + q == NBLK - 1

        def pt_bank(jj, q, half):
            return DB[half][:] if is_final(jj, q) else SB[:, 2 * half, :]

        def heads_of(t, half):
            return t[:, half, :, :, :].rearrange("p c e k -> p (c e) k")

        def blk(ii, p, per, c=0):
            return ii * (2 * per) + (per * p + c)

        def unit(jj, q, u, per=1, c=0):
            return jj * (2 * UNITS * per) + (per * (UNITS * q + u) + c)

        def bank_of(p, k):
            return (GROUPS * p + k) % 2

        def bank_uses(ii, p, k):
            return ii * GROUPS + (GROUPS * p + k) // 2

        def positive(eng, s, value):
            if isinstance(value, int) and value <= 0:
                return
            eng.wait_ge(s, value)

        CONSTS = 6

        def unit_half(jj, q, u, per):
            return jj * (UNITS * per) + per * ((UNITS * q + u) // 2)

        def run(eng, handlers):
            def step(dense, attn, ahead=None):
                first = attn is not None and isinstance(attn[0], int) and attn == (0, 0)
                for kind, arg in schedule(dense is not None, attn is not None, ahead is not None,
                                          carried=not first, final=dense is None):
                    f = handlers.get(kind)
                    if f is not None:
                        block = dense if kind in ("dense", "weights") else ahead if kind in ("xload", "xsplit") else attn
                        f(*block, arg)

            last = NBLK // 2 - 1
            step((0, 0), None, (0, 1))
            step((0, 1), (0, 0), (1, 0))
            with eng.Fori(1, last) as ii:
                step((ii, 0), (ii - 1, 1), (ii, 1))
                step((ii, 1), (ii, 0), (ii + 1, 0))
            step((last, 0), (last - 1, 1), (last, 1))
            step((last, 1), (last, 0))
            step(None, (last, 1))

        with nc.Block() as block:
            @block.sync
            def _(sp):
                def xload(ii, p, c):
                    sp.wait_ge(s_xlo, blk(ii, p, KD, c - 1))
                    sp.dma_start(raw[c % 2][:], a["x_T"][c * P:(c + 1) * P, bass.ds(blk(ii, p, BLK), BLK)])\
                      .then_inc(s_raw[c % 2], 16)

                for i, (n, src, hi, _) in enumerate(WLOADS):
                    if BEFORE[i]:
                        last = max(k for k in range(i) if STAGE_OF[k] == STAGE_OF[i])
                        sp.wait_ge(s_wlo, last + 1)
                    dst = staged(i, hi)
                    if len(src.shape) == 3:
                        dst = dst.rearrange("p (k m) -> p k m", k=KD)
                    sp.dma_start(dst, src).then_inc(s_wraw[STAGE_OF[i]], 16)
                    if n == "A":
                        for c in range(KD):
                            sp.dma_start(KT[0][:, c, :], a["x_T"][c * P:(c + 1) * P, 0:BLK]).then_inc(s_x0[c], 16)
                        for dst, src in ((owner, a["owner"]), (scal, a["scal"]), (lidx, a["lora_idx"].broadcast_to([P, B]))):
                            sp.dma_start(dst[:], src).then_inc(s_lora, 16)
                    if n == "Wk":
                        for dst, src in ((cos, a["cos"]), (sin, a["sin"]), (causal, a["causal"]), (ident, a["ident"]),
                                         (cond, a["cond"]), (gate, a["gate_T"].rearrange("(k p) m -> p k m", p=P))):
                            sp.dma_start(dst[:], src).then_inc(s_const, 16)
                sp.wait_ge(s_zero, 3)
                for rows in (a["xf"], a["out"]):
                    sp.dma_start(rows[N:N + P, :], xfT[:].rearrange("p k n -> p (k n)")).then_inc(s_dump, 16)
                sp.wait_ge(s_dump, 32)
                sp.wait_ge(s_const, CONSTS * 16)

                def load(jj, q, u):
                    j = u % 2
                    if not (isinstance(jj, int) and jj == 0 and q == 0 and u < 2):
                        sp.wait_ge(s_mix, unit(jj, q, u, 1, -1))
                        sp.sem_inc(s_turn, 1)
                        sp.wait_ge(s_x1st[j], unit_half(jj, q, u, 16))
                    g = unit(jj, q, u)
                    sp.dma_start(x1[j][:], a["x"][bass.ds(g * P, P), :]).then_inc(s_xt[j], 16)
                    for m in range(2):
                        c = sp.value_load(cond[0:1, bass.ds(g * 2 + m, 1)], min_val=0, max_val=a["mix_w"].shape[0] - 1)
                        sp.dma_start(mixw[j][m * T:(m + 1) * T, m * T:(m + 1) * T],
                                     a["mix_w"][bass.ds(c, 1), :, :].rearrange("o c d -> (o c) d")).then_inc(s_mw[j], 16)

                def wo(jj, q, u):
                    g = unit(jj, q, u)
                    sp.wait_ge(s_x1, unit(jj, q, u, 1, 1))
                    sp.dma_start(a["x1"][bass.ds(g * P, P), :], x1[u % 2][:]).then_inc(s_x1st[u % 2], 16)

                def mix(jj, q, u):
                    g = unit(jj, q, u)
                    sp.wait_ge(s_xfe, unit(jj, q, u, 1, 1))
                    sp.dma_start(a["xf"][bass.ds(g * P, P), :], xf[:]).then_inc(s_xfst, 16)

                def mixT(jj, q, u):
                    g = unit(jj, q, u)
                    sp.wait_ge(s_xfTe, unit(jj, q, u, 1, 1))
                    sp.dma_start(a["xfT"][bass.ds(g, 1), :, :].rearrange("g p n -> (g p) n"),
                                 xfT[:].rearrange("p k n -> p (k n)")).then_inc(s_xfTst, 16)

                def preload(jj, q, _):
                    sp.wait_ge(s_sc, NT - UNITS)
                    sp.wait_ge(s_rope, 8 * NBLK)
                    sp.wait_ge(s_xlo, KD * NBLK)
                    sp.wait_ge(s_xfTst, 16 * UNITS)
                    for u in range(UNITS):
                        sp.dma_start(keep["rows"][u][:], a["xfT"][u]).then_inc(keep["s_xraw"][u], 16)
                    for m in range(2):
                        sp.dma_start(keep["big"][:, m * PIECE:(m + 1) * PIECE], a["shared_w"][m]).then_inc(keep["s_praw"][m], 16)

                run(sp, {"preload": preload, "xload": xload, "load": load, "wo": wo, "mix": mix, "mixT": mixT})
                for s in s_x1st:
                    sp.wait_ge(s, 16 * (NT // 2))
                sp.wait_ge(s_xfst, 16 * NT)
                sp.wait_ge(s_xfTst, 16 * NT)

            @block.scalar
            def _(act):
                def xsplit(ii, p, c):
                    act.wait_ge(s_raw[c % 2], blk(ii, p, 32, 16 * (c // 2 + 1) - 32))
                    if c == 0:
                        positive(act, s_dense, blk(ii, p, GROUPS, HG + KD - GROUPS))
                    act.activation(x_hi[:, c, :], raw[c % 2][:], ACT.Copy).then_inc(s_xhi, 1)

                def split_w(i):
                    _, _, hi, _ = WLOADS[i]
                    act.wait_ge(s_wraw[STAGE_OF[i]], 16 * (BEFORE[i] + 1))
                    act.activation(flat(hi), staged(i, hi), ACT.Copy).then_inc(s_whi, 1)

                for i in range(FIRST):
                    split_w(i)
                    if i == 0:
                        for c in range(KD):
                            act.wait_ge(s_x0[c], 16)
                            act.activation(x_hi[:, c, :], KT[0][:, c, :], ACT.Copy).then_inc(s_xhi, 1)

                def weights(ii, p, n):
                    split_w(FIRST + n)

                def dense(ii, p, k):
                    bank = DB[bank_of(p, k)]
                    if k == XA:
                        act.wait_ge(s_free[bank_of(p, k)], bank_uses(ii, p, k) + 1)
                        act.activation(xa_hi[:], xa_f[:], ACT.Copy).then_inc(s_xahi, 1)
                        return
                    act.wait_ge(s_dense, blk(ii, p, GROUPS, k + 1))
                    if k < KG:
                        act.activation(h_hi[:, k - HG, :], bank[:], ACT.Copy).then_inc(s_hhi, 1)
                    elif k < VG:
                        n = k - KG
                        positive(act, s_rope, blk(ii, p, 8, max(0, n + 1 - ROTS)))
                        act.activation(rot[n % ROTS][:], bank[:], ACT.Copy).then_inc(s_free[bank_of(p, k)], 1)

                def exp(jj, q, uh):
                    u, half = uh
                    act.wait_ge(s_off, unit(jj, q, u, 2, half + 1))
                    act.activation(heads_of(probs, half), heads_of(probs, half), ACT.Exp).then_inc(s_exp, 1)

                def PTc(jj, q, uh):
                    u, half = uh
                    act.wait_ge(s_pt, unit(jj, q, u, 2, half + 1))
                    positive(act, s_pv, unit(jj, q, u))
                    act.activation(PT[half][:].rearrange("p c k -> p (c k)"), pt_bank(jj, q, half), ACT.Copy).then_inc(s_pte, 1)

                def oT(jj, q, u):
                    act.wait_ge(s_pv, unit(jj, q, u, 1, 1))
                    positive(act, s_wo, unit(jj, q, u))
                    act.activation(o_hi[:].rearrange("p c k -> p (c k)"), OB[:], ACT.Copy).then_inc(s_ohi, 1)

                def mix(jj, q, u):
                    act.wait_ge(s_mix, unit(jj, q, u, 1, 1))
                    positive(act, s_mixT, unit(jj, q, u))
                    positive(act, s_xfst, unit(jj, q, u, 16))
                    act.activation(xf[:], XB[:], ACT.Copy).then_inc(s_xfe, 1)

                def mixT(jj, q, u):
                    act.wait_ge(s_mixT, unit(jj, q, u, 1, 1))
                    positive(act, s_rt, unit(jj, q, u))
                    if isinstance(jj, int) and jj == 0 and q == 0 and u == 0:
                        act.wait_ge(s_dump, 32)
                    positive(act, s_xfTst, unit(jj, q, u, 16))
                    act.activation(xfT[:].rearrange("p c k -> p (c k)"), XB[:], ACT.Copy).then_inc(s_xfTe, 1)

                run(act, {"weights": weights, "xsplit": xsplit, "dense": dense, "exp": exp, "PT": PTc, "oT": oT,
                          "mix": mix, "mixT": mixT})

            @block.gpsimd
            def _(pool):
                nc.gpsimd.memset(xfT[:], 0.0).then_inc(s_zero, 1)
                for m in mixw:
                    nc.gpsimd.memset(m[:], 0.0).then_inc(s_zero, 1)
                pool.wait_ge(s_wlo, max(i for i, k in enumerate(STAGE_OF) if k >= 2) + 1)
                nc.gpsimd.memset(V[:], 0.0).then_inc(s_vzero, 1)

                def dense(ii, p, k):
                    if not KG <= k < VG:
                        return
                    n = k - KG
                    dst = (KT if k < QG else QT)[p][:, n % 4, :]
                    pool.wait_ge(s_swp, blk(ii, p, 8, n + 1))
                    if k == KG and isinstance(ii, int) and ii == 0 and p == 0:
                        pool.wait_ge(s_const, CONSTS * 16)
                    nc.gpsimd.tensor_tensor(dst.rearrange("p (b t) -> p b t", t=T), dst.rearrange("p (b t) -> p b t", t=T),
                                            sin[:].unsqueeze(1).broadcast_to([P, BB, T]), ALU.mult).then_inc(s_sind, 1)
                    pool.wait_ge(s_sind, blk(ii, p, 8, n + 1))
                    pool.wait_ge(s_cosd, blk(ii, p, 8, n + 1))
                    nc.gpsimd.tensor_tensor(dst, dst, rot[n % ROTS][:], ALU.add).then_inc(s_rope, 1)

                run(pool, {"dense": dense})

            @block.tensor
            def _(pe):
                def three(out, pairs, more=False, before=False):
                    n = len(pairs)
                    for i, ((lh, ll), (rh, rl)) in enumerate(pairs):
                        pe.matmul(out, lh, rh, start=(i == 0 and not before), stop=False)
                        pe.matmul(out, lh, rl, start=False, stop=False)
                        last = pe.matmul(out, ll, rh, start=False, stop=(i == n - 1 and not more))
                    return last

                def need(n, ii, p, upto=0):
                    if isinstance(ii, int) and ii == 0 and p == upto:
                        pe.wait_ge(s_wlo, WREADY[n])

                def dense(ii, p, k):
                    b = bank_of(p, k)
                    out = DB[b][:]
                    positive(pe, s_free[b], bank_uses(ii, p, k))
                    if k == XA:
                        need("A", ii, p)
                        pe.wait_ge(s_xlo, blk(ii, p, KD, KD))
                        last = three(out, [((A_hi[:, c, :], A_lo[:, c, :]), (x_hi[:, c, :], x_lo[:, c, :]))
                                           for c in range(KD)])
                    elif k < KG:
                        if k == HG:
                            need("W", ii, p)
                        m = slice((k - HG) * P, (k - HG + 1) * P)
                        three(out, [((w_hi["W"][:, c, m], w_lo["W"][:, c, m]), (x_hi[:, c, :], x_lo[:, c, :]))
                                    for c in range(KD)], more=True)
                        if k == HG:
                            need("B", ii, p)
                            pe.wait_ge(s_xalo, blk(ii, p, 1, 1))
                        last = three(out, [((B_hi[:, m], B_lo[:, m]), (xa_hi[:], xa_lo[:]))], before=True)
                    elif k < VG:
                        w = "Wk" if k < QG else "Wq"
                        if k == KG:
                            pe.wait_ge(s_free[bank_of(p, KG - 1)], bank_uses(ii, p, KG - 1) + 1)
                        if k in (KG, QG):
                            need(w, ii, p)
                        c0 = (k - KG) % 4
                        m = slice(c0 * P, (c0 + 1) * P)
                        last = three(out, [((w_hi[w][:, c, m], w_lo[w][:, c, m]), (h_hi[:, c, :], h_lo[:, c, :]))
                                           for c in range(KD)])
                    else:
                        if k == VG:
                            need("Wv", ii, p)
                        t = slice((k - VG) * P, (k - VG + 1) * P)
                        last = three(out, [((h_hi[:, c, t], h_lo[:, c, t]), (w_hi["Wv"][:, c, :], w_lo["Wv"][:, c, :]))
                                           for c in range(KD)])
                    last.then_inc(s_dense, 1)

                def scores(jj, q, u):
                    if u == 0:
                        pe.wait_ge(s_rope, blk(jj, q, 8, 8))
                    if is_final(jj, q) and u:
                        pe.wait_ge(s_sm, unit(jj, q, u, 2))
                    else:
                        positive(pe, s_pte, unit(jj, q, u, 2))
                    for c in range(KD):
                        for r in range(4):
                            for b in range(2):
                                rows = slice(DH * r, DH * r + DH)
                                t = slice(u * P + b * T, u * P + (b + 1) * T)
                                mm = pe.matmul(SB[b * T:(b + 1) * T, r, c * T:(c + 1) * T], QT[q][rows, c, t],
                                               KT[q][rows, c, t], start=True, stop=True)
                    mm.then_inc(s_sc, 1)

                def PTp(jj, q, uh):
                    u, half = uh
                    if isinstance(jj, int) and jj == 0 and q == 0 and u == 0 and half == 0:
                        pe.wait_ge(s_const, CONSTS * 16)
                    pe.wait_ge(s_pn, unit(jj, q, u, 2, half + 1))
                    if is_final(jj, q):
                        if u:
                            pe.wait_ge(s_pte, unit(jj, q, u, 2, half - 1))
                        else:
                            last_v(pe, jj, q)
                    for c in range(KD):
                        mm = pe.transpose(pt_bank(jj, q, half)[:, c * P:(c + 1) * P],
                                          probs[:, half, c, :, :].rearrange("p e k -> p (e k)"),
                                          ident[:])
                    mm.then_inc(s_pt, 1)

                def PV(jj, q, u):
                    if u == 0:
                        last_v(pe, jj, q)
                    positive(pe, s_olo, unit(jj, q, u))
                    pe.wait_ge(s_pte, unit(jj, q, u, 2, 2))
                    for c in range(KD):
                        for b in range(2):
                            for half in range(2):
                                o = c * P + b * T
                                mm = pe.matmul(OB[half * 2 * DH:(half + 1) * 2 * DH, o:o + T], V[:, u, b, 2 * c + half, :],
                                               PT[half][:, c, b * T:(b + 1) * T], start=True, stop=True)
                    mm.then_inc(s_pv, 1)

                def last_v(pe, jj, q):
                    for k in (GROUPS - 2, GROUPS - 1):
                        pe.wait_ge(s_free[bank_of(q, k)], bank_uses(jj, q, k) + 1)

                def wo(jj, q, u):
                    if isinstance(jj, int) and jj == 0 and q == 0 and u == 0:
                        pe.wait_ge(s_wlo, WREADY["Wo"])
                    pe.wait_ge(s_olo, unit(jj, q, u, 1, 1))
                    positive(pe, s_rte, unit(jj, q, u))
                    last = three(XB[:], [((o_hi[:, c, :], o_lo[:, c, :]), (w_hi["Wo"][:, c, :], w_lo["Wo"][:, c, :]))
                                         for c in range(KD)])
                    last.then_inc(s_wo, 1)

                def mix(jj, q, u):
                    pe.wait_ge(s_x1, unit(jj, q, u, 1, 1))
                    if isinstance(jj, int) and jj == 0 and q == 0 and u == 0:
                        pe.wait_ge(s_zero, 3)
                    pe.wait_ge(s_mw[u % 2], unit_half(jj, q, u, 32) + 32)
                    pe.matmul(XB[:], mixw[u % 2][:], x1[u % 2][:], start=True, stop=True).then_inc(s_mix, 1)

                def mixT(jj, q, u):
                    pe.wait_ge(s_xfe, unit(jj, q, u, 1, 1))
                    for c in range(KD):
                        mm = pe.transpose(XB[:, c * P:(c + 1) * P], xf[:, c * P:(c + 1) * P], ident[:])
                    mm.then_inc(s_mixT, 1)

                def router(jj, q, u):
                    pe.wait_ge(s_xfTe, unit(jj, q, u, 1, 1))
                    for c in range(KD):
                        mm = pe.matmul(XB[:, 0:E + 1], xfT[:, c, :], gate[:, c, :], start=(c == 0), stop=(c == KD - 1))
                    mm.then_inc(s_rt, 1)

                run(pe, {"dense": dense, "scores": scores, "PT": PTp, "PV": PV, "wo": wo, "mix": mix,
                         "mixT": mixT, "router": router})

            @block.vector
            def _(dve):
                v = nc.vector

                def xsplit(ii, p, c):
                    dve.wait_ge(s_xhi, blk(ii, p, KD, c + 1))
                    v.tensor_tensor(x_lo[:, c, :], raw[c % 2][:], x_hi[:, c, :].bitcast(F32), ALU.subtract)\
                     .then_inc(s_xlo, 1)

                def split_w(i):
                    _, _, hi, lo = WLOADS[i]
                    dve.wait_ge(s_whi, i + 1)
                    v.tensor_tensor(flat(lo), staged(i, hi), flat(hi).bitcast(F32), ALU.subtract).then_inc(s_wlo, 1)

                for i in range(FIRST):
                    split_w(i)
                    if i == 0:
                        for c in range(KD):
                            dve.wait_ge(s_xhi, c + 1)
                            v.tensor_tensor(x_lo[:, c, :], KT[0][:, c, :], x_hi[:, c, :].bitcast(F32), ALU.subtract)\
                             .then_inc(s_xlo, 1)
                        dve.wait_ge(s_lora, 48)
                        v.tensor_copy(lidf[:], lidx[:]).then_inc(s_lidf, 1)
                        dve.wait_ge(s_lidf, 1)
                        v.tensor_scalar(lmask[:], lidf[:], owner[:, 0:1], scal[:, 0:1], ALU.is_equal, ALU.mult)\
                         .then_inc(s_lmask, 1)
                        dve.wait_ge(s_lmask, 1)

                def weights(ii, p, n):
                    split_w(FIRST + n)

                def dense(ii, p, k):
                    b = bank_of(p, k)
                    if k == XA:
                        dve.wait_ge(s_dense, blk(ii, p, GROUPS, 1))
                        positive(dve, s_rope, blk(ii, p, 8))
                        mask = lmask[:, bass.ds(blk(ii, p, BB), BB)].unsqueeze(2).broadcast_to([P, BB, T])
                        v.tensor_tensor(xa_f[:].rearrange("p (b t) -> p b t", t=T),
                                        DB[b][:].rearrange("p (b t) -> p b t", t=T), mask, ALU.mult)\
                         .then_inc(s_free[b], 1)
                        dve.wait_ge(s_xahi, blk(ii, p, 1, 1))
                        v.tensor_tensor(xa_lo[:], xa_f[:], xa_hi[:].bitcast(F32), ALU.subtract).then_inc(s_xalo, 1)
                    elif k < KG:
                        dve.wait_ge(s_hhi, blk(ii, p, KD, k - HG + 1))
                        v.tensor_tensor(h_lo[:, k - HG, :], DB[b][:], h_hi[:, k - HG, :].bitcast(F32), ALU.subtract)\
                         .then_inc(s_free[b], 1)
                    elif k < VG:
                        n = k - KG
                        dst = (KT if k < QG else QT)[p][:, n % 4, :]
                        dve.wait_ge(s_free[b], bank_uses(ii, p, k) + 1)
                        dve.sem_inc(s_shuffle, 1)
                        if k == KG and isinstance(ii, int) and ii == 0 and p == 0:
                            dve.wait_ge(s_const, CONSTS * 16)
                        v.stream_shuffle(dst, rot[n % ROTS][:], SWAP).then_inc(s_swp, 1)
                        dve.wait_ge(s_swp, blk(ii, p, 8, n + 1))
                        r = rot[n % ROTS][:].rearrange("p (b t) -> p b t", t=T)
                        v.tensor_tensor(r, r, cos[:].unsqueeze(1).broadcast_to([P, BB, T]), ALU.mult).then_inc(s_cosd, 1)
                    else:
                        if k == VG and isinstance(ii, int) and ii == 0 and p == 0:
                            dve.wait_ge(s_vzero, 1)
                        dve.wait_ge(s_dense, blk(ii, p, GROUPS, k + 1))
                        for bb in range(2):
                            tokens = DB[b][bb * T:(bb + 1) * T, :].rearrange("t (m e d) -> t m e d", e=2, d=DH)
                            for e in range(2):
                                last = v.tensor_copy(V[e * T:(e + 1) * T, k - VG, bb, :, e * DH:(e + 1) * DH], tokens[:, :, e, :])
                        last.then_inc(s_free[b], 1)

                by_head = [P, H // 2, T]

                def soft(jj, q, uh):
                    u, half = uh
                    n = unit(jj, q, u, 2, half + 1)
                    pr = heads_of(probs, half)
                    dve.wait_ge(s_sc, unit(jj, q, u, 1, 1))
                    if is_final(jj, q):
                        dve.wait_ge(s_pt, unit(jj, q, u, 2, half - 1))
                    for r in range(2):
                        last = v.scalar_tensor_tensor(probs[:, half, :, r, :],
                                                      SB[:, 2 * half + r, 0:KD * T].rearrange("p (c k) -> p c k", c=KD),
                                                      SCALE, causal[:].unsqueeze(1).broadcast_to([P, KD, T]), ALU.mult, ALU.add)
                    last.then_inc(s_sm, 1)
                    dve.wait_ge(s_sm, n)
                    v.tensor_reduce(rmax[:, half, :], pr, AX_X, ALU.max).then_inc(s_max, 1)
                    dve.wait_ge(s_max, n)
                    v.tensor_tensor(pr, pr, rmax[:, half, :].unsqueeze(2).broadcast_to(by_head), ALU.subtract).then_inc(s_off, 1)

                def norm(jj, q, uh):
                    u, half = uh
                    n = unit(jj, q, u, 2, half + 1)
                    pr = heads_of(probs, half)
                    dve.wait_ge(s_exp, n)
                    v.tensor_reduce(sums[:, half, :], pr, AX_X, ALU.add).then_inc(s_sum, 1)
                    dve.wait_ge(s_sum, n)
                    v.reciprocal(rinv[:, half, :], sums[:, half, :]).then_inc(s_rinv, 1)
                    dve.wait_ge(s_rinv, n)
                    v.tensor_tensor(pr, pr, rinv[:, half, :].unsqueeze(2).broadcast_to(by_head), ALU.mult).then_inc(s_pn, 1)

                def oT(jj, q, u):
                    dve.wait_ge(s_ohi, unit(jj, q, u, 1, 1))
                    v.tensor_tensor(o_lo[:].rearrange("p c k -> p (c k)"), OB[:],
                                    o_hi[:].rearrange("p c k -> p (c k)").bitcast(F32), ALU.subtract).then_inc(s_olo, 1)

                def wo(jj, q, u):
                    dve.wait_ge(s_wo, unit(jj, q, u, 1, 1))
                    dve.wait_ge(s_xt[u % 2], unit_half(jj, q, u, 16) + 16)
                    v.tensor_tensor(x1[u % 2][:], XB[:], x1[u % 2][:], ALU.add).then_inc(s_x1, 1)

                def router(jj, q, u):
                    dve.wait_ge(s_rt, unit(jj, q, u, 1, 1))
                    v.tensor_copy(keep["logits"][:, bass.ds(unit(jj, q, u), 1), :],
                                  XB[:, 0:E + 1].unsqueeze(1)).then_inc(s_rte, 1)

                run(dve, {"weights": weights, "xsplit": xsplit, "dense": dense, "soft": soft, "norm": norm, "oT": oT,
                          "wo": wo, "router": router})


def stage_shared(nc, a, keep):
    with ExitStack() as ctx:
        def sb(name, shape, dt=F32):
            return ctx.enter_context(nc.sbuf_tensor(name, shape, dt))

        def sem(name):
            return ctx.enter_context(nc.semaphore(name))

        w_hi, w_lo = sb("s_hi", [P, KS, PIECE], F32R), sb("s_lo", [P, KS, PIECE], F32R)
        wraw = [keep["big"][:, i * PIECE:(i + 1) * PIECE] for i in range(2)]
        xraw = keep["rows"]
        x_hi, x_lo = sb("xb_hi", [P, KD, BLK], F32R), sb("xb_lo", [P, KD, BLK], F32R)
        hid = [sb(f"hidden{i}", [P, BLK]) for i in range(2)]
        h_hi = [sb(f"hs_hi{i}", [P, BLK], F32R) for i in range(2)]
        h_lo = [sb(f"hs_lo{i}", [P, BLK], F32R) for i in range(2)]
        x1 = [sb(f"x1s{i}", [P, D]) for i in range(UNITS)]
        gcol = sb("gcol", [P, UNITS])
        rank_tmp = keep["big"][:, 2 * PIECE:2 * PIECE + NT // 2 * E * E].rearrange("p (j e f) -> p j e f", e=E, f=E)
        prob, pick = sb("prob", [P, NT, E]), sb("pick", [P, 2, NT, E])
        both, slot = sb("both", [P, NT, E]), sb("slot", [P, NT, E])
        tmp, cnt = sb("tmp", [P, NT, E]), sb("cnt", [P, NT, E])
        col, sg = sb("col", [P, NT]), sb("sg", [P, NT])
        gate_of = sb("gate_of", [P, NT])
        ones, before, lower = sb("ones", [P, P]), sb("before", [P, P]), sb("lower", [P, E, E])
        starts, tno = sb("starts", [P, NT]), sb("tno", [P, TILES])
        ntile, ctile, base = sb("ntile", [P, E]), sb("ctile", [P, E]), sb("base", [P, E])
        rowf = sb("rowf", [P, 2, NT])
        rowi, rowa, rowb = sb("rowi", [P, 2, NT], I32), sb("rowa", [P, 2, NT], I32), sb("rowb", [P, 2, NT], I32)
        pair = sb("pair", [P, 2, NT, 2])
        tok = sb("tok", [P, NT], I32)
        tix = [sb(f"tix{i}", [P, 1], I32) for i in range(2)]
        tpay = [sb(f"tpay{i}", [P, 2]) for i in range(2)]

        ps = [ctx.enter_context(nc.psum_tensor(f"pt{i}", [P, 512], F32)) for i in range(8)]
        F1, F2, Y = ps[0:2], ps[2:4], ps[4:8]

        s_const = sem("s2_const")
        s_praw, s_xraw = keep["s_praw"], keep["s_xraw"]
        s_phi, s_plo = sem("s2_piece_hi"), sem("s2_piece_lo")
        s_xhi, s_xlo = sem("s2_x_hi"), sem("s2_x_lo")
        s_step = sem("s2_routing_step")
        s_exp, s_counts, s_pairs = sem("s2_router_exp"), sem("s2_counts"), sem("s2_pairs")
        s_tinit, s_tcopy = sem("s2_table_init"), sem("s2_pair_copied")
        s_tst = [sem(f"s2_pair_stored{i}") for i in range(2)]
        s_tb, s_issue = sem("s2_routed"), sem("s2_pair_issued")
        s_fc, s_silu, s_h, s_hhi, s_hlo = sem("s2_fc"), sem("s2_silu"), sem("s2_h"), sem("s2_h_hi"), sem("s2_h_lo")
        s_pj, s_yt, s_yo, s_g = sem("s2_proj"), sem("s2_y"), sem("s2_y_read"), sem("s2_gate_column")
        s_x1 = [sem(f"s2_x1_loaded{i}") for i in range(UNITS)]
        s_ost = [sem(f"s2_out_stored{i}") for i in range(UNITS)]

        PREFIX_READ = 22

        def blk(ii, p, per, c=0):
            return ii * (2 * per) + (per * p + c)

        def positive(eng, s, value):
            if isinstance(value, int) and value <= 0:
                return
            eng.wait_ge(s, value)

        def blocks(eng, body):
            last = NBLK // 2 - 1
            body(0, 0, (0, 1))
            body(0, 1, (1, 0))
            with eng.Fori(1, last) as ii:
                body(ii, 0, (ii, 1))
                body(ii, 1, (ii + 1, 0))
            body(last, 0, (last, 1))
            body(last, 1, None)

        def is_block(ii, p, n):
            return isinstance(ii, int) and 2 * ii + p == n

        with nc.Block() as block:
            @block.sync
            def _(sp):
                def load_x(ii, p):
                    for u in range(UNITS):
                        positive(sp, s_xlo, blk(ii, p, UNITS, u + 1 - UNITS))
                        sp.dma_start(xraw[u][:], a["xfT"][bass.ds(blk(ii, p, UNITS, u), 1), :, :]
                                     .rearrange("g p n -> (g p) n")).then_inc(s_xraw[u], 16)

                def piece(m):
                    if m >= 2:
                        sp.wait_ge(s_plo, m - 1)
                    sp.dma_start(wraw[m % 2][:], a["shared_w"][m]).then_inc(s_praw[m % 2], 16)

                consts = ((ones, a["ones"]), (before, a["before"]), (starts, a["starts"]), (tno, a["tno"]), (tok, a["tok"]))
                for dst, src in consts:
                    sp.dma_start(dst[:], src).then_inc(s_const, 16)
                sp.dma_start(lower[:].rearrange("p a b -> p (a b)"), a["lower"]).then_inc(s_const, 16)
                sp.dma_start(a["table"], a["table_init"]).then_inc(s_tinit, 16)
                for m in range(2, KS):
                    piece(m)

                def body(ii, p, nxt):
                    if nxt is not None:
                        load_x(*nxt)
                    for t in range(UNITS):
                        positive(sp, s_ost[t], blk(ii, p, 16))
                        sp.dma_start(x1[t][:], a["x1"][bass.ds(blk(ii, p, BLK, t * P), P), :]).then_inc(s_x1[t], 16)
                    if nxt is None:
                        sp.wait_ge(s_plo, KS)
                        sp.wait_ge(s_pairs, 1)
                        sp.dma_start(keep["big"][:], a["expert_w"][0]).then_inc(keep["s_first"], 16)
                    for t in range(UNITS):
                        sp.wait_ge(s_yo, blk(ii, p, UNITS, t + 1))
                        sp.dma_start(a["out"][bass.ds(blk(ii, p, BLK, t * P), P), :], x1[t][:]).then_inc(s_ost[t], 16)

                blocks(sp, body)
                for s in s_ost:
                    sp.wait_ge(s, 16 * NBLK)

            @block.scalar
            def _(act):
                def split_x(ii, p, units=range(UNITS)):
                    positive(act, s_fc, blk(ii, p, KS))
                    for u in units:
                        act.wait_ge(s_xraw[u], blk(ii, p, 16, 16))
                        act.activation(x_hi[:, :, u * P:(u + 1) * P], xraw[u][:].rearrange("p (k n) -> p k n", k=KD),
                                       ACT.Copy).then_inc(s_xhi, 1)

                def piece(m):
                    act.wait_ge(s_praw[m % 2], 16 * (m // 2 + 1))
                    act.activation(w_hi[:, m, :], wraw[m % 2][:], ACT.Copy).then_inc(s_phi, 1)

                lg = keep["logits"]
                split_x(0, 0)
                piece(0)
                piece(1)
                act.activation(sg[:], lg[:, :, E], ACT.Exp, scale=-1.0).then_inc(s_exp, 1)
                act.wait_ge(s_step, 2)
                act.activation(tmp[:], prob[:], ACT.Exp).then_inc(s_exp, 1)

                def body(ii, p, nxt):
                    for m in range(KS):
                        n = blk(ii, p, KS, m)
                        j = (KS * p + m) % 2
                        act.wait_ge(s_fc, n + 1)
                        positive(act, s_hlo, n - 1)
                        act.activation(hid[j][:], F1[j][:], ACT.Silu).then_inc(s_silu, 1)
                        if m == KS - 1 and nxt is not None:
                            split_x(*nxt, range(1))
                        act.wait_ge(s_h, n + 1)
                        positive(act, s_pj, n - 1)
                        act.activation(h_hi[j][:], hid[j][:], ACT.Copy).then_inc(s_hhi, 1)
                        if is_block(ii, p, 0) and m + 2 < KS:
                            piece(m + 2)
                    if nxt is not None:
                        split_x(*nxt, range(1, UNITS))

                blocks(act, body)

            @block.gpsimd
            def _(pool):
                pool.wait_ge(s_pairs, 1)
                pool.wait_ge(s_tinit, 16)
                rows = rowi[:].rearrange("p k j -> p (k j)")
                pays = pair[:].rearrange("p k j w -> p (k j) w")

                def put(ii, j, first):
                    n = ii * 2 + j
                    if not first:
                        pool.wait_ge(s_tst[j], ii * 16)
                    nc.gpsimd.tensor_copy(tix[j][:], rows[:, bass.ds(n, 1)]).then_inc(s_tcopy, 1)
                    nc.gpsimd.tensor_copy(tpay[j][:].unsqueeze(1), pays[:, bass.ds(n, 1), :]).then_inc(s_tcopy, 1)
                    pool.wait_ge(s_tcopy, n * 2 + 2)
                    pool.sem_inc(s_issue, 1)
                    nc.gpsimd.indirect_dma_start(out=a["table"], out_offset=bass.IndirectOffsetOnAxis(ap=tix[j][:], axis=0),
                                                 in_=tpay[j][:], in_offset=None).then_inc(s_tst[j], 16)
                put(0, 0, True)
                put(0, 1, True)
                with pool.Fori(1, NT) as ii:
                    put(ii, 0, False)
                    put(ii, 1, False)
                for s in s_tst:
                    pool.wait_ge(s, 16 * NT)
                nc.gpsimd.dma_start(keep["table"][:].rearrange("p t w -> p (t w)"),
                                    a["table"].rearrange("(p t) w -> p (t w)", p=P)).then_inc(keep["s_tab"], 16)
                pool.wait_ge(keep["s_tab"], 16)
                pool.wait_ge(s_xlo, NT)
                for i in range(2):
                    nc.gpsimd.tensor_copy(keep["gix"][i][:], keep["table"][:, i, 0:1]).then_inc(keep["s_gix"], 1)
                    pool.wait_ge(keep["s_gix"], i + 1)
                    nc.gpsimd.indirect_dma_start(out=keep["rows"][i][:], out_offset=None, in_=a["xf"],
                                                 in_offset=bass.IndirectOffsetOnAxis(ap=keep["gix"][i][:], axis=0))\
                      .then_inc(keep["s_g"][i], 16)

            @block.tensor
            def _(pe):
                def three(out, lh, ll, rh, rl, first, last):
                    pe.matmul(out, lh, rh, start=first, stop=False)
                    pe.matmul(out, lh, rl, start=False, stop=False)
                    return pe.matmul(out, ll, rh, start=False, stop=last)

                def counts():
                    pe.wait_ge(s_const, 96)
                    pe.wait_ge(s_tb, 1)
                    pe.wait_ge(s_yo, 1)
                    m = both[:].rearrange("p j e -> p (j e)")
                    pe.matmul(Y[0][:, 0:NT * E], before[:], m, start=True, stop=True)
                    pe.matmul(Y[0][:, NT * E:2 * NT * E], ones[:], m, start=True, stop=True).then_inc(s_counts, 1)

                def proj(ii, p, m):
                    n = blk(ii, p, KS, m)
                    j = (KS * p + m) % 2
                    pe.wait_ge(s_hlo, n + 1)
                    if is_block(ii, p, 1) and m == 0:
                        pe.wait_ge(s_step, PREFIX_READ)
                    w = slice(2 * KD * P, PIECE)
                    for t in range(UNITS):
                        if m == 0:
                            positive(pe, s_yo, blk(ii, p, UNITS, t + 1 - UNITS))
                        c = slice(t * P, (t + 1) * P)
                        mm = three(Y[t][:], h_hi[j][:, c], h_lo[j][:, c], w_hi[:, m, w], w_lo[:, m, w], m == 0, m == KS - 1)
                        if t == UNITS - 1:
                            mm.then_inc(s_pj, 1)
                        elif m == KS - 1:
                            mm.then_inc(s_yt, 1)

                def body(ii, p, nxt):
                    for m in range(KS):
                        n = blk(ii, p, KS, m)
                        j = (KS * p + m) % 2
                        if m == 0:
                            pe.wait_ge(s_xlo, blk(ii, p, UNITS, UNITS))
                        if is_block(ii, p, 0):
                            pe.wait_ge(s_plo, m + 1)
                        positive(pe, s_h, n - 1)
                        for f, bank in ((0, F1[j]), (1, F2[j])):
                            for k in range(KD):
                                c = slice((f * KD + k) * P, (f * KD + k + 1) * P)
                                mm = three(bank[:], w_hi[:, m, c], w_lo[:, m, c], x_hi[:, k, :], x_lo[:, k, :],
                                           k == 0, k == KD - 1)
                        mm.then_inc(s_fc, 1)
                        if m:
                            proj(ii, p, m - 1)
                    proj(ii, p, KS - 1)
                    if is_block(ii, p, 0):
                        counts()

                blocks(pe, body)

            @block.vector
            def _(dve):
                v = nc.vector
                steps = [0]

                def then(ins):
                    ins.then_inc(s_step, 1)
                    steps[0] += 1
                    dve.wait_ge(s_step, steps[0])

                lg = keep["logits"]
                by_e = [P, NT, E]
                wide = rank_tmp[:]
                pairwise = [P, NT // 2, E, E]
                halves = [(t, prob[:, t, :].unsqueeze(3).broadcast_to(pairwise), prob[:, t, :].unsqueeze(2).broadcast_to(pairwise))
                          for t in (slice(0, NT // 2), slice(NT // 2, NT))]

                def softmax():
                    dve.wait_ge(s_exp, 2)
                    then(v.tensor_reduce(col[:], tmp[:], AX_X, ALU.add))
                    then(v.reciprocal(col[:], col[:]))
                    then(v.tensor_tensor(prob[:], tmp[:], col[:].unsqueeze(2).broadcast_to(by_e), ALU.mult))
                    then(v.tensor_scalar(sg[:], sg[:], 1.0, None, ALU.add))
                    then(v.reciprocal(gate_of[:], sg[:]))

                def equal_before():
                    for t, mine, other in halves:
                        then(v.tensor_tensor(wide, other, mine, ALU.is_equal))
                        then(v.tensor_tensor(wide, wide, lower[:].unsqueeze(1).broadcast_to(pairwise), ALU.mult))
                        then(v.tensor_reduce(tmp[:, t, :], wide, AX_X, ALU.add))

                def higher():
                    for t, mine, other in halves:
                        then(v.tensor_tensor(wide, other, mine, ALU.is_gt))
                        then(v.tensor_reduce(cnt[:, t, :], wide, AX_X, ALU.add))
                    then(v.tensor_tensor(cnt[:], cnt[:], tmp[:], ALU.add))
                    for k in range(TOPK):
                        then(v.tensor_scalar(pick[:, k, :, :], cnt[:], float(k), None, ALU.is_equal))
                    v.tensor_tensor(both[:], pick[:, 0, :, :], pick[:, 1, :, :], ALU.add).then_inc(s_tb, 1)
                    dve.wait_ge(s_tb, 1)

                def read_counts():
                    dve.wait_ge(s_counts, 1)
                    then(v.tensor_copy(slot[:].rearrange("p j e -> p (j e)"), Y[0][:, 0:NT * E]))
                    then(v.tensor_copy(tmp[:].rearrange("p j e -> p (j e)"), Y[0][:, NT * E:2 * NT * E]))
                    assert steps[0] == PREFIX_READ

                def places():
                    for e in range(E):
                        then(v.tensor_tensor_scan(cnt[:, :, e], ones[:, 0:NT], tmp[:, :, e], 0.0, ALU.mult, ALU.add))
                    then(v.tensor_tensor(slot[:], slot[:], cnt[:], ALU.add))
                    then(v.tensor_tensor(slot[:], slot[:], tmp[:], ALU.subtract))
                    few = both[:].rearrange("p j e -> p (j e)").rearrange("p (e j) -> p e j", e=E)
                    then(v.tensor_tensor(few, cnt[:, NT - 1, :].unsqueeze(2).broadcast_to([P, E, NT]),
                                         starts[:].unsqueeze(1).broadcast_to([P, E, NT]), ALU.is_gt))
                    then(v.tensor_reduce(ntile[:], few, AX_X, ALU.add))
                    then(v.tensor_scalar(ntile[:], ntile[:], 1.0, None, ALU.max))
                    then(v.tensor_tensor_scan(ctile[:], ones[:, 0:E], ntile[:], 0.0, ALU.mult, ALU.add))
                    then(v.tensor_tensor(base[:], ctile[:], ntile[:], ALU.subtract))
                    then(v.tensor_scalar(base[:], base[:], float(P), None, ALU.mult))
                    then(v.tensor_tensor(slot[:], slot[:], base[:].unsqueeze(1).broadcast_to(by_e), ALU.add))
                    ends = rank_tmp[:].rearrange("p j e f -> p (j e f)")[:, 0:TILES * E].rearrange("p (t e) -> p t e", e=E)
                    then(v.tensor_tensor(ends, ctile[:].unsqueeze(1).broadcast_to([P, TILES, E]),
                                         tno[:].unsqueeze(2).broadcast_to([P, TILES, E]), ALU.is_le))
                    then(v.tensor_reduce(tno[:], ends, AX_X, ALU.add))
                    of = tno[0:1, :]
                    then(v.tensor_scalar(of, of, float(E - 1), None, ALU.min))
                    then(v.tensor_copy(keep["expert"][:], of))
                    more, which = rank_tmp[0:1, 0:2, :, :].rearrange("p j e f -> p (j e f)")[:, 0:TILES], \
                        rank_tmp[0:1, 2:4, :, :].rearrange("p j e f -> p (j e f)")[:, 0:TILES]
                    then(v.tensor_tensor(more[:, 0:TILES - 1], of[:, 1:TILES], of[:, 0:TILES - 1], ALU.subtract))
                    then(v.tensor_scalar(which[:, 0:TILES - 1], of[:, 1:TILES], float(1 - E), None, ALU.add))
                    then(v.tensor_tensor(more[:, 0:TILES - 1], more[:, 0:TILES - 1], which[:, 0:TILES - 1], ALU.mult))
                    then(v.tensor_scalar(keep["fresh"][:, 0:TILES - 1], more[:, 0:TILES - 1], float(E), None, ALU.add))

                def pairs():
                    for k in range(TOPK):
                        then(v.tensor_tensor(tmp[:], slot[:], pick[:, k, :, :], ALU.mult))
                        then(v.tensor_reduce(rowf[:, k, :], tmp[:], AX_X, ALU.add))
                        then(v.tensor_tensor(tmp[:], prob[:], pick[:, k, :, :], ALU.mult))
                        then(v.tensor_reduce(pair[:, k, :, 1], tmp[:], AX_X, ALU.add))
                        then(v.tensor_copy(pair[:, k, :, 0], tok[:]))
                    then(v.tensor_copy(rowi[:], rowf[:]))
                    then(v.tensor_scalar(rowa[:], rowi[:], P - 1, None, ALU.bitwise_and))
                    then(v.tensor_scalar(rowb[:], rowi[:], P.bit_length() - 1, None, ALU.logical_shift_right))
                    then(v.tensor_scalar(rowa[:], rowa[:], TILES, None, ALU.mult))
                    v.tensor_tensor(rowi[:], rowa[:], rowb[:], ALU.add).then_inc(s_pairs, 1)

                def split_x(ii, p, units=range(UNITS)):
                    for u in units:
                        dve.wait_ge(s_xhi, blk(ii, p, UNITS, u + 1))
                        t = slice(u * P, (u + 1) * P)
                        v.tensor_tensor(x_lo[:, :, t], xraw[u][:].rearrange("p (k n) -> p k n", k=KD),
                                        x_hi[:, :, t].bitcast(F32), ALU.subtract).then_inc(s_xlo, 1)

                def piece(m):
                    dve.wait_ge(s_phi, m + 1)
                    v.tensor_tensor(w_lo[:, m, :], wraw[m % 2][:], w_hi[:, m, :].bitcast(F32), ALU.subtract).then_inc(s_plo, 1)

                split_x(0, 0)
                piece(0)
                piece(1)
                then(v.tensor_reduce(col[:], lg[:, :, 0:E], AX_X, ALU.max))
                then(v.tensor_tensor(prob[:], lg[:, :, 0:E], col[:].unsqueeze(2).broadcast_to(by_e), ALU.subtract))

                def body(ii, p, nxt):
                    positive(dve, s_yo, blk(ii, p, UNITS))
                    v.tensor_copy(gcol[:], gate_of[:, bass.ds(blk(ii, p, UNITS), UNITS)]).then_inc(s_g, 1)
                    for m in range(KS):
                        n = blk(ii, p, KS, m)
                        j = (KS * p + m) % 2
                        dve.wait_ge(s_silu, n + 1)
                        positive(dve, s_hhi, n - 1)
                        v.tensor_tensor(hid[j][:], hid[j][:], F2[j][:], ALU.mult).then_inc(s_h, 1)
                        if m == KS - 1 and nxt is not None:
                            split_x(*nxt, range(1))
                        dve.wait_ge(s_hhi, n + 1)
                        v.tensor_tensor(h_lo[j][:], hid[j][:], h_hi[j][:].bitcast(F32), ALU.subtract).then_inc(s_hlo, 1)
                        if is_block(ii, p, 0):
                            if m + 2 < KS:
                                piece(m + 2)
                            if m == 4:
                                equal_before()
                            if m == 6:
                                higher()
                        if is_block(ii, p, 1) and m == 1:
                            places()
                        if is_block(ii, p, 1) and m == 3:
                            pairs()
                    if nxt is not None:
                        split_x(*nxt, range(1, UNITS))
                    dve.wait_ge(s_g, blk(ii, p, 1, 1))
                    for t in range(UNITS):
                        if t < UNITS - 1:
                            dve.wait_ge(s_yt, blk(ii, p, UNITS - 1, t + 1))
                        else:
                            dve.wait_ge(s_pj, blk(ii, p, KS, KS))
                        dve.wait_ge(s_x1[t], blk(ii, p, 16, 16))
                        v.scalar_tensor_tensor(x1[t][:], Y[t][:], gcol[:, t:t + 1], x1[t][:], ALU.mult, ALU.add)\
                         .then_inc(s_yo, 1)
                    if is_block(ii, p, 0):
                        read_counts()

                dve.wait_ge(s_const, 96)
                softmax()
                blocks(dve, body)


def stage_experts(nc, a, keep):
    with ExitStack() as ctx:
        def sb(name, shape, dt=F32):
            return ctx.enter_context(nc.sbuf_tensor(name, shape, dt))

        def sem(name):
            return ctx.enter_context(nc.semaphore(name))

        raw = sb("e_raw", [P, 2 * EW])
        w_hi, w_lo = sb("e_hi", [P, RING * EW], F32R), sb("e_lo", [P, RING * EW], F32R)
        ident, table = keep["ident"], keep["table"]
        two = range(2)
        gix = keep["gix"]
        six = [sb(f"six{i}", [P, 1], I32) for i in two]
        wt = [sb(f"wt{i}", [P, 1]) for i in two]
        xg = keep["rows"][0:2]
        xT_hi = [sb(f"xgT_hi{i}", [P, KD, P], F32R) for i in two]
        xT_lo = [sb(f"xgT_lo{i}", [P, KD, P], F32R) for i in two]
        silu = [sb(f"e_silu{i}", [P, FE]) for i in two]
        h = [sb(f"e_h{i}", [P, KE * P]) for i in two]
        hT_hi = [sb(f"e_hT_hi{i}", [P, KE, P], F32R) for i in two]
        hT_lo = [sb(f"e_hT_lo{i}", [P, KE, P], F32R) for i in two]
        y = [sb(f"e_y{i}", [P, D]) for i in two]
        ps = [ctx.enter_context(nc.psum_tensor(f"pu{i}", [P, 512], F32)) for i in range(8)]
        TX, TH, H1, H2, Y = ps[0], ps[1], ps[2:4], ps[4:6], ps[6:8]

        s_pad = sem("h_padding_zeroed")
        s_wraw = [sem(f"expert_part_loaded{i}") for i in range(3)]
        s_whi = [sem(f"expert_part_hi{i}") for i in range(3)]
        s_wlo = [sem(f"expert_part_lo{i}") for i in range(3)]
        s_issue = sem("e_dma_issued")
        s_gix, s_six, s_wt = keep["s_gix"], sem("scatter_index"), sem("weight_column")
        s_g = keep["s_g"]
        s_tx, s_xhi, s_xlo, s_f1, s_f2 = sem("xT_done"), sem("xT_hi"), sem("xT_lo"), sem("fc1_done"), sem("fc2_done")
        s_silu, s_h, s_th, s_hhi, s_hlo = sem("e_silu_done"), sem("e_h_done"), sem("hT_done"), sem("hT_hi"), sem("hT_lo")
        s_pj, s_yo, s_add = sem("e_proj_done"), sem("y_copied"), sem("y_added")

        def at(ii, p, per=1, c=0):
            return ii * (2 * per) + (per * p + c)

        def positive(eng, s, value):
            if isinstance(value, int) and value <= 0:
                return
            eng.wait_ge(s, value)

        def tiles(eng, body):
            for ii in (0, 1):
                body(ii, 0)
                body(ii, 1)
            with eng.Fori(2, PAIRS - 2) as ii:
                body(ii, 0)
                body(ii, 1)
            for t in range(2 * (PAIRS - 2), TILES):
                body(t // 2, t % 2)

        def after(ii, p, n):
            ii, p = ii + (p + n) // 2, (p + n) % 2
            return None if isinstance(ii, int) and 2 * ii + p >= TILES else (ii, p)

        def is_first(ii, p):
            return isinstance(ii, int) and ii == 0 and p == 0

        def part(place, i):
            return bass.ds(place * EW + PARTS[i][0], PARTS[i][1] - PARTS[i][0])

        def refill(eng, ii, p, split):
            if after(ii, p, 1) is None:
                return
            e = eng.value_load(keep["fresh"][0:1, bass.ds(at(ii, p), 1)], min_val=0, max_val=E)
            with eng.If(e < E):
                split(e)

        with nc.Block() as block:
            @block.sync
            def _(sp):
                for e in range(1, E):
                    for i, (c0, c1) in enumerate(PARTS):
                        if e > 1:
                            sp.wait_ge(s_wraw[i], 16 * (e - 1))
                        if e > 2:
                            sp.wait_ge(s_wlo[i], e - 1)
                        o = e % 2 * EW
                        sp.dma_start(raw[:, o + c0:o + c1], a["expert_w"][e][:, c0:c1]).then_inc(s_wraw[i], 16)

            @block.gpsimd
            def _(pool):
                toks = table[:].rearrange("p t w -> p (t w)")

                def gather(ii, p):
                    positive(pool, s_tx, at(ii, p, 1, -1))
                    positive(pool, s_g[p], ii * 16)
                    nc.gpsimd.tensor_copy(gix[p][:], toks[:, bass.ds(at(ii, p, 2), 1)]).then_inc(s_gix, 1)
                    pool.wait_ge(s_gix, at(ii, p, 1, 1))
                    pool.sem_inc(s_issue, 1)
                    nc.gpsimd.indirect_dma_start(out=xg[p][:], out_offset=None, in_=a["xf"],
                                                 in_offset=bass.IndirectOffsetOnAxis(ap=gix[p][:], axis=0))\
                      .then_inc(s_g[p], 16)

                def body(ii, p):
                    if (nxt := after(ii, p, 3)) is not None:
                        gather(*nxt)
                    positive(pool, s_add, at(ii, p, 16))
                    nc.gpsimd.tensor_copy(six[p][:], toks[:, bass.ds(at(ii, p, 2), 1)]).then_inc(s_six, 1)
                    pool.wait_ge(s_six, at(ii, p, 1, 1))
                    pool.wait_ge(s_yo, at(ii, p, 1, 1))
                    pool.sem_inc(s_issue, 1)
                    nc.gpsimd.indirect_dma_start(out=a["out"], out_offset=bass.IndirectOffsetOnAxis(ap=six[p][:], axis=0),
                                                 in_=y[p][:], in_offset=None, compute_op=ALU.add).then_inc(s_add, 16)

                gather(1, 0)
                tiles(pool, body)
                pool.wait_ge(s_add, 16 * TILES)

            @block.scalar
            def _(act):
                def first_w(i):
                    act.wait_ge(keep["s_first"], 16)
                    w = slice(*PARTS[i])
                    act.activation(w_hi[:, w], keep["big"][:, w], ACT.Copy).then_inc(s_whi[i], 1)

                def split_w(e, parts=range(3)):
                    for i in parts:
                        act.wait_ge(s_wraw[i], e * 16)
                        if not isinstance(e, int):
                            act.sem_inc(s_issue, 1)
                        w, wr = part(e % RING, i), part(e % 2, i)
                        act.activation(w_hi[:, w], raw[:, wr], ACT.Copy).then_inc(s_whi[i], 1)

                def split_x(ii, p):
                    act.wait_ge(s_tx, at(ii, p, 1, 1))
                    positive(act, s_f2, at(ii, p, 1, -1))
                    act.activation(xT_hi[p][:].rearrange("p c t -> p (c t)"), TX[:], ACT.Copy).then_inc(s_xhi, 1)

                def gate(ii, p):
                    act.wait_ge(s_f1, at(ii, p, 1, 1))
                    positive(act, s_h, at(ii, p, 1, -1))
                    act.activation(silu[p][:], H1[p][:, 0:FE], ACT.Silu).then_inc(s_silu, 1)

                def body(ii, p):
                    if (nxt := after(ii, p, 1)) is not None:
                        gate(*nxt)
                    act.wait_ge(s_th, at(ii, p, 1, 1))
                    positive(act, s_pj, at(ii, p, 1, -1))
                    act.activation(hT_hi[p][:].rearrange("p c t -> p (c t)"), TH[:, 0:KE * P], ACT.Copy).then_inc(s_hhi, 1)
                    if (nxt := after(ii, p, 2)) is not None:
                        split_x(*nxt)
                    if is_first(ii, p):
                        split_w(1, [1, 2])
                    refill(act, ii, p, split_w)
                    act.wait_ge(s_pj, at(ii, p, 1, 1))
                    positive(act, s_add, at(ii, p, 16, -16))
                    act.activation(y[p][:], Y[p][:], ACT.Copy).then_inc(s_yo, 1)

                first_w(0)
                split_x(0, 0)
                first_w(1)
                gate(0, 0)
                split_x(0, 1)
                first_w(2)
                split_w(1, [0])
                tiles(act, body)

            @block.tensor
            def _(pe):
                def three(out, lh, ll, w, first, last):
                    pe.matmul(out, lh, w_hi[:, w], start=first, stop=False)
                    pe.matmul(out, lh, w_lo[:, w], start=False, stop=False)
                    return pe.matmul(out, ll, w_hi[:, w], start=False, stop=last)

                def turn_x(ii, p):
                    pe.wait_ge(s_g[p], ii * 16 + 16)
                    positive(pe, s_xlo, at(ii, p))
                    for c in range(KD):
                        mm = pe.transpose(TX[:, c * P:(c + 1) * P], xg[p][:, c * P:(c + 1) * P], ident[:])
                    mm.then_inc(s_tx, 1)

                def expert(ii, p):
                    e = pe.value_load(keep["expert"][0:1, bass.ds(at(ii, p), 1)], min_val=0, max_val=E - 1)
                    return e, e % RING

                def fc(ii, p, e, place, f, bank, done):
                    pe.wait_ge(s_wlo[f], e + 1)
                    for c in range(KD):
                        mm = three(bank[:, 0:FE], xT_hi[p][:, c, :], xT_lo[p][:, c, :],
                                   bass.ds(place * EW + (f * KD + c) * FE, FE), c == 0, c == KD - 1)
                    mm.then_inc(done, 1)

                def turn_h(ii, p):
                    pe.wait_ge(s_h, at(ii, p, 1, 1))
                    positive(pe, s_hlo, at(ii, p))
                    for c in range(KE):
                        mm = pe.transpose(TH[:, c * P:(c + 1) * P], h[p][:, c * P:(c + 1) * P], ident[:])
                    mm.then_inc(s_th, 1)

                def proj(ii, p, e, place):
                    pe.wait_ge(s_wlo[2], e + 1)
                    pe.wait_ge(s_hlo, at(ii, p, 1, 1))
                    positive(pe, s_yo, at(ii, p, 1, -1))
                    for c in range(KE):
                        mm = three(Y[p][:], hT_hi[p][:, c, :], hT_lo[p][:, c, :],
                                   bass.ds(place * EW + PARTS[2][0] + c * D, D), c == 0, c == KE - 1)
                    mm.then_inc(s_pj, 1)

                def body(ii, p):
                    nxt = after(ii, p, 1)
                    if nxt is not None:
                        e1, place1 = expert(*nxt)
                        pe.wait_ge(s_xlo, at(*nxt, 1, 1))
                        positive(pe, s_h, at(*nxt, 1, -1))
                        fc(*nxt, e1, place1, 0, H1[nxt[1]], s_f1)
                    turn_h(ii, p)
                    if (later := after(ii, p, 2)) is not None:
                        turn_x(*later)
                    if nxt is not None:
                        fc(*nxt, e1, place1, 1, H2[nxt[1]], s_f2)
                    proj(ii, p, *expert(ii, p))

                turn_x(0, 0)
                pe.wait_ge(s_xlo, 1)
                fc(0, 0, 0, 0, 0, H1[0], s_f1)
                turn_x(0, 1)
                fc(0, 0, 0, 0, 1, H2[0], s_f2)
                tiles(pe, body)

            @block.vector
            def _(dve):
                v = nc.vector
                flat = table[:].rearrange("p t w -> p (t w)")

                def first_w(i):
                    dve.wait_ge(s_whi[i], 1)
                    w = slice(*PARTS[i])
                    v.tensor_tensor(w_lo[:, w], keep["big"][:, w], w_hi[:, w].bitcast(F32), ALU.subtract).then_inc(s_wlo[i], 1)

                def split_w(e, parts=range(3)):
                    for i in parts:
                        dve.wait_ge(s_whi[i], e + 1)
                        if not isinstance(e, int):
                            dve.sem_inc(s_issue, 1)
                        w, wr = part(e % RING, i), part(e % 2, i)
                        v.tensor_tensor(w_lo[:, w], raw[:, wr], w_hi[:, w].bitcast(F32), ALU.subtract).then_inc(s_wlo[i], 1)

                def split_x(ii, p):
                    dve.wait_ge(s_xhi, at(ii, p, 1, 1))
                    v.tensor_tensor(xT_lo[p][:].rearrange("p c t -> p (c t)"), TX[:],
                                    xT_hi[p][:].rearrange("p c t -> p (c t)").bitcast(F32), ALU.subtract).then_inc(s_xlo, 1)

                def weigh(ii, p):
                    v.tensor_copy(wt[p][:], flat[:, bass.ds(at(ii, p, 2, 1), 1)]).then_inc(s_wt, 1)
                    dve.wait_ge(s_wt, at(ii, p, 1, 1))
                    dve.wait_ge(s_silu, at(ii, p, 1, 1))
                    dve.wait_ge(s_f2, at(ii, p, 1, 1))
                    positive(dve, s_th, at(ii, p, 1, -1))
                    v.scalar_tensor_tensor(h[p][:, 0:FE], silu[p][:], wt[p][:, 0:1], H2[p][:, 0:FE], ALU.mult, ALU.mult)\
                     .then_inc(s_h, 1)

                def body(ii, p):
                    dve.wait_ge(s_hhi, at(ii, p, 1, 1))
                    v.tensor_tensor(hT_lo[p][:].rearrange("p c t -> p (c t)"), TH[:, 0:KE * P],
                                    hT_hi[p][:].rearrange("p c t -> p (c t)").bitcast(F32), ALU.subtract).then_inc(s_hlo, 1)
                    if (nxt := after(ii, p, 2)) is not None:
                        split_x(*nxt)
                    if is_first(ii, p):
                        split_w(1, [1])
                    if (nxt := after(ii, p, 1)) is not None:
                        weigh(*nxt)
                    if is_first(ii, p):
                        split_w(1, [2])
                    refill(dve, ii, p, split_w)

                for i in two:
                    v.memset(h[i][:, FE:], 0.0).then_inc(s_pad, 1)
                dve.wait_ge(s_pad, 2)
                first_w(0)
                split_x(0, 0)
                first_w(1)
                split_x(0, 1)
                weigh(0, 0)
                first_w(2)
                split_w(1, [0])
                tiles(dve, body)


def build(nc, a):
    a["xf"] = nc.dram_tensor("xf_rows", [N + P, D], F32).ap()
    a["xfT"] = nc.dram_tensor("xf_T", [NT, P, D], F32).ap()
    a["x1"] = nc.dram_tensor("x1_rows", [N, D], F32).ap()
    a["table"] = nc.dram_tensor("slot_table", [P * TILES, 2], F32).ap()
    with ExitStack() as ctx:
        def sb(name, shape, dt=F32):
            return ctx.enter_context(nc.sbuf_tensor(name, shape, dt))

        def sem(name):
            return ctx.enter_context(nc.semaphore(name))

        keep = {"logits": sb("logits", [P, NT, E + 1]), "ident": sb("ident", [P, P]),
                "big": sb("big", [P, EW]), "rows": [sb(f"rows{i}", [P, D]) for i in range(4)],
                "s_xraw": [sem(f"s2_x_raw{i}") for i in range(UNITS)],
                "s_praw": [sem(f"s2_piece_raw{i}") for i in range(2)],
                "s_first": sem("first_expert_loaded"), "s_tab": sem("table_loaded"),
                "s_gix": sem("gather_index"), "s_g": [sem(f"gathered{i}") for i in range(2)]}
        stage_attention(nc, a, keep)
        for name in ("expert", "fresh"):
            keep[name] = sb(f"tile_{name}", [1, TILES], I32)
        keep["table"] = sb("e_table", [P, TILES, 2])
        keep["gix"] = [sb(f"gix{i}", [P, 1], I32) for i in range(2)]
        stage_shared(nc, a, keep)
        stage_experts(nc, a, keep)


def layouts(np, inputs):
    x = np.asarray(inputs["x"]).reshape(N, D)
    turned = lambda name: np.ascontiguousarray(np.swapaxes(np.asarray(inputs[name]), -1, -2))
    r = {
        "x": x, "x_T": np.ascontiguousarray(x.T),
        "lora_idx": np.asarray(inputs["itok_B_0_6"]).reshape(1, B),
        "cond": np.asarray(inputs["itok_B_1_198"]).reshape(1, B),
        "W_T": turned("L0_cond_W"),
        "A_T": np.ascontiguousarray(np.asarray(inputs["L0_cond_A"]).reshape(ADAPTERS * RANK, D).T),
        "B_T": turned("L0_cond_Bm").reshape(ADAPTERS * RANK, D),
        "scal": np.repeat(np.asarray(inputs["L0_cond_scalings"]), RANK).reshape(P, 1),
        "Wq_T": turned("L0_attn_Wq"), "Wk_T": turned("L0_attn_Wk"), "Wv_T": turned("L0_attn_Wv"),
        "Wo_T": turned("L0_attn_Wo"),
        "mix_w": np.asarray(inputs["L0_cond2_weights"]),
        "gate_T": np.ascontiguousarray(np.concatenate([np.asarray(inputs["L0_ffn_gate_w"]),
                                                       np.asarray(inputs["L0_ffn_shared_gate_w"])]).T),
    }
    fc = [turned(f"L0_ffn_shared_fc{i}").reshape(KD, P, KS, P).transpose(2, 1, 0, 3).reshape(KS, P, KD * P) for i in (1, 2)]
    r["shared_w"] = np.ascontiguousarray(np.concatenate(fc + [turned("L0_ffn_shared_proj").reshape(KS, P, D)], axis=2))
    fc = [turned(f"L0_ffn_expert_fc{i}").reshape(E, KD, P, FE).transpose(0, 2, 1, 3).reshape(E, P, KD * FE) for i in (1, 2)]
    proj = np.zeros((E, KE * P, D), np.float32)
    proj[:, :FE] = turned("L0_ffn_expert_proj")
    r["expert_w"] = np.ascontiguousarray(np.concatenate(
        fc + [proj.reshape(E, KE, P, D).transpose(0, 2, 1, 3).reshape(E, P, KE * D)], axis=2))
    f = np.float32
    p = np.arange(P)
    theta = f(10000.0) ** (f(-2.0) * np.arange(DH // 2, dtype=f) / f(DH))
    angles = np.arange(T, dtype=f)[:, None] * theta.astype(f)[None, :]
    lane = (p % DH) // 2
    sign = np.where(p % 2 == 0, -1, 1).astype(f)
    r["cos"] = np.ascontiguousarray(np.cos(angles).astype(f)[:, lane].T)
    r["sin"] = np.ascontiguousarray(np.sin(angles).astype(f)[:, lane].T * sign[:, None])
    r["causal"] = np.where(np.arange(T)[None, :] <= p[:, None] % T, 0, MASKED).astype(f)
    r["ident"] = np.eye(P, dtype=f)
    r["owner"] = (p // RANK).astype(f).reshape(P, 1)
    r["ones"] = np.ones((P, P), f)
    r["before"] = (p[:, None] < p[None, :]).astype(f)
    e = np.arange(E)
    r["lower"] = np.broadcast_to((e[None, :] < e[:, None]).astype(f).reshape(1, E * E), (P, E * E)).copy()
    r["starts"] = np.broadcast_to((np.arange(NT) * P).astype(f), (P, NT)).copy()
    r["tno"] = np.broadcast_to(np.arange(TILES).astype(f), (P, TILES)).copy()
    r["tok"] = np.ascontiguousarray((np.arange(NT)[None, :] * P + p[:, None]).astype(np.int32))
    init = np.zeros((P, TILES, 2), f)
    init[:, :, 0] = (N + p)[:, None]
    r["table_init"] = init.reshape(P * TILES, 2)
    return r


def kernel(**inputs):
    import numpy as np
    import concourse.bacc as bacc
    from concourse.bass_utils import run_bass_kernel_spmd

    nc = bacc.Bacc("TRN2", target_bir_lowering=False, num_devices=1)
    arrays = layouts(np, inputs)
    a = {n: nc.dram_tensor(f"in_{n}", v.shape, mybir.dt.from_np(v.dtype), kind="ExternalInput").ap() for n, v in arrays.items()}
    a["out"] = nc.dram_tensor("out", [N + P, D], F32, kind="ExternalOutput").ap()
    build(nc, a)
    got = run_bass_kernel_spmd(nc, [{f"in_{n}": v for n, v in arrays.items()}], core_ids=[0])
    return got.results[0]["out"][:N].reshape(B, T, D)
```
